# Optimizing a Trainium2 kernel written in Bass

```python
import numpy as np
import jax
import jax.numpy as jnp

def _softmax(x, axis=-1):
    return jax.nn.softmax(x, axis=axis)

def _gelu(x):
    return jax.nn.gelu(x, approximate=True)

def _silu(x):
    return jax.nn.silu(x)

def _sigmoid(x):
    return jax.nn.sigmoid(x)

def _layernorm(x, axis=-1, eps=1e-05):
    m = jnp.mean(x, axis=axis, keepdims=True)
    v = jnp.var(x, axis=axis, keepdims=True)
    return (x - m) / jnp.sqrt(v + eps)

def _scatter_add(tgt, idx, src, axis=0):
    return tgt.at[idx].add(src)

def _segment_sum(src, seg, n):
    return jax.ops.segment_sum(src, seg, n)
kernel_name = 'mk_decoder_preln_d1_seqx_r8_a3bb90'

def setup_inputs(seed: int=0):
    np.random.seed(seed)
    _w = jnp.asarray

    def _rec_inputs():
        import jax
        import jax.numpy as jnp
        _rk = jax.random.key(seed)
        x = -0.0003929 + 0.9999 * jax.random.normal(jax.random.fold_in(_rk, 1), (4, 256, 128), jnp.float32)
        _lenS = 256 - jax.random.randint(jax.random.fold_in(_rk, 7), (4,), 0, max(1, 256 // 4) + 1, jnp.int32)
        _lenS2 = 1601 - jax.random.randint(jax.random.fold_in(_rk, 8), (4,), 0, max(1, 1601 // 4) + 1, jnp.int32)
        _ctx_512P = jax.random.normal(jax.random.fold_in(_rk, 11), (4, 16, 64), jnp.float32)
        _ctx_512c = jax.random.dirichlet(jax.random.fold_in(_rk, 511), 0.3 * jnp.ones((16,), jnp.float32), (4, 1601))
        _ctx_512t = jnp.einsum('bsk,bkd->bsd', _ctx_512c, _ctx_512P)
        _ctx_512t = _ctx_512t * jax.lax.rsqrt(jnp.mean(jnp.square(_ctx_512t)) + 1e-12) * 0.953939
        ctx_512 = 4.13588e-05 + 0.999923 * (_ctx_512t + 0.3 * jax.random.normal(jax.random.fold_in(_rk, 611), (4, 1601, 64), jnp.float32))
        return (x, ctx_512)
    x, ctx_512 = _rec_inputs()

    def _L0_attn_setup():
        import jax, jax.numpy as jnp
        import numpy as np
        import math
        N_HEADS = 8

        def _head_dirs():
            t = np.array([[(i >> 2 & 1) * 2 - 1, (i >> 1 & 1) * 2 - 1, (i & 1) * 2 - 1] for i in range(8)], dtype=np.float32)
            return jnp.asarray(t / np.sqrt(3.0, dtype=np.float32))
        key = jax.random.key(seed)
        k1, k2, k3, k4 = jax.random.split(key, 4)
        B, T, C = (2, 256, 128)
        x = jax.random.normal(k1, (B, T, C), dtype=jnp.float32)
        w_qkv = jax.random.normal(k2, (C, 3 * C), dtype=jnp.float32) * (1.0 / math.sqrt(C))
        w_out = jax.random.normal(k3, (C, C), dtype=jnp.float32) * (1.0 / math.sqrt(C))
        head_scales = jax.random.normal(k4, (N_HEADS,), dtype=jnp.float32) * 0.1
        return {'x': x, 'w_qkv': w_qkv, 'w_out': w_out, 'head_scales': head_scales}
    _L0_attn_all = _L0_attn_setup()
    _L0_attn_in = {k: v for k, v in _L0_attn_all.items() if k in ('w_qkv', 'w_out', 'head_scales')}
    del _L0_attn_all

    def _L0_xattn_setup():
        import jax, jax.numpy as jnp
        import numpy as np
        B, LQ, LK = (8, 256, 256)
        QD, KD, VD = (128, 64, 64)
        key = jax.random.key(seed)
        ks = jax.random.split(key, 9)
        s = 0.02
        return {'query': jax.random.normal(ks[0], (B, LQ, QD), jnp.float32), 'key': jax.random.normal(ks[1], (B, LK, KD), jnp.float32), 'value': jax.random.normal(ks[2], (B, LK, VD), jnp.float32), 'Wq': jax.random.normal(ks[3], (QD, QD), jnp.float32) * s, 'bq': jnp.zeros((QD,), jnp.float32), 'Wk': jax.random.normal(ks[4], (KD, QD), jnp.float32) * s, 'bk': jnp.zeros((QD,), jnp.float32), 'Wv': jax.random.normal(ks[5], (VD, QD), jnp.float32) * s, 'bv': jnp.zeros((QD,), jnp.float32)}
    _L0_xattn_all = _L0_xattn_setup()
    _L0_xattn_in = {k: v for k, v in _L0_xattn_all.items() if k in ('Wq', 'bq', 'Wk', 'bk', 'Wv', 'bv')}
    del _L0_xattn_all

    def _L0_ffn_setup():
        import jax, jax.numpy as jnp
        import numpy as np
        H = 128
        I = 4 * H
        E = 8
        K = 2
        B, S = (2, 128)
        STD = 0.02 / np.sqrt(H)
        key = jax.random.key(seed)
        ks = jax.random.split(key, 8)
        x = jax.random.normal(ks[0], (B, S, H), dtype=jnp.float32)
        gate_w = jax.random.normal(ks[1], (H, E), dtype=jnp.float32) * STD
        bias = jnp.zeros((E,), dtype=jnp.float32)
        up_w = jax.random.normal(ks[2], (E, H, I), dtype=jnp.float32) * STD
        up_b = jnp.zeros((E, I), dtype=jnp.float32)
        down_w = jax.random.normal(ks[3], (E, I, H), dtype=jnp.float32) * STD
        down_b = jnp.zeros((E, H), dtype=jnp.float32)
        sw_up = jax.random.normal(ks[4], (H, I), dtype=jnp.float32) * STD
        sb_up = jnp.zeros((I,), dtype=jnp.float32)
        sw_down = jax.random.normal(ks[5], (I, H), dtype=jnp.float32) * STD
        sb_down = jnp.zeros((H,), dtype=jnp.float32)
        return {'x': x, 'gate_w': gate_w, 'bias': bias, 'up_w': up_w, 'up_b': up_b, 'down_w': down_w, 'down_b': down_b, 'sw_up': sw_up, 'sb_up': sb_up, 'sw_down': sw_down, 'sb_down': sb_down}
    _L0_ffn_all = _L0_ffn_setup()
    _L0_ffn_in = {k: v for k, v in _L0_ffn_all.items() if k in ('gate_w', 'bias', 'up_w', 'up_b', 'down_w', 'down_b', 'sw_up', 'sb_up', 'sw_down', 'sb_down')}
    del _L0_ffn_all
    return {'x': x, 'ctx_512': ctx_512, 'L0_attn_w_qkv': _L0_attn_in['w_qkv'], 'L0_attn_w_out': _L0_attn_in['w_out'], 'L0_attn_head_scales': _L0_attn_in['head_scales'], 'L0_xattn_Wq': _L0_xattn_in['Wq'], 'L0_xattn_bq': _L0_xattn_in['bq'], 'L0_xattn_Wk': _L0_xattn_in['Wk'], 'L0_xattn_bk': _L0_xattn_in['bk'], 'L0_xattn_Wv': _L0_xattn_in['Wv'], 'L0_xattn_bv': _L0_xattn_in['bv'], 'L0_ffn_gate_w': _L0_ffn_in['gate_w'], 'L0_ffn_bias': _L0_ffn_in['bias'], 'L0_ffn_up_w': _L0_ffn_in['up_w'], 'L0_ffn_up_b': _L0_ffn_in['up_b'], 'L0_ffn_down_w': _L0_ffn_in['down_w'], 'L0_ffn_down_b': _L0_ffn_in['down_b'], 'L0_ffn_sw_up': _L0_ffn_in['sw_up'], 'L0_ffn_sb_up': _L0_ffn_in['sb_up'], 'L0_ffn_sw_down': _L0_ffn_in['sw_down'], 'L0_ffn_sb_down': _L0_ffn_in['sb_down']}

def reference(x, ctx_512, L0_attn_w_qkv, L0_attn_w_out, L0_attn_head_scales, L0_xattn_Wq, L0_xattn_bq, L0_xattn_Wk, L0_xattn_bk, L0_xattn_Wv, L0_xattn_bv, L0_ffn_gate_w, L0_ffn_bias, L0_ffn_up_w, L0_ffn_up_b, L0_ffn_down_w, L0_ffn_down_b, L0_ffn_sw_up, L0_ffn_sb_up, L0_ffn_sw_down, L0_ffn_sb_down):
    import jax
    import jax.numpy as jnp

    def _L0_attn_ref(x, w_qkv, w_out, head_scales):
        import jax, jax.numpy as jnp
        import numpy as np
        import math
        N_HEADS = 8

        def _head_dirs():
            t = np.array([[(i >> 2 & 1) * 2 - 1, (i >> 1 & 1) * 2 - 1, (i & 1) * 2 - 1] for i in range(8)], dtype=np.float32)
            return jnp.asarray(t / np.sqrt(3.0, dtype=np.float32))
        B, T, C = x.shape
        H = N_HEADS
        hd = C // H
        scale = 1.0 / math.sqrt(hd)
        dirs = _head_dirs()
        qkv = (x @ w_qkv).reshape(B, T, 3, H, hd)
        q = jnp.transpose(qkv[:, :, 0], (0, 2, 1, 3))
        k = jnp.transpose(qkv[:, :, 1], (0, 2, 1, 3))
        v = jnp.transpose(qkv[:, :, 2], (0, 2, 1, 3))
        scores = jnp.einsum('bhqd,bhkd->bhqk', q, k) * scale
        causal = jnp.tril(jnp.ones((T, T), dtype=bool))
        scores = jnp.where(causal[None, None], scores, -jnp.inf)
        q_proj = jnp.einsum('bhtd,hd->bht', q[..., :3], dirs)
        k_proj = jnp.einsum('bhtd,hd->bht', k[..., :3], dirs)
        geo = q_proj[..., :, None] * k_proj[..., None, :]
        scores = scores + head_scales[None, :, None, None] * geo
        attn = jax.nn.softmax(scores, axis=-1)
        out = jnp.einsum('bhqk,bhkd->bqhd', attn, v).reshape(B, T, C)
        return out @ w_out

    def _L0_xattn_ref(query, key, value, Wq, bq, Wk, bk, Wv, bv):
        import jax, jax.numpy as jnp
        import numpy as np
        B, LQ, LK = (8, 256, 256)
        QD, KD, VD = (128, 64, 64)
        q = jnp.einsum('bld,de->ble', query, Wq) + bq
        k = jnp.einsum('bld,de->ble', key, Wk) + bk
        v = jnp.einsum('bld,de->ble', value, Wv) + bv
        scores = jnp.einsum('bqe,bke->bqk', q, k)
        attn = jax.nn.softmax(scores, axis=-1)
        out = jnp.einsum('bqk,bke->bqe', attn, v)
        return out

    def _L0_ffn_ref(x, gate_w, bias, up_w, up_b, down_w, down_b, sw_up, sb_up, sw_down, sb_down):
        import jax, jax.numpy as jnp
        import numpy as np
        H = 128
        I = 4 * H
        E = 8
        K = 2
        B, S = (2, 128)
        STD = 0.02 / np.sqrt(H)
        b, s, h = x.shape
        xf = x.reshape(-1, h)
        T = xf.shape[0]
        scores = jax.nn.sigmoid(xf @ gate_w + bias)
        top_scores, top_idx = jax.lax.top_k(scores, K)
        top_scores = top_scores / (jnp.sum(top_scores, axis=-1, keepdims=True) + 1e-06)
        w = jnp.zeros((T, E), dtype=xf.dtype).at[jnp.arange(T)[:, None], top_idx].add(top_scores)
        up = jnp.einsum('th,ehi->tei', xf, up_w) + up_b
        hact = jax.nn.gelu(up, approximate=False)
        eo = jnp.einsum('tei,eih->teh', hact, down_w) + down_b
        combined = jnp.einsum('teh,te->th', eo * 0.1, w)
        shared = (jax.nn.gelu(xf @ sw_up + sb_up, approximate=False) @ sw_down + sb_down) * 0.1
        out = (shared + combined).reshape(b, s, h)
        out = out / (jnp.max(jnp.abs(out), axis=-1, keepdims=True) + 1e-06)
        return out
    x = x + _L0_attn_ref(_layernorm(x, axis=-1), L0_attn_w_qkv, L0_attn_w_out, L0_attn_head_scales)
    x = x + _L0_xattn_ref(_layernorm(x, axis=-1), ctx_512, ctx_512, L0_xattn_Wq, L0_xattn_bq, L0_xattn_Wk, L0_xattn_bk, L0_xattn_Wv, L0_xattn_bv)
    x = x + _L0_ffn_ref(_layernorm(x, axis=-1), L0_ffn_gate_w, L0_ffn_bias, L0_ffn_up_w, L0_ffn_up_b, L0_ffn_down_w, L0_ffn_down_b, L0_ffn_sw_up, L0_ffn_sb_up, L0_ffn_sw_down, L0_ffn_sb_down)
    return x

_drawn_inputs = setup_inputs


def setup_inputs(seed=0):
    import zlib

    import numpy as np

    out = dict(_drawn_inputs(seed))
    spreads = {'L0_xattn_bq': (0.0, 0.513),
     'L0_xattn_bk': (0.0, 0.8),
     'L0_xattn_bv': (0.0, 0.1),
     'L0_ffn_bias': (0.0, 0.1),
     'L0_ffn_up_b': (0.0, 0.8),
     'L0_ffn_down_b': (0.0, 0.1),
     'L0_ffn_sb_up': (0.0, 0.8),
     'L0_ffn_sb_down': (0.0, 0.1)}
    factors = {'L0_xattn_Wq': 3.53,
     'L0_xattn_Wk': 2.983,
     'L0_ffn_up_w': 8.0,
     'L0_ffn_down_w': 8.0,
     'L0_ffn_sw_up': 8.0,
     'L0_ffn_sw_down': 7.579}
    for name, (base, spread) in spreads.items():
        noise = np.random.default_rng([zlib.crc32(name.encode()), seed]).standard_normal(out[name].shape)
        drawn = base * np.exp(spread * noise) if base else spread * noise
        out[name] = jnp.asarray(drawn.astype(out[name].dtype))
    for name, factor in factors.items():
        out[name] = (out[name] * factor).astype(out[name].dtype)
    return out
```

```python
import math
from contextlib import ExitStack

import numpy as np

import concourse.bass as bass
from concourse import mybir

F32 = mybir.dt.float32
F32R = mybir.dt.float32r
BF16 = mybir.dt.bfloat16
U32 = mybir.dt.uint32
ALU = mybir.AluOpType
ACT = mybir.ActivationFunctionType
X = mybir.AxisListType.X

P = 128
NEG = -1.0e30


def schedule(B):
    order = [("ctx", 0), ("norm1", 0), ("project", 0)]
    for i in range(B + 1):
        if i < B:
            order.append(("self_max", i))
        if i + 1 < B:
            order.append(("norm1", i + 1))
        if i >= 1:
            order.append(("cross_max", i - 1))
        if i + 1 < B:
            order.append(("project", i + 1))
        if i < B:
            order += [("self_shift", i), ("self_attend", i)]
        if i >= 1:
            order += [("cross_shift", i - 1), ("cross_attend", i - 1)]
        if i + 1 < B:
            order.append(("ctx", i + 1))
        if i < B:
            order += [("self_norm", i), ("self_out", i)]
        if i >= 1:
            order.append(("cross_out", i - 1))
        if i < B:
            order.append(("query", i))
        if i >= 1:
            order += [("gate", i - 1), ("route", i - 1)]
    return order


def decoder_layer(nc, x, ctx_in, w_qkv, w_out, head_scales, Wq, bq, Wk, bk, Wv, bv, gate_w,
                  gate_b, up_w, up_b, down_w, down_b, sw_up, sb_up, sw_down, sb_down, dirs_outer,
                  out):
    B, T, C = x.shape
    H = head_scales.shape[0]
    D = C // H
    NK, KD = ctx_in.shape[1:]
    E, _, I = up_w.shape
    TT = T // P
    NT = B * TT
    PAIRS = H // 2
    KF = NK // P
    KR = NK - KF * P
    KT = KF + 1
    NKE = KF * P + KR + KR % 2
    IT = I // P
    HALF = B * T // 2
    SCALE = 1.0 / math.sqrt(D)
    CH = [0, 402, 802, 1202, NKE]
    assert C == P and T == 2 * P and D == 16 and KD == 64 and HALF == 512

    SCHED = schedule(B)

    def turns(uses):
        at, first = 0, {}
        for unit in SCHED:
            first[unit] = at
            at += uses.get(unit[0], 0)
        return first, at

    W0, W_ALL = turns({"ctx": 4, "project": 6, "self_max": 2 * PAIRS, "self_norm": 1,
                       "self_out": 1, "cross_max": TT * 4, "cross_out": 1, "gate": 1})
    T0, T_ALL = turns({"project": 2, "self_shift": 1, "self_out": 1, "query": 2,
                       "cross_shift": 1, "gate": 1, "route": 1})
    S0, S_ALL = turns({"self_attend": H, "cross_attend": (KT + 1) // 2})
    O0, O_ALL = turns({"self_attend": 1, "cross_attend": 1})
    L0, L_ALL = turns({"norm1": 1, "self_out": 1, "cross_out": 1})
    LOW, LOW_ALL = turns({"project": 1, "query": 1, "gate": 1})
    TURNED = {L0["norm1", b]: T0["project", b] for b in range(B)}
    TURNED |= {L0["self_out", b]: T0["query", b] for b in range(B)}
    TURNED |= {L0["cross_out", b]: T0["gate", b] for b in range(B)}
    NH = 12
    NW, NS, NP = 4, 2, 6

    with ExitStack() as st:
        def sb(name, shape, dt=F32):
            return st.enter_context(nc.sbuf_tensor(name, shape, dt))

        def sem(name):
            return st.enter_context(nc.semaphore(name))

        work = [st.enter_context(nc.psum_tensor(f"work{i}", [P, 512], F32)) for i in range(NW)]
        score = [st.enter_context(nc.psum_tensor(f"score{i}", [P, 512], F32)) for i in range(NS)]
        turn = st.enter_context(nc.psum_tensor("turn", [P, 512], F32))
        attended = st.enter_context(nc.psum_tensor("attended", [P, 512], F32))

        ident = sb("ident", [P, P])
        identb = sb("identb", [P, P], BF16)
        ones = sb("ones", [P, P])
        causal_q = sb("causal_q", [P, P], BF16)
        causal_k = sb("causal_k", [P, P], BF16)
        aux_rows = sb("aux_rows", [P, 2, 1])
        low_q = sb("low_q", [P, 1])
        low_k = sb("low_k", [P, 1])
        low_c = sb("low_c", [P, 1])
        minus_half = sb("minus_half", [P, 2])
        iota_e = sb("iota_e", [P, 16])
        pick_f = sb("pick_f", [P, E + 1, 1])
        pick = sb("pick", [P, E + 1, P], F32R)

        x_in = sb("x_in", [P, NT, C])
        x1 = sb("x1", [P, NT, C])
        x2 = sb("x2", [P, NT, C])
        wqkv = sb("wqkv", [P, 3 * C])
        wout = sb("wout", [P, C])
        hs = sb("hs", [P, 1])
        dirs = sb("dirs", [P, P])
        geo = sb("geo", [P, P])
        geo_d = sb("geo_d", [P, P])
        wkT = sb("wkT", [P, P])
        wqk_h = sb("wqk_h", [P, PAIRS + H, P], F32R)
        wqk_l = sb("wqk_l", [P, PAIRS + H, P], F32R)
        wq_x = sb("wq_x", [P, P])
        bq_x = sb("bq_x", [P, 1])
        wk_x = sb("wk_x", [KD, P])
        bk_x = sb("bk_x", [P, 1])
        wqT_x = sb("wqT_x", [P, P])
        wka = sb("wka", [P, 2 * P])
        w2 = sb("w2", [P, 2 * P])
        w2_h = sb("w2_h", [P, 2 * P], F32R)
        w2_l = sb("w2_l", [P, 2 * P], F32R)
        b2 = sb("b2", [P, 2])
        wva = sb("wva", [KD + 1, P + 2])
        gate = sb("gate", [P, E])
        gate_bias = sb("gate_bias", [P, E])
        bias_f = sb("bias_f", [P, P])
        bias_h = sb("bias_h", [P, P], F32R)
        bias_l = sb("bias_l", [P, P], F32R)
        up_bias = sb("up_bias", [P, E + 1, IT])

        stats = sb("stats", [P, TT, 6])
        mean_var = sb("mean_var", [P, TT, 2])
        var_eps = sb("var_eps", [P, TT])
        rstd = sb("rstd", [P, TT])
        xn = sb("xn", [P, 2, TT, C])
        xT = sb("xT", [P, 2, T])
        xT_h = sb("xT_h", [P, 2, T], F32R)
        xT_l = sb("xT_l", [P, 2, T], F32R)
        all_h = sb("all_h", [P, 2, 512], F32R)
        qS = sb("qS", [P, 2, PAIRS, T], F32R)
        kS = sb("kS", [P, 2, H, T], F32R)
        v = sb("v", [P, 2, TT, H, 32])
        nmax = sb("nmax", [P, TT, H])
        nmax_h = sb("nmax_h", [P, TT, H], F32R)
        shift = sb("shift", [P, TT, PAIRS, 32])
        probs = sb("probs", [P, NP, 512])
        wqk = probs[:, 0:3, :].rearrange("p n (c k) -> p (n c) k", k=P)
        oT = sb("oT", [P, 512])
        rden = sb("rden", [P, TT, H, 1])
        o = sb("o", [P, TT, H, D])
        onT = sb("onT", [P, T])

        c_nat = sb("c_nat", [P, B, KT, KD + 1])
        c_hl = sb("c_hl", [P, KT, P], F32R)
        cA = sb("cA", [P, 2, NKE], F32R)
        cB = sb("cB", [P, 2, NKE], F32R)
        x2T = sb("x2T", [P, T])
        x2T_h = sb("x2T_h", [P, T], F32R)
        x2T_l = sb("x2T_l", [P, T], F32R)
        qA = sb("qA", [P, 2, T], F32R)
        qB = sb("qB", [P, 2, T], F32R)
        qB_f = sb("qB_f", [P, T])
        qB_h = sb("qB_h", [P, T], F32R)
        cmax = sb("cmax", [P, TT, 4])
        cnmax = sb("cnmax", [P, TT])
        cnmax_h = sb("cnmax_h", [P, TT], F32R)
        cshift = sb("cshift", [P, TT, P])
        cshiftT = sb("cshiftT", [P, T])
        coT = sb("coT", [KD + 1, T])
        crden = sb("crden", [P, TT, 1])

        x3T = sb("x3T", [P, 2, T])
        x3T_h = sb("x3T_h", [P, B * T], F32R)
        x3T_l = sb("x3T_l", [P, B * T], F32R)
        z = sb("z", [P, TT, E])
        ez = sb("ez", [P, TT, E])
        sig = sb("sig", [P, TT, E])
        top = sb("top", [P, TT, 8])
        top_i = sb("top_i", [P, TT, 8], U32)
        top_f = sb("top_f", [P, TT, 8])
        den = sb("den", [P, TT])
        share = sb("share", [P, TT, 2])
        wsel = sb("wsel", [P, 2, 16])
        wgt = sb("wgt", [P, TT, 16])
        wgt_h = sb("wgt_h", [P, TT, 16], F32R)
        wgt_hl = sb("wgt_hl", [P, TT, P])
        wgtT = sb("wgtT", [P, B * T], F32R)
        up_raw = sb("up_raw", [P, 2, I])
        up_h = sb("up_h", [P, 2, IT, P], F32R)
        up_l = sb("up_l", [P, 2, IT, P], F32R)
        down = sb("down", [P, 2, IT, C])
        hid = sb("hid", [P, NH - NP, HALF])
        peak = sb("peak", [P, NT])
        free = c_nat[:].rearrange("p b j d -> p (b j d)")
        wide = free[:, 0:2 * B * T].rearrange("p (e t) -> p e t", e=2)
        acc = free[:, 2 * B * T:3 * B * T].rearrange("p (s t) -> p s t", s=2)
        part = x1[:].rearrange("p (s i) c -> p s (i c)", s=2)
        y = x_in

        def hidden_at(n):
            n %= NH
            return probs[:, n, :] if n < NP else hid[:, n - NP, :]

        x_loaded = [sem(f"x_loaded{b}") for b in range(B)]
        c_loaded = [sem(f"c_loaded{b}") for b in range(B)]
        attn_loaded = sem("attn_loaded")
        cross_loaded = sem("cross_loaded")
        ffn_loaded = sem("ffn_loaded")
        up_loaded = [sem(f"up_loaded{i}") for i in range(2)]
        down_loaded = [sem(f"down_loaded{i}") for i in range(2)]
        pool_chain = sem("pool_chain")
        ready_consts = sem("ready_consts")
        dve_chain = sem("dve_chain")
        weights_turned = sem("weights_turned")
        weights_taken = sem("weights_taken")
        ready_weights = sem("ready_weights")
        var_ready = sem("var_ready")
        rstd_ready = sem("rstd_ready")
        xn_ready = sem("xn_ready")
        low_ready = sem("low_ready")
        work_filled = sem("work_filled")
        work_freed = sem("work_freed")
        all_h_ready = sem("all_h_ready")
        turn_filled = sem("turn_filled")
        turn_freed = sem("turn_freed")
        shift_ready = sem("shift_ready")
        score_filled = sem("score_filled")
        probs_ready = sem("probs_ready")
        probs_used = sem("probs_used")
        attended_freed = sem("attended_freed")
        c_split = sem("c_split")
        cB_ready = sem("cB_ready")
        qB_ready = sem("qB_ready")
        cshift_ready = sem("cshift_ready")
        qB_shifted = sem("qB_shifted")
        ez_ready = sem("ez_ready")
        mix_ready = sem("mix_ready")
        up_split = sem("up_split")
        up_filled = sem("up_filled")
        hid_ready = sem("hid_ready")
        wide_filled = sem("wide_filled")
        wide_ready = sem("wide_ready")
        hid_used = sem("hid_used")
        bias_filled = sem("bias_filled")
        down_taken = sem("down_taken")
        acc_ready = sem("acc_ready")
        acc_turned = sem("acc_turned")
        y_ready = sem("y_ready")
        y_stored = sem("y_stored")

        def f(ap):
            return ap.bitcast(F32)

        block = st.enter_context(nc.Block())

        @block.sync
        def _(sp):
            def rows(t):
                return t.rearrange("(i p) c -> p i c", p=P)

            def load_x(b):
                sp.dma_start(x_in[:, TT * b:TT * b + TT, :], rows(x[b])).then_inc(x_loaded[b], 16)

            def load_ctx(b):
                sp.dma_start(c_nat[:, b, 0:KF, 0:KD],
                             ctx_in[b, 0:KF * P, :].rearrange("(p j) d -> p j d", j=KF)
                             ).then_inc(c_loaded[b], 16)
                sp.dma_start(c_nat[0:KR, b, KF, 0:KD], ctx_in[b, KF * P:NK, :]
                             ).then_inc(c_loaded[b], 16)
                sp.dma_start(c_nat[KR:KR + 1, b, KF, 0:KD], ctx_in[b, NK - 1:NK, :]
                             ).then_inc(c_loaded[b], 16)

            load_x(0)
            sp.dma_start(wqkv[:], w_qkv).then_inc(attn_loaded, 16)
            for h in range(H):
                sp.dma_start(hs[D * h:D * h + D, :], head_scales[h:h + 1].rearrange("(a b) -> a b", b=1)
                             .to_broadcast([D, 1])).then_inc(attn_loaded, 16)
            sp.dma_start(dirs[:], dirs_outer).then_inc(attn_loaded, 16)
            load_ctx(0)
            load_x(1)
            sp.dma_start(wout[:], w_out).then_inc(cross_loaded, 16)
            sp.dma_start(wq_x[:], Wq).then_inc(cross_loaded, 16)
            sp.dma_start(wk_x[:], Wk).then_inc(cross_loaded, 16)
            sp.dma_start(bq_x[:], bq.rearrange("(a b) -> a b", b=1)).then_inc(cross_loaded, 16)
            sp.dma_start(bk_x[:], bk.rearrange("(a b) -> a b", b=1)).then_inc(cross_loaded, 16)
            sp.wait_ge(ready_consts, 1)
            sp.dma_start(wva[0:KD, 0:P], Wv).then_inc(cross_loaded, 16)
            sp.dma_start(wva[KD:KD + 1, 0:P], bv.rearrange("(a b) -> a b", a=1)
                         ).then_inc(cross_loaded, 16)
            for b in range(1, B):
                load_ctx(b)
                if b + 1 < B:
                    load_x(b + 1)
            sp.dma_start(gate[:], gate_w).then_inc(ffn_loaded, 16)
            sp.dma_start(gate_bias[:], gate_b.rearrange("(a e) -> a e", a=1).to_broadcast([P, E])
                         ).then_inc(ffn_loaded, 16)
            for r in (0, 16):
                sp.dma_start(bias_f[r:r + E, :], down_b).then_inc(ffn_loaded, 16)
                sp.dma_start(bias_f[r + E:r + E + 1, :], sb_down.rearrange("(a c) -> a c", a=1)
                             ).then_inc(ffn_loaded, 16)
            sp.dma_start(up_bias[:, 0:E, :], up_b.rearrange("e (p i) -> p e i", i=IT)
                         ).then_inc(ffn_loaded, 16)
            sp.dma_start(up_bias[:, E, :], sb_up.rearrange("(p i) -> p i", i=IT)
                         ).then_inc(ffn_loaded, 16)
            for e in range(E + 1):
                if e >= 2:
                    sp.wait_ge(up_split, e - 1)
                sp.dma_start(up_raw[:, e % 2, :], up_w[e] if e < E else sw_up
                             ).then_inc(up_loaded[e % 2], 16)
                if e >= 2:
                    sp.wait_ge(hid_used, 2 * IT * (e - 1))
                sp.dma_start(down[:, e % 2, :, :], (down_w[e] if e < E else sw_down)
                             .rearrange("(p i) c -> p i c", i=IT)).then_inc(down_loaded[e % 2], 16)
            for b in range(B):
                sp.wait_ge(y_ready, b + 1)
                sp.dma_start(rows(out[b]), y[:, TT * b:TT * b + TT, :]).then_inc(y_stored, 16)
            sp.wait_ge(y_stored, 16 * B)

        @block.gpsimd
        def _(pool):
            done = [0]

            def link(ins):
                done[0] += 1
                ins.then_inc(pool_chain, 1)
                pool.wait_ge(pool_chain, done[0])

            g = nc.gpsimd
            link(g.memset(wva[:], 0.0))
            link(g.memset(bias_f[:], 0.0))
            g.memset(wva[KD:KD + 1, P:P + 1], 1.0).then_inc(ready_consts, 1)
            pool.wait_ge(ready_consts, 1)
            link(g.memset(ident[:], 0.0))
            link(g.memset(causal_q[:], 0.0))
            link(g.memset(causal_k[:], 0.0))
            link(g.memset(ones[:], 1.0))
            link(g.memset(aux_rows[:], 0.0))
            link(g.memset(wqk, 0.0))
            link(g.memset(low_q[:], 0.0))
            link(g.memset(low_k[:], 0.0))
            link(g.memset(low_c[:], 0.0))
            link(g.memset(wka[:], 0.0))
            link(g.memset(low_q[32:64, :], -1.0))
            link(g.memset(low_k[64:96, :], -1.0))
            link(g.memset(low_c[0:64, :], -1.0))
            link(g.affine_select(out=ident[:], in_=ident[:], compare_op=ALU.not_equal, fill=1.0,
                                 base=0, pattern=[[-1, P]], channel_multiplier=1))
            link(g.affine_select(out=causal_q[:], in_=causal_q[:], compare_op=ALU.is_ge, fill=NEG,
                                 base=0, pattern=[[-1, P]], channel_multiplier=1))
            link(g.affine_select(out=causal_k[:], in_=causal_k[:], compare_op=ALU.is_ge, fill=NEG,
                                 base=0, pattern=[[1, P]], channel_multiplier=-1))
            for a in range(2):
                for r in range(2):
                    part_rows = aux_rows[96:128, a, :]
                    link(g.affine_select(out=part_rows, in_=part_rows, compare_op=ALU.not_equal,
                                         fill=1.0, base=-(2 * a + r), pattern=[[0, 1]],
                                         channel_multiplier=1))
            link(g.affine_select(out=low_c[64:96, :], in_=low_c[64:96, :], compare_op=ALU.not_equal,
                                 fill=-1.0, base=-1, pattern=[[0, 1]], channel_multiplier=1))
            link(g.tensor_copy(identb[:], ident[:]))
            link(g.memset(minus_half[:], -0.5))
            link(g.memset(shift[:], 0.0))
            link(g.memset(cshift[:], 0.0))
            link(g.memset(wgt_hl[:], 0.0))
            link(g.memset(wgt[:], 0.0))
            link(g.memset(c_nat[:, :, :, KD:KD + 1], 1.0))
            link(g.memset(v[:, :, :, :, D + 1:32], 0.0))
            link(g.memset(v[:, :, :, :, D:D + 1], 1.0))
            link(g.iota(iota_e[:], pattern=[[1, 16]], base=0, channel_multiplier=0,
                        allow_small_or_imprecise_dtypes=True))
            link(g.memset(pick_f[:], 0.0))
            for r in (0, 16):
                link(g.affine_select(out=pick_f[:], in_=pick_f[:], compare_op=ALU.not_equal,
                                     fill=1.0, base=-r, pattern=[[-1, E + 1], [0, 1]],
                                     channel_multiplier=1))
            g.memset(wgt[:, :, E:E + 1], 0.1).then_inc(ready_consts, 1)
            pool.wait_ge(ready_consts, 2)

            for n in range(L_ALL):
                pool.wait_ge(var_ready, n + 1)
                g.tensor_tensor(rstd[:], var_eps[:], minus_half[:, 0:TT], ALU.pow
                                ).then_inc(rstd_ready, 1)

        @block.tensor
        def _(pe):
            mm = nc.tensor.matmul
            tr = nc.tensor.transpose

            def fill(ring, filled, freed, u):
                n = len(ring)
                if u >= n:
                    pe.wait_ge(freed, u - n + 1)
                return ring[u % n]

            def work_bank(u):
                return fill(work, work_filled, work_freed, u)

            def turn_bank(u):
                return fill([turn], turn_filled, turn_freed, u)

            def three(dst, w_h, w_l, x_h, x_l):
                mm(dst, w_h, x_h, start=True, stop=False)
                mm(dst, w_l, x_h, start=False, stop=False)
                return mm(dst, w_h, x_l, start=False, stop=True)

            pe.wait_ge(ready_consts, 2)
            pe.wait_ge(attn_loaded, 16 * (H + 2))
            tr(attended[:, 0:P], wqkv[:, C:2 * C], ident[:]).then_inc(weights_turned, 1)
            pe.wait_ge(cross_loaded, 16 * 7)
            tr(turn[:, P:2 * P], wq_x[:], ident[:])
            tr(turn[:, 2 * P:2 * P + KD], wk_x[:], ident[0:KD, 0:KD]).then_inc(weights_turned, 1)
            pe.wait_ge(weights_taken, 1)
            mm(score[0][:, 0:P], wkT[:], geo[:], start=True, stop=True).then_inc(weights_turned, 1)
            pe.wait_ge(weights_taken, 2)
            mm(score[1][:, P:3 * P], wqT_x[:], wka[:], start=True, stop=True)
            mm(score[1][:, 3 * P:3 * P + 1], wka[:, 0:P], bq_x[:], start=True, stop=True)
            mm(score[1][:, 3 * P + 1:3 * P + 2], wka[:, P:2 * P], bq_x[:], start=True, stop=True
               ).then_inc(weights_turned, 1)
            pe.wait_ge(ready_weights, 1)

            def turn_norm(n, dst_use):
                bank = turn_bank(dst_use)
                pe.wait_ge(xn_ready, n + 1)
                for t in range(TT):
                    last = tr(bank[:, t * P:(t + 1) * P], xn[:, n % 2, t, :], ident[:])
                last.then_inc(turn_filled, 1)

            def ctx(b):
                pe.wait_ge(c_split, b + 1)
                for i in range(4):
                    bank = work_bank(W0["ctx", b] + i)
                    for j in range(4 * i, min(4 * i + 4, KT)):
                        m = P if j < KF else NKE - KF * P
                        last = tr(bank[:, (j - 4 * i) * P:(j - 4 * i) * P + m],
                                  f(c_hl[0:m, j, :]), ident[0:m, 0:m])
                    last.then_inc(work_filled, 1)

            def project(b):
                turn_norm(L0["norm1", b], T0["project", b])
                pe.wait_ge(turn_freed, T0["project", b] + 1)
                bank = turn_bank(T0["project", b] + 1)
                for t in range(TT):
                    last = mm(bank[:, t * P:(t + 1) * P], xT[:, b % 2, t * P:(t + 1) * P],
                              wqkv[:, 2 * C:3 * C], start=True, stop=True)
                last.then_inc(turn_filled, 1)
                pe.wait_ge(low_ready, LOW["project", b] + 1)
                for i in range((PAIRS + H) // 2):
                    bank = work_bank(W0["project", b] + i)
                    for s in range(2):
                        c = 2 * i + s
                        last = three(bank[:, s * T:(s + 1) * T], wqk_h[:, c, :], wqk_l[:, c, :],
                                     xT_h[:, b % 2, :], xT_l[:, b % 2, :])
                    last.then_inc(work_filled, 1)

            def self_max(b):
                pe.wait_ge(work_freed, W0["project", b] + 6)
                for r in range(PAIRS):
                    for t in (1, 0):
                        n = (t + 1) * P
                        bank = work_bank(W0["self_max", b] + 2 * r + 1 - t)
                        dst = bank[:, 0:2 * n].rearrange("p (a k) -> p a k", a=2)
                        mm(dst, qS[0:96, b % 2, r, t * P:(t + 1) * P],
                           kS[0:96, b % 2, 2 * r:2 * r + 2, 0:n], start=True, stop=False)
                        mm(dst[:, :, t * P:n], identb[:],
                           causal_q[:].unsqueeze(1).to_broadcast([P, 2, P]),
                           start=False, stop=True).then_inc(work_filled, 1)

            def self_shift(b):
                bank = turn_bank(T0["self_shift", b])
                pe.wait_ge(shift_ready, b + 1)
                for t in range(TT):
                    last = tr(bank[:, t * P:(t + 1) * P],
                              shift[:, t, :, :].rearrange("p r c -> p (r c)"), ident[:])
                last.then_inc(turn_filled, 1)

            def self_attend(b):
                pe.wait_ge(turn_freed, T0["self_shift", b] + 1)
                for h in range(H + 2):
                    if h < H:
                        u = S0["self_attend", b] + h
                        bank = fill(score, score_filled, probs_ready, u)
                        mm(bank[:, P:3 * P], kS[:, b % 2, h, P:2 * P], qS[:, b % 2, h // 2, :],
                           start=True, stop=False)
                        mm(bank[:, 2 * P:3 * P], identb[:], causal_k[:], start=False, stop=True)
                        mm(bank[:, 0:2 * P], kS[:, b % 2, h, 0:P], qS[:, b % 2, h // 2, :],
                           start=True, stop=False)
                        mm(bank[:, 0:P], identb[:], causal_k[:], start=False, stop=True
                           ).then_inc(score_filled, 1)
                    if h % 4 == 1 and h >= 5:
                        group(b, h // 4 - 1)

            def group(b, g):
                if g == 0 and O0["self_attend", b] >= 1:
                    pe.wait_ge(attended_freed, O0["self_attend", b])
                u = S0["self_attend", b] + 4 * g
                pe.wait_ge(probs_ready, u + 4)
                for k in range(2):
                    for j in range(4):
                        s = (u + j) % NP
                        src = probs[:, s, 0:2 * P] if k == 0 else probs[:, s, 2 * P:3 * P]
                        last = mm(attended[32 * j:32 * j + 32, g * T + k * P:(g + 1) * T],
                                  v[:, b % 2, k, 4 * g + j, :], src, start=(k == 0), stop=(k == 1))
                        if k == 1:
                            last.then_inc(probs_used, 1)

            def self_norm(b):
                bank = work_bank(W0["self_norm", b])
                pe.wait_ge(attended_freed, O0["self_attend", b] + 1)
                for t in range(TT):
                    for g in range(2):
                        last = tr(bank[:, (2 * t + g) * P:(2 * t + g + 1) * P],
                                  oT[:, g * T + t * P:g * T + (t + 1) * P], ident[:])
                last.then_inc(work_filled, 1)

            def self_out(b):
                bank = turn_bank(T0["self_out", b])
                pe.wait_ge(work_freed, W0["self_norm", b] + 1)
                for t in range(TT):
                    last = tr(bank[:, t * P:(t + 1) * P],
                              o[:, t, :, :].rearrange("p h d -> p (h d)"), ident[:])
                last.then_inc(turn_filled, 1)
                pe.wait_ge(turn_freed, T0["self_out", b] + 1)
                bank = work_bank(W0["self_out", b])
                for t in range(TT):
                    last = mm(bank[:, t * P:(t + 1) * P], onT[:, t * P:(t + 1) * P], wout[:],
                              start=True, stop=True)
                last.then_inc(work_filled, 1)

            def query(b):
                turn_norm(L0["self_out", b], T0["query", b])
                pe.wait_ge(low_ready, LOW["query", b] + 1)
                bank = turn_bank(T0["query", b] + 1)
                for s in range(2):
                    cols = slice(s * P, (s + 1) * P)
                    last = three(bank[:, s * T:(s + 1) * T], w2_h[:, cols], w2_l[:, cols],
                                 x2T_h[:], x2T_l[:])
                last.then_inc(turn_filled, 1)

            def cross_max(b):
                pe.wait_ge(cB_ready, b + 1)
                pe.wait_ge(qB_ready, b + 1)
                for t in range(TT):
                    rows = slice(t * P, (t + 1) * P)
                    for i in range(4):
                        bank = work_bank(W0["cross_max", b] + 4 * t + i)
                        a, n = CH[i], CH[i + 1] - CH[i]
                        mm(bank[:, 0:n], qA[:, b % 2, rows], cA[:, b % 2, a:a + n],
                           start=True, stop=False)
                        mm(bank[:, 0:n], qB[:, b % 2, rows], cB[:, b % 2, a:a + n],
                           start=False, stop=True).then_inc(work_filled, 1)

            def cross_shift(b):
                bank = turn_bank(T0["cross_shift", b])
                pe.wait_ge(cshift_ready, b + 1)
                for t in range(TT):
                    last = tr(bank[:, t * P:(t + 1) * P], cshift[:, t, :], ident[:])
                last.then_inc(turn_filled, 1)

            def cross_attend(b):
                pe.wait_ge(qB_shifted, b + 1)
                pairs = (KT + 1) // 2

                def values(i):
                    u = S0["cross_attend", b] + i
                    if i == 0:
                        pe.wait_ge(attended_freed, O0["cross_attend", b])
                    pe.wait_ge(probs_ready, u + 1)
                    for j in range(2 * i, min(2 * i + 2, KT)):
                        m = P if j < KF else KR
                        last = mm(attended[0:KD + 1, 0:T], c_nat[0:m, b, j, :],
                                  probs[0:m, u % NP, (j % 2) * T:(j % 2 + 1) * T],
                                  start=(j == 0), stop=(j == KT - 1))
                    last.then_inc(probs_used, 1)

                for i in range(pairs + 2):
                    if i < pairs:
                        bank = fill(score, score_filled, probs_ready, S0["cross_attend", b] + i)
                        for j in range(2 * i, min(2 * i + 2, KT)):
                            m = P if j < KF else KR
                            dst = bank[0:m, (j % 2) * T:(j % 2 + 1) * T]
                            mm(dst, cA[:, b % 2, j * P:j * P + m], qA[:, b % 2, :],
                               start=True, stop=False)
                            last = mm(dst, cB[:, b % 2, j * P:j * P + m], qB[:, b % 2, :],
                                      start=False, stop=True)
                        last.then_inc(score_filled, 1)
                    if i >= 2:
                        values(i - 2)

            def cross_out(b):
                bank = work_bank(W0["cross_out", b])
                pe.wait_ge(attended_freed, O0["cross_attend", b] + 1)
                for t in range(TT):
                    last = mm(bank[:, t * 256:t * 256 + P + 2], coT[:, t * P:(t + 1) * P], wva[:],
                              start=True, stop=True)
                last.then_inc(work_filled, 1)

            def gate_(b):
                turn_norm(L0["cross_out", b], T0["gate", b])
                pe.wait_ge(turn_freed, T0["gate", b] + 1)
                bank = work_bank(W0["gate", b])
                for t in range(TT):
                    last = mm(bank[:, t * E:(t + 1) * E], x3T[:, b % 2, t * P:(t + 1) * P], gate[:],
                              start=True, stop=True)
                last.then_inc(work_filled, 1)

            def route(b):
                bank = turn_bank(T0["route", b])
                pe.wait_ge(mix_ready, b + 1)
                for t in range(TT):
                    last = tr(bank[:, t * P:(t + 1) * P], wgt_hl[:, t, :], ident[:])
                last.then_inc(turn_filled, 1)

            pe.wait_ge(ffn_loaded, 16 * 8)
            units = {"ctx": ctx, "project": project, "self_max": self_max, "self_shift": self_shift,
                     "self_attend": self_attend, "self_norm": self_norm, "self_out": self_out,
                     "query": query, "cross_max": cross_max, "cross_shift": cross_shift,
                     "cross_attend": cross_attend, "cross_out": cross_out, "gate": gate_,
                     "route": route}
            for name, b in SCHED:
                if name in units:
                    units[name](b)

            pe.wait_ge(turn_freed, T_ALL)
            pe.wait_ge(work_freed, W_ALL)
            pe.wait_ge(low_ready, LOW_ALL)
            pe.wait_ge(probs_ready, S_ALL)

            def up(e, i):
                if i == 0:
                    pe.wait_ge(up_split, e + 1)
                banks = []
                for s in range(2):
                    u = (e * IT + i) * 2 + s
                    if u >= NW:
                        pe.wait_ge(hid_ready, u - NW + 1)
                    banks.append(work[u % NW])
                w_h, w_l = up_h[:, e % 2, i, :], up_l[:, e % 2, i, :]
                half = [slice(s * HALF, (s + 1) * HALF) for s in range(2)]
                for s in range(2):
                    mm(banks[s][:], w_h, x3T_h[:, half[s]], start=True, stop=False)
                for s in range(2):
                    mm(banks[s][:], w_h, x3T_l[:, half[s]], start=False, stop=False)
                for s in range(2):
                    mm(banks[s][:], w_l, x3T_h[:, half[s]], start=False, stop=True
                       ).then_inc(up_filled, 1)

            def widen(e):
                for s in range(2):
                    n = 2 * e + s
                    if n:
                        pe.wait_ge(wide_ready, n)
                    mm(turn[:], pick[:, e, :], wgtT[:, s * HALF:(s + 1) * HALF],
                       start=True, stop=True).then_inc(wide_filled, 1)

            def down_(e, i):
                if i == 0:
                    pe.wait_ge(down_loaded[e % 2], 16 * (e // 2 + 1))
                    if e:
                        pe.wait_ge(down_taken, 2 * e)
                for s in range(2):
                    n = (e * IT + i) * 2 + s
                    pe.wait_ge(hid_ready, n + 1)
                    mm(score[s][:], down[:, e % 2, i, :], hidden_at(n), start=(i == 0),
                       stop=(i == IT - 1)).then_inc(hid_used, 1)

            for i in range(IT):
                up(0, i)
            for e in range(E + 1):
                widen(e)
                for i in range(IT):
                    if e < E:
                        up(e + 1, i)
                    down_(e, i)
            pe.wait_ge(hid_ready, 2 * IT * (E + 1))
            for s in range(2):
                half = slice(s * HALF, (s + 1) * HALF)
                mm(work[s][:], bias_h[:], wgtT[:, half], start=True, stop=False)
                mm(work[s][:], bias_l[:], wgtT[:, half], start=False, stop=True
                   ).then_inc(bias_filled, 1)
            for s in range(2):
                pe.wait_ge(acc_ready, s + 1)
                for t in range(4):
                    last = tr(score[s][:, t * P:(t + 1) * P], acc[:, s, t * P:(t + 1) * P], ident[:])
                last.then_inc(acc_turned, 1)

        @block.scalar
        def _(act):
            a = nc.scalar

            def copy(dst, src):
                return a.activation(dst, src, ACT.Copy)

            def ctx(b):
                pe_done = ("cross_attend", b - 2)
                if b >= 2:
                    act.wait_ge(score_filled, S0[pe_done] + (KT + 1) // 2)
                act.wait_ge(work_freed, W0["ctx", b] + 4)
                if b < 2:
                    act.wait_ge(ready_consts, 2)
                copy(cB[0:KD, b % 2, :], f(cA[0:KD, b % 2, :])).then_inc(cB_ready, 1)

            def norm_out(u, dst, dst_h, used):
                if used is not None:
                    act.wait_ge(*used)
                act.wait_ge(turn_filled, u + 1)
                copy(dst, turn[:, 0:T])
                copy(dst_h, turn[:, 0:T]).then_inc(turn_freed, 1)

            def project(b):
                used = (work_filled, W0["project", b - 2] + 6) if b >= 2 else None
                norm_out(T0["project", b], xT[:, b % 2, :], xT_h[:, b % 2, :], used)
                act.wait_ge(turn_filled, T0["project", b] + 2)
                if b >= 2:
                    act.wait_ge(probs_used, S0["self_attend", b - 2] + H)
                copy(v[:, b % 2, :, :, 0:D],
                     turn[:, 0:T].rearrange("p (t h d) -> p t h d", t=TT, d=D)
                     ).then_inc(turn_freed, 1)
                for i in range((PAIRS + H) // 2):
                    u = W0["project", b] + i
                    n = b * 6 + i
                    act.wait_ge(work_filled, u + 1)
                    if n >= 2:
                        m = n - 2
                        act.wait_ge(work_freed, W0["project", m // 6] + m % 6 + 1)
                    copy(all_h[0:96, n % 2, :], work[u % NW][0:96, :]).then_inc(all_h_ready, 1)

            def self_shift(b):
                act.wait_ge(turn_filled, T0["self_shift", b] + 1)
                for r in range(PAIRS):
                    last = copy(qS[96:128, b % 2, r, :], turn[32 * r:32 * r + 32, 0:T])
                last.then_inc(turn_freed, 1)

            def exp(u, m, n):
                act.wait_ge(score_filled, u + 1)
                if u >= NP:
                    act.wait_ge(probs_used, u - NP + 1)
                a.activation(probs[0:m, u % NP, 0:n], score[u % NS][0:m, 0:n], ACT.Exp
                             ).then_inc(probs_ready, 1)

            def self_attend(b):
                for h in range(H):
                    exp(S0["self_attend", b] + h, P, 3 * P)
                act.wait_ge(probs_used, S0["self_attend", b] + H)
                if b >= 1:
                    act.wait_ge(work_filled, W0["self_norm", b - 1] + 1)
                copy(oT[:], attended[:]).then_inc(attended_freed, 1)

            def self_out(b):
                act.wait_ge(turn_filled, T0["self_out", b] + 1)
                if b >= 1:
                    act.wait_ge(work_filled, W0["self_out", b - 1] + 1)
                copy(onT[:], turn[:, 0:T]).then_inc(turn_freed, 1)

            def query(b):
                used = (turn_filled, T0["query", b - 1] + 2) if b else None
                norm_out(T0["query", b], x2T[:], x2T_h[:], used)
                u = T0["query", b] + 1
                act.wait_ge(turn_filled, u + 1)
                if b >= 1:
                    act.wait_ge(qB_ready, b)
                if b >= 2:
                    act.wait_ge(score_filled, S0["cross_attend", b - 2] + (KT + 1) // 2)
                a.activation(qA[:, b % 2, :], turn[:, 0:T], ACT.Identity, bias=b2[:, 0:1])
                a.activation(qB_f[:], turn[:, T:2 * T], ACT.Identity, bias=b2[:, 1:2])
                a.activation(qB_h[:], turn[:, T:2 * T], ACT.Identity, bias=b2[:, 1:2]
                             ).then_inc(turn_freed, 1)

            def cross_shift(b):
                act.wait_ge(turn_filled, T0["cross_shift", b] + 1)
                if b:
                    act.wait_ge(qB_shifted, b)
                copy(cshiftT[64:128, :], turn[64:128, 0:T]).then_inc(turn_freed, 1)

            def cross_attend(b):
                for i in range((KT + 1) // 2):
                    full = 2 * i + 2 <= KF
                    exp(S0["cross_attend", b] + i, P if full else KR, 2 * T if full else T)
                act.wait_ge(probs_used, S0["cross_attend", b] + (KT + 1) // 2)
                if b:
                    act.wait_ge(work_filled, W0["cross_out", b - 1] + 1)
                copy(coT[:], attended[0:KD + 1, 0:T]).then_inc(attended_freed, 1)

            def gate_(b):
                used = (work_filled, W0["gate", b - 2] + 1) if b >= 2 else None
                norm_out(T0["gate", b], x3T[:, b % 2, :], x3T_h[:, b * T:(b + 1) * T], used)
                act.wait_ge(work_freed, W0["gate", b] + 1)
                a.activation(ez[:], z[:], ACT.Exp, scale=-1.0).then_inc(ez_ready, 1)

            def route(b):
                act.wait_ge(turn_filled, T0["route", b] + 1)
                copy(wgtT[:, b * T:(b + 1) * T], turn[:, 0:T]).then_inc(turn_freed, 1)

            act.wait_ge(ready_weights, 1)
            units = {"ctx": ctx, "project": project, "self_shift": self_shift,
                     "self_attend": self_attend, "self_out": self_out, "query": query,
                     "cross_shift": cross_shift, "cross_attend": cross_attend, "gate": gate_,
                     "route": route}
            for name, b in SCHED:
                if name in units:
                    units[name](b)

            act.wait_ge(ffn_loaded, 16 * 8)

            def hidden(e, i):
                for s in range(2):
                    n = (e * IT + i) * 2 + s
                    act.wait_ge(up_filled, n + 1)
                    if n >= NH:
                        act.wait_ge(hid_used, n - NH + 1)
                    a.activation(hidden_at(n), work[n % NW][:], ACT.Gelu,
                                 bias=up_bias[:, e, i:i + 1]).then_inc(hid_ready, 1)

            def widen(e):
                for s in range(2):
                    act.wait_ge(wide_filled, 2 * e + s + 1)
                    if e >= 2:
                        act.wait_ge(down_taken, 2 * (e - 1))
                    copy(wide[:, e % 2, s * HALF:(s + 1) * HALF], turn[:]).then_inc(wide_ready, 1)

            for i in range(IT):
                hidden(0, i)
            for e in range(E + 1):
                widen(e)
                if e < E:
                    for i in range(IT):
                        hidden(e + 1, i)

        @block.vector
        def _(dve):
            d = nc.vector
            done = [0]

            def link(ins):
                done[0] += 1
                ins.then_inc(dve_chain, 1)
                dve.wait_ge(dve_chain, done[0])

            dve.wait_ge(attn_loaded, 16 * (H + 2))
            dve.wait_ge(ready_consts, 2)
            link(d.tensor_scalar(geo_d[:], dirs[:], hs[:, 0:1], None, ALU.mult))
            link(d.scalar_tensor_tensor(out=geo[:], in0=ident[:], scalar=SCALE, in1=geo_d[:],
                                        op0=ALU.mult, op1=ALU.add))
            dve.wait_ge(weights_turned, 1)
            d.tensor_copy(wkT[:], attended[:, 0:P]).then_inc(weights_taken, 1)
            dve.wait_ge(weights_turned, 2)
            dve.wait_ge(cross_loaded, 16 * 7)
            d.tensor_copy(wqT_x[:], turn[:, P:2 * P])
            for i in range(3):
                d.tensor_copy(wka[:, i * KD:(i + 1) * KD], turn[:, 2 * P:2 * P + KD])
            d.tensor_copy(wka[:, 3 * KD:3 * KD + 2], bk_x[:].to_broadcast([P, 2])
                          ).then_inc(weights_taken, 1)
            for i in range(3):
                d.tensor_copy(wqk[:, 0:PAIRS, 32 * i:32 * i + 32],
                              wqkv[:, 0:C].rearrange("p (r c) -> p r c", c=32))
            dve.wait_ge(weights_turned, 3)
            for i in range(3):
                for s in range(2):
                    last = d.tensor_copy(
                        wqk[:, PAIRS:, :].rearrange("p (r a) c -> p r a c", a=2)
                        [:, :, s, 32 * i + D * s:32 * i + D * s + D],
                        score[0][:, 0:P].rearrange("p (r a c) -> p r a c", a=2, c=D)[:, :, s, :])
            link(last)
            link(d.tensor_copy(wqk_h[:], wqk))
            link(d.tensor_tensor(wqk_l[:], wqk, f(wqk_h[:]), ALU.subtract))
            dve.wait_ge(weights_turned, 4)
            link(d.tensor_copy(w2[:], score[1][:, P:3 * P]))
            d.tensor_copy(b2[:], score[1][:, 3 * P:3 * P + 2])
            link(d.tensor_copy(w2_h[:], w2[:]))
            d.tensor_tensor(w2_l[:], w2[:], f(w2_h[:]), ALU.subtract)
            for s in range(2):
                d.tensor_copy(kS[96:128, s, :, :].rearrange("p (r a) t -> p r a t", a=2)[:, :, 0, :],
                              aux_rows[96:128, 0:1, :].to_broadcast([32, PAIRS, T]))
                d.tensor_copy(kS[96:128, s, :, :].rearrange("p (r a) t -> p r a t", a=2)[:, :, 1, :],
                              aux_rows[96:128, 1:2, :].to_broadcast([32, PAIRS, T]))
                d.tensor_copy(cB[64:128, s, :], ones[64:128, 0:1].to_broadcast([64, NKE]))
            link(d.tensor_copy(pick[:], pick_f[:].to_broadcast([P, E + 1, P])))
            dve.wait_ge(ffn_loaded, 16 * 8)
            link(d.tensor_copy(bias_h[:], bias_f[:]))
            d.tensor_tensor(bias_l[:], bias_f[:], f(bias_h[:]), ALU.subtract
                            ).then_inc(ready_weights, 1)

            def norm(src, n):
                for t in range(TT):
                    link(d.bn_stats(stats[:, t, :], src[:, t, :]))
                    link(d.bn_aggr(mean_var[:, t, :], stats[:, t, :]))
                d.tensor_scalar(var_eps[:], mean_var[:, :, 1], 1e-5, None, ALU.add
                                ).then_inc(var_ready, 1)
                if n >= 2:
                    dve.wait_ge(turn_filled, TURNED[n - 2] + 1)
                dve.wait_ge(rstd_ready, n + 1)
                for t in range(TT):
                    last = d.tensor_scalar(xn[:, n % 2, t, :], src[:, t, :], mean_var[:, t, 0:1],
                                           rstd[:, t:t + 1], ALU.subtract, ALU.mult)
                last.then_inc(xn_ready, 1)

            def low_part(u, dst, full, high):
                dve.wait_ge(turn_freed, u + 1)
                d.tensor_tensor(dst, full, f(high), ALU.subtract).then_inc(low_ready, 1)

            def split_max(nm, nm_h, dst_h, dst_l):
                link(d.tensor_copy(nm_h, nm))
                d.tensor_copy(dst_h, f(nm_h))
                return d.tensor_tensor(dst_l, nm, f(nm_h), ALU.subtract)

            def ctx(b):
                dve.wait_ge(c_loaded[b], 48)
                if b:
                    dve.wait_ge(work_filled, W0["ctx", b - 1] + 4)
                for n, j in ((P, slice(0, KF)), (KR + 1, slice(KF, KT))):
                    link(d.tensor_copy(c_hl[0:n, j, 0:KD], c_nat[0:n, b, j, 0:KD]))
                    last = d.tensor_tensor(c_hl[0:n, j, KD:2 * KD], c_nat[0:n, b, j, 0:KD],
                                           f(c_hl[0:n, j, 0:KD]), ALU.subtract)
                last.then_inc(c_split, 1)
                if b >= 2:
                    dve.wait_ge(score_filled, S0["cross_attend", b - 2] + (KT + 1) // 2)
                for i in range(4):
                    u = W0["ctx", b] + i
                    a, n = 512 * i, min(512, NKE - 512 * i)
                    dve.wait_ge(work_filled, u + 1)
                    d.tensor_copy(cA[:, b % 2, a:a + n], work[u % NW][:, 0:n]
                                  ).then_inc(work_freed, 1)

            def norm1(b):
                dve.wait_ge(x_loaded[b], 16)
                norm(x_in[:, TT * b:TT * b + TT, :], L0["norm1", b])

            def project(b):
                low_part(T0["project", b], xT_l[:, b % 2, :], xT[:, b % 2, :], xT_h[:, b % 2, :])
                if b >= 2:
                    dve.wait_ge(score_filled, S0["self_attend", b - 2] + H)
                for i in range((PAIRS + H) // 2):
                    u = W0["project", b] + i
                    n = b * 6 + i
                    dve.wait_ge(all_h_ready, n + 1)
                    if i < PAIRS // 2:
                        dst, low = qS[0:96, b % 2, 2 * i:2 * i + 2, :], low_q
                    else:
                        k = 2 * i - PAIRS
                        dst, low = kS[0:96, b % 2, k:k + 2, :], low_k
                    d.scalar_tensor_tensor(
                        out=dst, in0=f(all_h[0:96, n % 2, :]).rearrange("p (a t) -> p a t", a=2),
                        scalar=low[0:96, 0:1],
                        in1=work[u % NW][0:96, :].rearrange("p (a t) -> p a t", a=2),
                        op0=ALU.mult, op1=ALU.add).then_inc(work_freed, 1)

            def self_max(b):
                for r in range(PAIRS):
                    for t in (1, 0):
                        u = W0["self_max", b] + 2 * r + 1 - t
                        n = (t + 1) * P
                        dve.wait_ge(work_filled, u + 1)
                        d.tensor_reduce(nmax[:, t, 2 * r:2 * r + 2],
                                        work[u % NW][:, 0:2 * n].rearrange("p (a k) -> p a k", a=2),
                                        X, ALU.max, negate=True).then_inc(work_freed, 1)
                dve.wait_ge(work_freed, W0["self_max", b] + 2 * PAIRS)
                if b:
                    dve.wait_ge(turn_filled, T0["self_shift", b - 1] + 1)
                link(d.tensor_copy(nmax_h[:], nmax[:]))
                for t in range(TT):
                    at = shift[:, t, :, 0:4].rearrange("p r (a l) -> p r a l", l=2)
                    hi = f(nmax_h[:, t, :]).rearrange("p (r a) -> p r a", a=2)
                    d.tensor_copy(at[:, :, :, 0], hi)
                    last = d.tensor_tensor(at[:, :, :, 1],
                                           nmax[:, t, :].rearrange("p (r a) -> p r a", a=2), hi,
                                           ALU.subtract)
                last.then_inc(shift_ready, 1)

            def self_norm(b):
                u = W0["self_norm", b]
                dve.wait_ge(work_filled, u + 1)
                if b:
                    dve.wait_ge(turn_filled, T0["self_out", b - 1] + 1)
                src = work[u % NW][:].rearrange("p (t h c) -> p t h c", t=TT, c=32)
                link(d.reciprocal(rden[:], src[:, :, :, D:D + 1]))
                d.tensor_tensor(o[:], src[:, :, :, 0:D], rden[:].to_broadcast([P, TT, H, D]),
                                ALU.mult).then_inc(work_freed, 1)

            def self_out(b):
                u = W0["self_out", b]
                tiles = slice(TT * b, TT * b + TT)
                dve.wait_ge(work_filled, u + 1)
                d.tensor_tensor(x1[:, tiles, :],
                                work[u % NW][:, 0:T].rearrange("p (t c) -> p t c", t=TT),
                                x_in[:, tiles, :], ALU.add).then_inc(work_freed, 1)
                dve.wait_ge(work_freed, u + 1)
                norm(x1[:, tiles, :], L0["self_out", b])

            def query(b):
                low_part(T0["query", b], x2T_l[:], x2T[:], x2T_h[:])
                dve.wait_ge(turn_freed, T0["query", b] + 2)
                if b >= 2:
                    dve.wait_ge(score_filled, S0["cross_attend", b - 2] + (KT + 1) // 2)
                d.scalar_tensor_tensor(out=qB[:, b % 2, :], in0=f(qB_h[:]), scalar=low_c[:, 0:1],
                                       in1=qB_f[:], op0=ALU.mult, op1=ALU.add
                                       ).then_inc(qB_ready, 1)

            def cross_max(b):
                for t in range(TT):
                    for i in range(4):
                        u = W0["cross_max", b] + 4 * t + i
                        dve.wait_ge(work_filled, u + 1)
                        d.tensor_reduce(cmax[:, t, i:i + 1], work[u % NW][:, 0:CH[i + 1] - CH[i]],
                                        X, ALU.max).then_inc(work_freed, 1)
                dve.wait_ge(work_freed, W0["cross_max", b] + 4 * TT)
                link(d.tensor_reduce(cnmax[:], cmax[:], X, ALU.max, negate=True))
                if b:
                    dve.wait_ge(turn_filled, T0["cross_shift", b - 1] + 1)
                split_max(cnmax[:], cnmax_h[:], cshift[:, :, KD + 2], cshift[:, :, KD + 3]
                          ).then_inc(cshift_ready, 1)

            def cross_shift(b):
                dve.wait_ge(turn_freed, T0["cross_shift", b] + 1)
                d.tensor_tensor(qB[64:128, b % 2, :], f(qB[64:128, b % 2, :]), cshiftT[64:128, :],
                                ALU.add).then_inc(qB_shifted, 1)

            def cross_out(b):
                u = W0["cross_out", b]
                dve.wait_ge(work_filled, u + 1)
                src = work[u % NW][:].rearrange("p (t c) -> p t c", t=TT)
                link(d.reciprocal(crden[:], src[:, :, P:P + 1]))
                for t in range(TT):
                    last = d.scalar_tensor_tensor(
                        out=x2[:, TT * b + t, :], in0=src[:, t, 0:P], scalar=crden[:, t, :],
                        in1=x1[:, TT * b + t, :], op0=ALU.mult, op1=ALU.add)
                last.then_inc(work_freed, 1)
                dve.wait_ge(work_freed, u + 1)
                norm(x2[:, TT * b:TT * b + TT, :], L0["cross_out", b])

            def gate_(b):
                low_part(T0["gate", b], x3T_l[:, b * T:(b + 1) * T], x3T[:, b % 2, :],
                         x3T_h[:, b * T:(b + 1) * T])
                u = W0["gate", b]
                dve.wait_ge(work_filled, u + 1)
                for t in range(TT):
                    last = d.tensor_tensor(z[:, t, :], work[u % NW][:, t * E:(t + 1) * E],
                                           gate_bias[:], ALU.add)
                last.then_inc(work_freed, 1)
                dve.wait_ge(ez_ready, b + 1)
                link(d.tensor_scalar(sig[:], ez[:], 1.0, None, ALU.add))
                link(d.reciprocal(ez[:], sig[:]))
                for t in range(TT):
                    link(d.max(top[:, t, :], ez[:, t, :]))
                    link(d.max_index(top_i[:, t, :], top[:, t, :], ez[:, t, :]))
                d.tensor_copy(top_f[:], top_i[:])
                link(d.scalar_tensor_tensor(out=den[:], in0=top[:, :, 0], scalar=1e-6,
                                            in1=top[:, :, 1], op0=ALU.add, op1=ALU.add))
                link(d.reciprocal(den[:], den[:]))
                for t in range(TT):
                    link(d.tensor_scalar(share[:, t, :], top[:, t, 0:2], den[:, t:t + 1], 0.1,
                                         ALU.mult, ALU.mult))
                    for k in range(2):
                        last = d.tensor_scalar(wsel[:, k, :], iota_e[:], top_f[:, t, k:k + 1],
                                               share[:, t, k:k + 1], ALU.is_equal, ALU.mult)
                    link(last)
                    link(d.tensor_tensor(wgt[:, t, 0:E], wsel[:, 0, 0:E], wsel[:, 1, 0:E], ALU.add))
                if b:
                    dve.wait_ge(turn_filled, T0["route", b - 1] + 1)
                link(d.tensor_copy(wgt_h[:], wgt[:]))
                d.tensor_copy(wgt_hl[:, :, 0:16], f(wgt_h[:]))
                d.tensor_tensor(wgt_hl[:, :, 16:32], wgt[:], f(wgt_h[:]), ALU.subtract
                                ).then_inc(mix_ready, 1)

            units = {"ctx": ctx, "norm1": norm1, "project": project, "self_max": self_max,
                     "self_norm": self_norm, "self_out": self_out, "query": query,
                     "cross_max": cross_max, "cross_shift": cross_shift, "cross_out": cross_out,
                     "gate": gate_}
            for name, b in SCHED:
                if name in units:
                    units[name](b)

            def split(e):
                dve.wait_ge(up_loaded[e % 2], 16 * (e // 2 + 1))
                if e >= 2:
                    dve.wait_ge(up_filled, 2 * IT * (e - 1))
                raw = up_raw[:, e % 2, :].rearrange("p (c i) -> p i c", i=IT)
                link(d.tensor_copy(up_h[:, e % 2, :, :], raw))
                d.tensor_tensor(up_l[:, e % 2, :, :], raw, f(up_h[:, e % 2, :, :]), ALU.subtract
                                ).then_inc(up_split, 1)

            split(0)
            split(1)
            for e in range(E + 1):
                dve.wait_ge(hid_used, 2 * IT * (e + 1))
                dve.wait_ge(wide_ready, 2 * e + 2)
                for s in range(2):
                    dst = acc[:, s, :] if e == 0 else part[:, s, :]
                    d.tensor_tensor(dst, score[s][:], wide[:, e % 2, s * HALF:(s + 1) * HALF],
                                    ALU.mult).then_inc(down_taken, 1)
                dve.wait_ge(down_taken, 2 * e + 2)
                if e:
                    for s in range(2):
                        last = d.tensor_tensor(acc[:, s, :], acc[:, s, :], part[:, s, :], ALU.add)
                    link(last)
                if e + 2 <= E:
                    split(e + 2)
            for s in range(2):
                dve.wait_ge(bias_filled, s + 1)
                d.tensor_tensor(acc[:, s, :], acc[:, s, :], work[s][:], ALU.add
                                ).then_inc(acc_ready, 1)
            for s in range(2):
                dve.wait_ge(acc_turned, s + 1)
                tiles = slice(4 * s, 4 * s + 4)
                src = score[s][:].rearrange("p (t c) -> p t c", t=4)
                link(d.tensor_reduce(peak[:, tiles], src, X, ALU.max, apply_absolute_value=True))
                link(d.tensor_scalar(peak[:, tiles], peak[:, tiles], 1e-6, None, ALU.add))
                link(d.reciprocal(peak[:, tiles], peak[:, tiles]))
                for t in range(4):
                    last = d.scalar_tensor_tensor(
                        out=y[:, 4 * s + t, :], in0=src[:, t, :], scalar=peak[:, 4 * s + t:4 * s + t + 1],
                        in1=x2[:, 4 * s + t, :], op0=ALU.mult, op1=ALU.add)
                    if t % TT == TT - 1:
                        last.then_inc(y_ready, 1)


_INS = ["x", "ctx_512", "L0_attn_w_qkv", "L0_attn_w_out", "L0_attn_head_scales", "L0_xattn_Wq",
        "L0_xattn_bq", "L0_xattn_Wk", "L0_xattn_bk", "L0_xattn_Wv", "L0_xattn_bv",
        "L0_ffn_gate_w", "L0_ffn_bias", "L0_ffn_up_w", "L0_ffn_up_b", "L0_ffn_down_w",
        "L0_ffn_down_b", "L0_ffn_sw_up", "L0_ffn_sb_up", "L0_ffn_sw_down", "L0_ffn_sb_down"]


def head_dirs_outer(heads, dim):
    m = np.zeros((heads * dim, heads * dim), np.float32)
    for h in range(heads):
        v = np.array([(h >> 2 & 1) * 2 - 1, (h >> 1 & 1) * 2 - 1, (h & 1) * 2 - 1], np.float32)
        m[h * dim:h * dim + 3, h * dim:h * dim + 3] = np.outer(v, v) / np.float32(3.0)
    return m


def kernel(**inputs):
    import concourse.bacc as bacc
    from concourse.bass_utils import run_bass_kernel_spmd

    nc = bacc.Bacc("TRN2", target_bir_lowering=False, num_devices=1)
    arrays, args = {}, []
    given = {n: np.ascontiguousarray(inputs[n]) for n in _INS}
    given["dirs_outer"] = head_dirs_outer(8, 16)
    for name, a in given.items():
        arrays[f"in_{name}"] = a
        args.append(nc.dram_tensor(f"in_{name}", a.shape, mybir.dt.from_np(a.dtype),
                                   kind="ExternalInput").ap())
    args.append(nc.dram_tensor("out_x", given["x"].shape, F32, kind="ExternalOutput").ap())
    decoder_layer(nc, *args)
    r = run_bass_kernel_spmd(nc, [arrays], core_ids=[0])
    return r.results[0]["out_x"]
```

```python
import math
from contextlib import ExitStack

import numpy as np

import concourse.bass as bass
from concourse import mybir

F32 = mybir.dt.float32
F32R = mybir.dt.float32r
BF16 = mybir.dt.bfloat16
U32 = mybir.dt.uint32
ALU = mybir.AluOpType
ACT = mybir.ActivationFunctionType
X = mybir.AxisListType.X

P = 128
NEG = -1.0e30


SELF = [("stats1", 1, 1.2), ("norm1", 1, 0.6), ("turn1", 1, 1.6), ("values", 1, 0.3), ("qk", 6, 0.8),
        ("self_max", 4, 0.9), ("self_split", 1, 1.0), ("self_shift", 1, 2.0), ("self_score", 8, 0.5),
        ("self_pv", 2, 1.5), ("self_norm", 1, 1.5), ("self_turn", 1, 1.2), ("self_out", 1, 1.2),
        ("stats2", 1, 1.2), ("norm2", 1, 0.6), ("turn2", 1, 1.6), ("query", 1, 2.0),
        ("cross_max", 8, 0.55), ("cross_split", 1, 0.8), ("cross_shift", 1, 1.3),
        ("cross_score", 7, 0.75), ("cross_pv", 7, 0.75), ("cross_out", 1, 1.6), ("stats3", 1, 1.2),
        ("norm3", 1, 0.6), ("turn3", 1, 1.2), ("gate", 1, 0.5)]
CONTEXT = [("ctx_split", 1, 1.5), ("ctx_turn", 4, 0.8), ("ctx_copy", 1, 1.5)]
START = [0.0, 8.0, 52.0, 60.0]
CONTEXT_START = [20.0, 28.0, 72.0, 80.0]
EARLY_SETUP = 1.1
LATE_SETUP = 4.0


def schedule(B):
    steps = [(LATE_SETUP, 0, ("late_setup", 0, 0)), (EARLY_SETUP, 0, ("early_setup", 0, 0))]
    ends = {}
    for b in range(B):
        t = START[b]
        for name, count, pace in SELF:
            if name == "qk" and b >= 2:
                t = max(t, ends["self_score", b - 2] + 0.1)
            if name == "query" and b >= 2:
                t = max(t, ends["cross_pv", b - 2] + 0.1)
            if name == "cross_max":
                t = max(t, ctx_end(b, ends) + 0.1)
            first = t
            for i in range(count):
                at = first + i * pace
                if name == "cross_pv":
                    at = ends["cross_score0", b] + (i + 2.5) * pace
                if name == "self_pv":
                    at = ends["self_score0", b] + (4 * i + 5.5) * 0.5
                steps.append((at, b, (name, b, i)))
            t = at + pace
            if name in ("self_score", "cross_score"):
                ends[name + "0", b] = first
            ends[name, b] = at
            if name == "cross_score":
                t = first
    for b in range(B):
        t = ctx_begin(b, ends)
        for name, count, pace in CONTEXT:
            for i in range(count):
                steps.append((t, b, (name, b, i)))
                t += pace
    return [step for _, _, step in sorted(steps, key=lambda s: (s[0], s[1]))]


def ctx_begin(b, ends):
    return CONTEXT_START[b] if b < 2 else max(CONTEXT_START[b], ends["cross_pv", b - 2] + 0.1)


def ctx_end(b, ends):
    return ctx_begin(b, ends) + sum(count * pace for _, count, pace in CONTEXT)


def decoder_layer(nc, x, ctx_in, w_qkv, w_out, head_scales, Wq, bq, Wk, bk, Wv, bv, gate_w,
                  gate_b, up_w, up_b, down_w, down_b, sw_up, sb_up, sw_down, sb_down, dirs_outer,
                  out):
    B, T, C = x.shape
    H = head_scales.shape[0]
    D = C // H
    NK, KD = ctx_in.shape[1:]
    E, _, I = up_w.shape
    TT = T // P
    NT = B * TT
    PAIRS = H // 2
    KF = NK // P
    KR = NK - KF * P
    KT = KF + 1
    NKE = KF * P + KR + KR % 2
    IT = I // P
    HALF = B * T // 2
    SCALE = 1.0 / math.sqrt(D)
    CH = [0, 402, 802, 1202, NKE]
    assert C == P and T == 2 * P and D == 16 and KD == 64 and HALF == 512

    SCHED = schedule(B)

    def turns(uses):
        at, first = 0, {}
        for step in SCHED:
            first[step] = at
            at += uses.get(step[0], 0)
        return first, at

    W0, W_ALL = turns({"ctx_turn": 1, "qk": 1, "self_max": 2, "self_norm": 1, "self_out": 1,
                       "cross_max": 1, "cross_out": 1, "gate": 1, "late_setup": 1})
    T0, T_ALL = turns({"turn1": 1, "values": 1, "self_shift": 1, "self_turn": 1, "turn2": 1,
                       "query": 1, "cross_shift": 1, "turn3": 1, "late_setup": 1})
    S0, S_ALL = turns({"self_score": 1, "cross_score": 1})
    L0, L_ALL = turns({"stats1": 1, "stats2": 1, "stats3": 1})
    LOW, LOW_ALL = turns({"turn1": 1, "turn2": 1, "turn3": 1})
    TURNED = {}
    for kind in "123":
        for b in range(B):
            TURNED[L0["stats" + kind, b, 0]] = T0["turn" + kind, b, 0]
    KP = (KT + 1) // 2
    NW, NS = 3, 2
    NP, NC = 6, 3
    NG, NH = 6, 12

    with ExitStack() as st:
        def sb(name, shape, dt=F32):
            return st.enter_context(nc.sbuf_tensor(name, shape, dt))

        def sem(name):
            return st.enter_context(nc.semaphore(name))

        work = [st.enter_context(nc.psum_tensor(f"work{i}", [P, 512], F32)) for i in range(NW)]
        score = [st.enter_context(nc.psum_tensor(f"score{i}", [P, 512], F32)) for i in range(NS)]
        turn = st.enter_context(nc.psum_tensor("turn", [P, 512], F32))
        self_sum = st.enter_context(nc.psum_tensor("self_sum", [P, 512], F32))
        cross_sum = st.enter_context(nc.psum_tensor("cross_sum", [P, 512], F32))

        up_banks = work + [self_sum]
        NU = len(up_banks)
        wide_banks = [turn, cross_sum]

        ident = sb("ident", [P, P])
        identb = sb("identb", [P, P], BF16)
        ones = sb("ones", [P, P])
        causal_q = sb("causal_q", [P, P], BF16)
        causal_k = sb("causal_k", [P, P], BF16)
        aux_rows = sb("aux_rows", [P, 2, 1])
        low_q = sb("low_q", [P, 1])
        low_k = sb("low_k", [P, 1])
        low_c = sb("low_c", [P, 1])
        minus_half = sb("minus_half", [P, 2])
        iota_e = sb("iota_e", [P, 16])
        pick_f = sb("pick_f", [P, E + 1, 1])
        pick = sb("pick", [P, E + 1, P], F32R)

        x_in = sb("x_in", [P, NT, C])
        x1 = sb("x1", [P, NT, C])
        x2 = sb("x2", [P, NT, C])
        wqkv = sb("wqkv", [P, 3 * C])
        wout = sb("wout", [P, C])
        hs = sb("hs", [P, 1])
        dirs = sb("dirs", [P, P])
        geo = sb("geo", [P, P])
        geo_d = sb("geo_d", [P, P])
        wkT = sb("wkT", [P, P])
        wqk_h = sb("wqk_h", [P, PAIRS + H, P], F32R)
        wqk_l = sb("wqk_l", [P, PAIRS + H, P], F32R)
        wq_x = sb("wq_x", [P, P])
        bq_x = sb("bq_x", [P, 1])
        wk_x = sb("wk_x", [KD, P])
        bk_x = sb("bk_x", [P, 1])
        wqT_x = sb("wqT_x", [P, P])
        wka = sb("wka", [P, 2 * P])
        w2 = sb("w2", [P, 2 * P])
        w2_h = sb("w2_h", [P, 2 * P], F32R)
        w2_l = sb("w2_l", [P, 2 * P], F32R)
        b2 = sb("b2", [P, 2])
        wva = sb("wva", [KD + 1, P + 2])
        gate = sb("gate", [P, E])
        gate_bias = sb("gate_bias", [P, E])
        bias_f = sb("bias_f", [P, P])
        bias_h = sb("bias_h", [P, P], F32R)
        bias_l = sb("bias_l", [P, P], F32R)
        up_bias = sb("up_bias", [P, E + 1, IT])

        bn = sb("bn", [P, TT, 6])
        mean_var = sb("mean_var", [P, TT, 2])
        var_eps = sb("var_eps", [P, TT])
        rstd = sb("rstd", [P, TT])
        xn = sb("xn", [P, 2, TT, C])
        xT = sb("xT", [P, 2, T])
        xT_h = sb("xT_h", [P, 2, T], F32R)
        xT_l = sb("xT_l", [P, 2, T], F32R)
        all_h = sb("all_h", [P, 2, 512], F32R)
        qS = sb("qS", [P, 2, PAIRS, T], F32R)
        kS = sb("kS", [P, 2, H, T], F32R)
        v = sb("v", [P, 2, TT, H, 32])
        nmax = sb("nmax", [P, TT, H])
        nmax_h = sb("nmax_h", [P, TT, H], F32R)
        shift = sb("shift", [P, TT, PAIRS, 32])
        probs = sb("probs", [P, NP, 3 * P])
        wqk = probs[:, 0:4, :].rearrange("p n (c k) -> p (n c) k", k=P)
        oT = sb("oT", [P, 512])
        rden = sb("rden", [P, TT, H, 1])
        o = sb("o", [P, TT, H, D])
        onT = sb("onT", [P, T])

        c_nat = sb("c_nat", [P, B, KT, KD + 1])
        c_hl = sb("c_hl", [P, KT, P], F32R)
        cA = sb("cA", [P, 2, NKE], F32R)
        cB = sb("cB", [P, 2, NKE], F32R)
        x2T = sb("x2T", [P, T])
        x2T_h = sb("x2T_h", [P, T], F32R)
        x2T_l = sb("x2T_l", [P, T], F32R)
        qA = sb("qA", [P, 2, T], F32R)
        qB = sb("qB", [P, 2, T], F32R)
        qB_f = sb("qB_f", [P, T])
        qB_h = sb("qB_h", [P, T], F32R)
        cprobs = sb("cprobs", [P, NC, 2 * T])
        cmax = sb("cmax", [P, TT, 4])
        cnmax = sb("cnmax", [P, TT])
        cnmax_h = sb("cnmax_h", [P, TT], F32R)
        cshift = sb("cshift", [P, TT, P])
        cshiftT = sb("cshiftT", [P, T])
        coT = sb("coT", [KD + 1, T])
        crden = sb("crden", [P, TT, 1])

        x3T = sb("x3T", [P, 2, T])
        x3T_h = sb("x3T_h", [P, B * T], F32R)
        x3T_l = sb("x3T_l", [P, B * T], F32R)
        z = sb("z", [P, NT, E])
        sig = sb("sig", [P, NT, E])
        top = sb("top", [P, NT, 8])
        top_i = sb("top_i", [P, NT, 8], U32)
        top_f = sb("top_f", [P, NT, 8])
        den = sb("den", [P, NT, 1])
        share = sb("share", [P, NT, 2])
        hit = sb("hit", [P, 2, NT, E])
        wgt = sb("wgt", [P, NT, 16])
        wgt_h = sb("wgt_h", [P, NT, 16], F32R)
        wgt_hl = sb("wgt_hl", [P, NT, P])
        wgtT = sb("wgtT", [P, B * T], F32R)
        up_raw = sb("up_raw", [P, 2, I])
        up_h = sb("up_h", [P, 2, IT, P], F32R)
        up_l = sb("up_l", [P, 2, IT, P], F32R)
        down_raw = sb("down_raw", [P, 2, I])
        down_h = sb("down_h", [P, 2, IT, C], F32R)
        down_l = sb("down_l", [P, 2, IT, C], F32R)
        peak = sb("peak", [P, NT])
        free = c_nat[:].rearrange("p b j d -> p (b j d)")
        wide = free[:, 0:2 * B * T].rearrange("p (e t) -> p e t", e=2)
        acc = free[:, 2 * B * T:3 * B * T].rearrange("p (s t) -> p s t", s=2)
        part = x1[:].rearrange("p (s i) c -> p s (i c)", s=2)
        y = x_in

        def slots(t):
            flat = t[:].rearrange("p a b t -> p (a b t)") if len(t.shape) == 4 \
                else t[:].rearrange("p a t -> p (a t)")
            return [flat[:, i * HALF:(i + 1) * HALF] for i in range(flat.shape[1] // HALF)]

        hid_h = (slots(kS) + slots(qS))[0:NH]
        hid_l = (slots(cA) + slots(cB))[0:NH]
        flat = probs[:].rearrange("p n k -> p (n k)")
        hid = [cprobs[:, i, :] for i in range(NC)]
        hid += [flat[:, i * HALF:(i + 1) * HALF] for i in range(NG - NC)]

        x_loaded = [sem(f"x_loaded{b}") for b in range(B)]
        c_loaded = [sem(f"c_loaded{b}") for b in range(B)]
        up_loaded = [sem(f"up_loaded{i}") for i in range(2)]
        down_loaded = [sem(f"down_loaded{i}") for i in range(2)]
        attn_loaded, cross_loaded, ffn_loaded = sem("attn_loaded"), sem("cross_loaded"), sem("ffn_loaded")
        pool_chain, dve_chain = sem("pool_chain"), sem("dve_chain")
        consts_ready = sem("consts_ready")
        weights_turned = sem("weights_turned")
        weights_taken = sem("weights_taken")
        weights_ready = sem("weights_ready")
        var_ready, rstd_ready, xn_ready = sem("var_ready"), sem("rstd_ready"), sem("xn_ready")
        low_ready = sem("low_ready")
        work_filled, work_freed = sem("work_filled"), sem("work_freed")
        turn_filled, turn_freed = sem("turn_filled"), sem("turn_freed")
        all_h_ready = sem("all_h_ready")
        shift_ready = sem("shift_ready")
        score_filled, score_freed = sem("score_filled"), sem("score_freed")
        probs_used, cprobs_used = sem("probs_used"), sem("cprobs_used")
        self_sum_freed, cross_sum_freed = sem("self_sum_freed"), sem("cross_sum_freed")
        c_split, cB_ready = sem("c_split"), sem("cB_ready")
        qB_ready, cshift_ready, qB_shifted = sem("qB_ready"), sem("cshift_ready"), sem("qB_shifted")
        ez_ready, mix_ready = sem("ez_ready"), sem("mix_ready")
        mix_turned, mixT_ready = sem("mix_turned"), sem("mixT_ready")
        w_high, w_low = sem("w_high"), sem("w_low")
        up_filled = sem("up_filled")
        hid_ready, hid_h_ready = sem("hid_ready"), sem("hid_h_ready")
        hid_l_dve, hid_l_pool = sem("hid_l_dve"), sem("hid_l_pool")
        hid_used = sem("hid_used")
        bias_filled = sem("bias_filled")
        wide_filled, wide_ready = sem("wide_filled"), sem("wide_ready")
        down_taken = sem("down_taken")
        acc_ready, acc_turned = sem("acc_ready"), sem("acc_turned")
        y_ready, y_stored = sem("y_ready"), sem("y_stored")

        PARTS = [("up", 0), ("up", 1), ("down", 0)]
        for e in range(2, E + 1):
            PARTS += [("up", e), ("down", e - 1)]
        PARTS.append(("down", E))
        PART = {p: n for n, p in enumerate(PARTS)}

        def f(ap):
            return ap.bitcast(F32)

        def weight_parts(kind, e):
            if kind == "up":
                return (up_raw[:, e % 2, :].rearrange("p (c i) -> p i c", i=IT),
                        up_h[:, e % 2, :, :], up_l[:, e % 2, :, :])
            return (down_raw[:, e % 2, :].rearrange("p (i c) -> p i c", i=IT),
                    down_h[:, e % 2, :, :], down_l[:, e % 2, :, :])

        block = st.enter_context(nc.Block())

        @block.sync
        def _(sp):
            def rows(t):
                return t.rearrange("(i p) c -> p i c", p=P)

            def load_x(b):
                sp.dma_start(x_in[:, TT * b:TT * b + TT, :], rows(x[b])).then_inc(x_loaded[b], 16)

            def load_ctx(b):
                sp.dma_start(c_nat[:, b, 0:KF, 0:KD],
                             ctx_in[b, 0:KF * P, :].rearrange("(p j) d -> p j d", j=KF)
                             ).then_inc(c_loaded[b], 16)
                sp.dma_start(c_nat[0:KR, b, KF, 0:KD], ctx_in[b, KF * P:NK, :]
                             ).then_inc(c_loaded[b], 16)
                sp.dma_start(c_nat[KR:KR + 1, b, KF, 0:KD], ctx_in[b, NK - 1:NK, :]
                             ).then_inc(c_loaded[b], 16)

            load_x(0)
            sp.dma_start(wqkv[:], w_qkv).then_inc(attn_loaded, 16)
            for h in range(H):
                sp.dma_start(hs[D * h:D * h + D, :], head_scales[h:h + 1].rearrange("(a b) -> a b", b=1)
                             .to_broadcast([D, 1])).then_inc(attn_loaded, 16)
            sp.dma_start(dirs[:], dirs_outer).then_inc(attn_loaded, 16)
            load_ctx(0)
            load_x(1)
            sp.dma_start(wout[:], w_out).then_inc(cross_loaded, 16)
            sp.dma_start(wq_x[:], Wq).then_inc(cross_loaded, 16)
            sp.dma_start(wk_x[:], Wk).then_inc(cross_loaded, 16)
            sp.dma_start(bq_x[:], bq.rearrange("(a b) -> a b", b=1)).then_inc(cross_loaded, 16)
            sp.dma_start(bk_x[:], bk.rearrange("(a b) -> a b", b=1)).then_inc(cross_loaded, 16)
            sp.wait_ge(consts_ready, 3)
            sp.dma_start(wva[0:KD, 0:P], Wv).then_inc(cross_loaded, 16)
            sp.dma_start(wva[KD:KD + 1, 0:P], bv.rearrange("(a b) -> a b", a=1)
                         ).then_inc(cross_loaded, 16)
            for b in range(1, B):
                load_ctx(b)
                if b + 1 < B:
                    load_x(b + 1)
            sp.dma_start(gate[:], gate_w).then_inc(ffn_loaded, 16)
            sp.dma_start(gate_bias[:], gate_b.rearrange("(a e) -> a e", a=1).to_broadcast([P, E])
                         ).then_inc(ffn_loaded, 16)
            for r in (0, 16):
                sp.dma_start(bias_f[r:r + E, :], down_b).then_inc(ffn_loaded, 16)
                sp.dma_start(bias_f[r + E:r + E + 1, :], sb_down.rearrange("(a c) -> a c", a=1)
                             ).then_inc(ffn_loaded, 16)
            sp.dma_start(up_bias[:, 0:E, :], up_b.rearrange("e (p i) -> p e i", i=IT)
                         ).then_inc(ffn_loaded, 16)
            sp.dma_start(up_bias[:, E, :], sb_up.rearrange("(p i) -> p i", i=IT)
                         ).then_inc(ffn_loaded, 16)
            for kind, e in PARTS:
                if e >= 2:
                    sp.wait_ge(w_low, PART[kind, e - 2] + 1)
                if kind == "up":
                    sp.dma_start(up_raw[:, e % 2, :], up_w[e] if e < E else sw_up
                                 ).then_inc(up_loaded[e % 2], 16)
                else:
                    sp.dma_start(down_raw[:, e % 2, :], (down_w[e] if e < E else sw_down)
                                 .rearrange("(p i) c -> p (i c)", i=IT)
                                 ).then_inc(down_loaded[e % 2], 16)
            for b in range(B):
                sp.wait_ge(y_ready, b + 1)
                sp.dma_start(rows(out[b]), y[:, TT * b:TT * b + TT, :]).then_inc(y_stored, 16)
            sp.wait_ge(y_stored, 16 * B)

        @block.gpsimd
        def _(pool):
            done = [0]

            def link(ins):
                done[0] += 1
                ins.then_inc(pool_chain, 1)
                pool.wait_ge(pool_chain, done[0])

            g = nc.gpsimd

            def select(t, op, fill, base, pattern, by):
                return g.affine_select(out=t, in_=t, compare_op=op, fill=fill, base=base,
                                       pattern=pattern, channel_multiplier=by)

            link(g.memset(ident[:], 0.0))
            select(ident[:], ALU.not_equal, 1.0, 0, [[-1, P]], 1).then_inc(consts_ready, 1)
            pool.wait_ge(consts_ready, 1)
            link(g.memset(minus_half[:], -0.5))
            link(g.memset(wqk, 0.0))
            link(g.memset(low_q[:], 0.0))
            link(g.memset(low_k[:], 0.0))
            link(g.memset(low_q[32:64, :], -1.0))
            g.memset(low_k[64:96, :], -1.0).then_inc(consts_ready, 1)
            pool.wait_ge(consts_ready, 2)
            norms = [0]

            def rstd_next():
                norms[0] += 1
                pool.wait_ge(var_ready, norms[0])
                g.tensor_tensor(rstd[:], var_eps[:], minus_half[:, 0:TT], ALU.pow
                                ).then_inc(rstd_ready, 1)
                pool.wait_ge(rstd_ready, norms[0])

            rstd_next()
            link(g.tensor_copy(identb[:], ident[:]))
            link(g.memset(causal_q[:], 0.0))
            link(g.memset(causal_k[:], 0.0))
            link(select(causal_q[:], ALU.is_ge, NEG, 0, [[-1, P]], 1))
            link(select(causal_k[:], ALU.is_ge, NEG, 0, [[1, P]], -1))
            link(g.memset(v[:, :, :, :, D + 1:32], 0.0))
            link(g.memset(v[:, :, :, :, D:D + 1], 1.0))
            link(g.memset(shift[:], 0.0))
            link(g.memset(aux_rows[:], 0.0))
            for a in range(2):
                for r in range(2):
                    link(select(aux_rows[96:128, a, :], ALU.not_equal, 1.0, -(2 * a + r),
                                [[0, 1]], 1))
            link(g.memset(wka[:], 0.0))
            link(g.memset(wva[:], 0.0))
            link(g.memset(wva[KD:KD + 1, P:P + 1], 1.0))
            link(g.memset(bias_f[:], 0.0))
            link(g.memset(ones[:], 1.0))
            link(g.memset(c_nat[:, :, :, KD:KD + 1], 1.0))
            link(g.memset(low_c[:], 0.0))
            link(g.memset(low_c[0:64, :], -1.0))
            link(select(low_c[64:96, :], ALU.not_equal, -1.0, -1, [[0, 1]], 1))
            g.memset(cshift[:], 0.0).then_inc(consts_ready, 1)
            pool.wait_ge(consts_ready, 3)
            rstd_next()
            link(g.memset(wgt_hl[:], 0.0))
            link(g.memset(wgt[:], 0.0))
            link(g.memset(wgt[:, :, E:E + 1], 0.1))
            link(g.iota(iota_e[:], pattern=[[1, 16]], base=0, channel_multiplier=0,
                        allow_small_or_imprecise_dtypes=True))
            link(g.memset(pick_f[:], 0.0))
            link(select(pick_f[:], ALU.not_equal, 1.0, 0, [[-1, E + 1], [0, 1]], 1))
            select(pick_f[:], ALU.not_equal, 1.0, -16, [[-1, E + 1], [0, 1]], 1
                   ).then_inc(consts_ready, 1)
            pool.wait_ge(consts_ready, 4)
            while norms[0] < L_ALL:
                rstd_next()

            def weights_low(kind, e):
                n = PART[kind, e]
                pool.wait_ge(w_high, n + 1)
                raw, high, low = weight_parts(kind, e)
                g.tensor_tensor(low, raw, f(high), ALU.subtract).then_inc(w_low, 1)

            def hidden_low(e, i):
                n = (e * IT + i) * 2 + 1
                pool.wait_ge(hid_h_ready, n + 1)
                g.tensor_tensor(hid_l[n % NH], hid[n % NG], f(hid_h[n % NH]), ALU.subtract
                                ).then_inc(hid_l_pool, 1)

            for kind, e in PARTS[0:3]:
                weights_low(kind, e)
            for i in range(IT):
                hidden_low(0, i)
            for e in range(E + 1):
                if e + 2 <= E:
                    weights_low("up", e + 2)
                if e + 1 <= E:
                    weights_low("down", e + 1)
                    for i in range(IT):
                        hidden_low(e + 1, i)

        @block.tensor
        def _(pe):
            mm = nc.tensor.matmul
            tr = nc.tensor.transpose

            def work_bank(step):
                u = W0[step]
                if u >= NW:
                    pe.wait_ge(work_freed, u - NW + 1)
                return work[u % NW]

            def turn_bank(step):
                if T0[step]:
                    pe.wait_ge(turn_freed, T0[step])
                return turn

            def score_bank(step):
                u = S0[step]
                if u >= NS:
                    pe.wait_ge(score_freed, u - NS + 1)
                return score[u % NS]

            def three(dst, w_h, w_l, x_h, x_l):
                mm(dst, w_h, x_h, start=True, stop=False)
                mm(dst, w_l, x_h, start=False, stop=False)
                return mm(dst, w_h, x_l, start=False, stop=True)

            def early_setup(step, b, i):
                pe.wait_ge(consts_ready, 1)
                pe.wait_ge(attn_loaded, 16 * (H + 2))
                tr(self_sum[:, 0:P], wqkv[:, C:2 * C], ident[:]).then_inc(weights_turned, 1)
                pe.wait_ge(weights_taken, 1)
                mm(cross_sum[:, 0:P], wkT[:], geo[:], start=True, stop=True
                   ).then_inc(weights_turned, 1)

            def late_setup(step, b, i):
                bank = turn_bank(step)
                pe.wait_ge(cross_loaded, 16 * 7)
                tr(bank[:, 0:P], wq_x[:], ident[:])
                tr(bank[:, P:P + KD], wk_x[:], ident[0:KD, 0:KD]).then_inc(turn_filled, 1)
                pe.wait_ge(turn_freed, T0[step] + 1)
                bank = work_bank(step)
                mm(bank[:, 0:2 * P], wqT_x[:], wka[:], start=True, stop=True)
                mm(bank[:, 2 * P:2 * P + 1], wka[:, 0:P], bq_x[:], start=True, stop=True)
                mm(bank[:, 2 * P + 1:2 * P + 2], wka[:, P:2 * P], bq_x[:], start=True, stop=True
                   ).then_inc(work_filled, 1)

            def ctx_turn(step, b, i):
                bank = work_bank(step)
                pe.wait_ge(c_split, b + 1)
                for j in range(4 * i, min(4 * i + 4, KT)):
                    m = P if j < KF else NKE - KF * P
                    at = (j - 4 * i) * P
                    last = tr(bank[:, at:at + m], f(c_hl[0:m, j, :]), ident[0:m, 0:m])
                last.then_inc(work_filled, 1)

            def turn_norm(step, b, i):
                n = L0["stats" + step[0][-1], b, 0]
                bank = turn_bank(step)
                pe.wait_ge(xn_ready, n + 1)
                for t in range(TT):
                    last = tr(bank[:, t * P:(t + 1) * P], xn[:, n % 2, t, :], ident[:])
                last.then_inc(turn_filled, 1)

            def values(step, b, i):
                bank = turn_bank(step)
                pe.wait_ge(turn_freed, T0["turn1", b, 0] + 1)
                for t in range(TT):
                    last = mm(bank[:, t * P:(t + 1) * P], xT[:, b % 2, t * P:(t + 1) * P],
                              wqkv[:, 2 * C:3 * C], start=True, stop=True)
                last.then_inc(turn_filled, 1)

            def qk(step, b, i):
                bank = work_bank(step)
                if i == 0:
                    pe.wait_ge(low_ready, LOW["turn1", b, 0] + 1)
                    if b == 0:
                        pe.wait_ge(weights_ready, 1)
                for s in range(2):
                    c = 2 * i + s
                    last = three(bank[:, s * T:(s + 1) * T], wqk_h[:, c, :], wqk_l[:, c, :],
                                 xT_h[:, b % 2, :], xT_l[:, b % 2, :])
                last.then_inc(work_filled, 1)

            def self_max(step, b, r):
                if r == 0:
                    pe.wait_ge(work_freed, W0["qk", b, 5] + 1)
                    if b == 0:
                        pe.wait_ge(consts_ready, 3)
                for k, t in enumerate((1, 0)):
                    n = (t + 1) * P
                    u = W0[step] + k
                    if u >= NW:
                        pe.wait_ge(work_freed, u - NW + 1)
                    dst = work[u % NW][:, 0:2 * n].rearrange("p (a k) -> p a k", a=2)
                    mm(dst, qS[0:96, b % 2, r, t * P:(t + 1) * P],
                       kS[0:96, b % 2, 2 * r:2 * r + 2, 0:n], start=True, stop=False)
                    mm(dst[:, :, t * P:n], identb[:],
                       causal_q[:].unsqueeze(1).to_broadcast([P, 2, P]),
                       start=False, stop=True).then_inc(work_filled, 1)

            def self_shift(step, b, i):
                bank = turn_bank(step)
                pe.wait_ge(shift_ready, b + 1)
                for t in range(TT):
                    last = tr(bank[:, t * P:(t + 1) * P],
                              shift[:, t, :, :].rearrange("p r c -> p (r c)"), ident[:])
                last.then_inc(turn_filled, 1)

            def self_score(step, b, h):
                bank = score_bank(step)
                if h == 0:
                    pe.wait_ge(turn_freed, T0["self_shift", b, 0] + 1)
                    if b == 0:
                        pe.wait_ge(weights_ready, 2)
                mm(bank[:, P:3 * P], kS[:, b % 2, h, P:2 * P], qS[:, b % 2, h // 2, :],
                   start=True, stop=False)
                mm(bank[:, 2 * P:3 * P], identb[:], causal_k[:], start=False, stop=True)
                mm(bank[:, 0:2 * P], kS[:, b % 2, h, 0:P], qS[:, b % 2, h // 2, :],
                   start=True, stop=False)
                mm(bank[:, 0:P], identb[:], causal_k[:], start=False, stop=True
                   ).then_inc(score_filled, 1)

            def self_pv(step, b, g):
                if g == 0 and b:
                    pe.wait_ge(self_sum_freed, b)
                pe.wait_ge(score_freed, S0["self_score", b, 4 * g + 3] + 1)
                for k in range(2):
                    for j in range(4):
                        s = (b * H + 4 * g + j) % NP
                        src = probs[:, s, 0:2 * P] if k == 0 else probs[:, s, 2 * P:3 * P]
                        last = mm(self_sum[32 * j:32 * j + 32, g * T + k * P:(g + 1) * T],
                                  v[:, b % 2, k, 4 * g + j, :], src, start=(k == 0), stop=(k == 1))
                        if k == 1:
                            last.then_inc(probs_used, 1)

            def self_norm(step, b, i):
                bank = work_bank(step)
                pe.wait_ge(self_sum_freed, b + 1)
                for t in range(TT):
                    for g in range(2):
                        last = tr(bank[:, (2 * t + g) * P:(2 * t + g + 1) * P],
                                  oT[:, g * T + t * P:g * T + (t + 1) * P], ident[:])
                last.then_inc(work_filled, 1)

            def self_turn(step, b, i):
                bank = turn_bank(step)
                pe.wait_ge(work_freed, W0["self_norm", b, 0] + 1)
                for t in range(TT):
                    last = tr(bank[:, t * P:(t + 1) * P],
                              o[:, t, :, :].rearrange("p h d -> p (h d)"), ident[:])
                last.then_inc(turn_filled, 1)

            def self_out(step, b, i):
                bank = work_bank(step)
                pe.wait_ge(turn_freed, T0["self_turn", b, 0] + 1)
                if b == 0:
                    pe.wait_ge(cross_loaded, 16 * 7)
                for t in range(TT):
                    last = mm(bank[:, t * P:(t + 1) * P], onT[:, t * P:(t + 1) * P], wout[:],
                              start=True, stop=True)
                last.then_inc(work_filled, 1)

            def query(step, b, i):
                bank = turn_bank(step)
                pe.wait_ge(low_ready, LOW["turn2", b, 0] + 1)
                for s in range(2):
                    cols = slice(s * P, (s + 1) * P)
                    last = three(bank[:, s * T:(s + 1) * T], w2_h[:, cols], w2_l[:, cols],
                                 x2T_h[:], x2T_l[:])
                last.then_inc(turn_filled, 1)

            def cross_max(step, b, n):
                t, i = divmod(n, 4)
                if n == 0:
                    pe.wait_ge(cB_ready, b + 1)
                    pe.wait_ge(qB_ready, b + 1)
                bank = work_bank(step)
                rows = slice(t * P, (t + 1) * P)
                a, m = CH[i], CH[i + 1] - CH[i]
                mm(bank[:, 0:m], qA[:, b % 2, rows], cA[:, b % 2, a:a + m], start=True, stop=False)
                mm(bank[:, 0:m], qB[:, b % 2, rows], cB[:, b % 2, a:a + m], start=False, stop=True
                   ).then_inc(work_filled, 1)

            def cross_shift(step, b, i):
                bank = turn_bank(step)
                pe.wait_ge(cshift_ready, b + 1)
                for t in range(TT):
                    last = tr(bank[:, t * P:(t + 1) * P], cshift[:, t, :], ident[:])
                last.then_inc(turn_filled, 1)

            def cross_score(step, b, i):
                bank = score_bank(step)
                if i == 0:
                    pe.wait_ge(qB_shifted, b + 1)
                for j in range(2 * i, min(2 * i + 2, KT)):
                    m = P if j < KF else KR
                    dst = bank[0:m, (j % 2) * T:(j % 2 + 1) * T]
                    mm(dst, cA[:, b % 2, j * P:j * P + m], qA[:, b % 2, :], start=True, stop=False)
                    last = mm(dst, cB[:, b % 2, j * P:j * P + m], qB[:, b % 2, :],
                              start=False, stop=True)
                last.then_inc(score_filled, 1)

            def cross_pv(step, b, i):
                if i == 0 and b:
                    pe.wait_ge(cross_sum_freed, b)
                pe.wait_ge(score_freed, S0["cross_score", b, i] + 1)
                for j in range(2 * i, min(2 * i + 2, KT)):
                    m = P if j < KF else KR
                    last = mm(cross_sum[0:KD + 1, 0:T], c_nat[0:m, b, j, :],
                              cprobs[0:m, (b * KP + i) % NC, (j % 2) * T:(j % 2 + 1) * T],
                              start=(j == 0), stop=(j == KT - 1))
                last.then_inc(cprobs_used, 1)

            def cross_out(step, b, i):
                bank = work_bank(step)
                pe.wait_ge(cross_sum_freed, b + 1)
                for t in range(TT):
                    last = mm(bank[:, t * 256:t * 256 + P + 2], coT[:, t * P:(t + 1) * P], wva[:],
                              start=True, stop=True)
                last.then_inc(work_filled, 1)

            def gate_(step, b, i):
                bank = work_bank(step)
                pe.wait_ge(turn_freed, T0["turn3", b, 0] + 1)
                if b == 0:
                    pe.wait_ge(ffn_loaded, 16 * 8)
                for t in range(TT):
                    last = mm(bank[:, t * E:(t + 1) * E], x3T[:, b % 2, t * P:(t + 1) * P], gate[:],
                              start=True, stop=True)
                last.then_inc(work_filled, 1)

            steps = {"early_setup": early_setup, "late_setup": late_setup, "ctx_turn": ctx_turn,
                     "turn1": turn_norm, "turn2": turn_norm, "turn3": turn_norm, "values": values,
                     "qk": qk, "self_max": self_max, "self_shift": self_shift,
                     "self_score": self_score, "self_pv": self_pv, "self_norm": self_norm,
                     "self_turn": self_turn, "self_out": self_out, "query": query,
                     "cross_max": cross_max, "cross_shift": cross_shift,
                     "cross_score": cross_score, "cross_pv": cross_pv, "cross_out": cross_out,
                     "gate": gate_}
            for step in SCHED:
                if step[0] in steps:
                    steps[step[0]](step, *step[1:])

            pe.wait_ge(turn_freed, T_ALL)
            pe.wait_ge(work_freed, W_ALL)
            pe.wait_ge(score_freed, S_ALL)
            pe.wait_ge(low_ready, LOW_ALL)
            half = [slice(s * HALF, (s + 1) * HALF) for s in range(2)]

            def up(e, i):
                if i == 0:
                    pe.wait_ge(w_low, PART["up", e] + 1)
                banks = []
                for s in range(2):
                    n = (e * IT + i) * 2 + s
                    if n >= NU:
                        pe.wait_ge(hid_ready, n - NU + 1)
                    banks.append(up_banks[n % NU])
                w_h, w_l = up_h[:, e % 2, i, :], up_l[:, e % 2, i, :]
                for s in range(2):
                    mm(banks[s][:], w_h, x3T_h[:, half[s]], start=True, stop=False)
                for s in range(2):
                    mm(banks[s][:], w_h, x3T_l[:, half[s]], start=False, stop=False)
                for s in range(2):
                    mm(banks[s][:], w_l, x3T_h[:, half[s]], start=False, stop=True
                       ).then_inc(up_filled, 1)

            def widen(e):
                for s in range(2):
                    if e:
                        pe.wait_ge(wide_ready, 2 * e + s - 1)
                    mm(wide_banks[s][:], pick[:, e, :], wgtT[:, half[s]], start=True, stop=True
                       ).then_inc(wide_filled, 1)

            def down(e, i):
                if i == 0:
                    pe.wait_ge(w_low, PART["down", e] + 1)
                    if e:
                        pe.wait_ge(down_taken, 2 * e)
                w_h, w_l = down_h[:, e % 2, i, :], down_l[:, e % 2, i, :]
                n = (e * IT + i) * 2
                for s in range(2):
                    pe.wait_ge(hid_h_ready, n + s + 1)
                    mm(score[s][:], w_h, hid_h[(n + s) % NH], start=(i == 0), stop=False)
                for s in range(2):
                    mm(score[s][:], w_l, hid_h[(n + s) % NH], start=False, stop=False)
                for s in range(2):
                    pe.wait_ge(hid_l_pool if s else hid_l_dve, n // 2 + 1)
                    mm(score[s][:], w_h, hid_l[(n + s) % NH], start=False, stop=(i == IT - 1)
                       ).then_inc(hid_used, 1)

            def turn_mixture():
                pe.wait_ge(mix_ready, 1)
                for s in range(2):
                    for t in range(4):
                        last = tr(wide_banks[s][:, t * P:(t + 1) * P], wgt_hl[:, 4 * s + t, :],
                                  ident[:])
                    last.then_inc(mix_turned, 1)
                pe.wait_ge(mixT_ready, 2)

            for i in range(IT):
                up(0, i)
            turn_mixture()
            for e in range(E + 1):
                for i in range(IT):
                    if e < E:
                        up(e + 1, i)
                    down(e, i)
                    if i == 0:
                        widen(e)
            pe.wait_ge(hid_ready, 2 * IT * (E + 1))
            for s in range(2):
                mm(up_banks[s][:], bias_h[:], wgtT[:, half[s]], start=True, stop=False)
                mm(up_banks[s][:], bias_l[:], wgtT[:, half[s]], start=False, stop=True
                   ).then_inc(bias_filled, 1)
            for s in range(2):
                pe.wait_ge(acc_ready, s + 1)
                for t in range(4):
                    last = tr(score[s][:, t * P:(t + 1) * P], acc[:, s, t * P:(t + 1) * P], ident[:])
                last.then_inc(acc_turned, 1)

        @block.scalar
        def _(act):
            a = nc.scalar

            def copy(dst, src):
                return a.activation(dst, src, ACT.Copy)

            def late_setup(step, b, i):
                act.wait_ge(turn_filled, T0[step] + 1)
                act.wait_ge(consts_ready, 3)
                copy(wqT_x[:], turn[:, 0:P])
                for k in range(3):
                    copy(wka[:, k * KD:(k + 1) * KD], turn[:, P:P + KD])
                copy(wka[:, 3 * KD:3 * KD + 2], bk_x[:].to_broadcast([P, 2])).then_inc(turn_freed, 1)

            def ctx_copy(step, b, i):
                act.wait_ge(work_freed, W0["ctx_turn", b, 3] + 1)
                if b >= 2:
                    act.wait_ge(score_filled, S0["cross_score", b - 2, KP - 1] + 1)
                copy(cB[0:KD, b % 2, :], f(cA[0:KD, b % 2, :])).then_inc(cB_ready, 1)

            def norm_out(step, dst, dst_h):
                act.wait_ge(turn_filled, T0[step] + 1)
                copy(dst, turn[:, 0:T])
                copy(dst_h, turn[:, 0:T]).then_inc(turn_freed, 1)

            def turn1(step, b, i):
                if b >= 2:
                    act.wait_ge(work_filled, W0["qk", b - 2, 5] + 1)
                norm_out(step, xT[:, b % 2, :], xT_h[:, b % 2, :])

            def values(step, b, i):
                act.wait_ge(turn_filled, T0[step] + 1)
                if b >= 2:
                    act.wait_ge(probs_used, H * (b - 1))
                if b == 0:
                    act.wait_ge(consts_ready, 3)
                copy(v[:, b % 2, :, :, 0:D],
                     turn[:, 0:T].rearrange("p (t h d) -> p t h d", t=TT, d=D)
                     ).then_inc(turn_freed, 1)

            def qk(step, b, i):
                n = b * 6 + i
                act.wait_ge(work_filled, W0[step] + 1)
                if n >= 2:
                    act.wait_ge(work_freed, W0["qk", (n - 2) // 6, (n - 2) % 6] + 1)
                copy(all_h[0:96, n % 2, :], work[W0[step] % NW][0:96, :]).then_inc(all_h_ready, 1)

            def self_shift(step, b, i):
                act.wait_ge(turn_filled, T0[step] + 1)
                for r in range(PAIRS):
                    last = copy(qS[96:128, b % 2, r, :], turn[32 * r:32 * r + 32, 0:T])
                last.then_inc(turn_freed, 1)

            def self_score(step, b, h):
                u = S0[step]
                n = b * H + h
                act.wait_ge(score_filled, u + 1)
                if n >= NP:
                    act.wait_ge(probs_used, n - NP + 1)
                a.activation(probs[:, n % NP, :], score[u % NS][:, 0:3 * P], ACT.Exp
                             ).then_inc(score_freed, 1)

            def self_pv(step, b, g):
                if g == 1:
                    act.wait_ge(probs_used, H * (b + 1))
                    if b:
                        act.wait_ge(work_filled, W0["self_norm", b - 1, 0] + 1)
                    copy(oT[:], self_sum[:]).then_inc(self_sum_freed, 1)

            def self_turn(step, b, i):
                act.wait_ge(turn_filled, T0[step] + 1)
                if b:
                    act.wait_ge(work_filled, W0["self_out", b - 1, 0] + 1)
                copy(onT[:], turn[:, 0:T]).then_inc(turn_freed, 1)

            def turn2(step, b, i):
                if b:
                    act.wait_ge(turn_filled, T0["query", b - 1, 0] + 1)
                norm_out(step, x2T[:], x2T_h[:])

            def query(step, b, i):
                act.wait_ge(turn_filled, T0[step] + 1)
                if b == 0:
                    act.wait_ge(weights_ready, 2)
                if b:
                    act.wait_ge(qB_ready, b)
                if b >= 2:
                    act.wait_ge(score_filled, S0["cross_score", b - 2, KP - 1] + 1)
                a.activation(qA[:, b % 2, :], turn[:, 0:T], ACT.Identity, bias=b2[:, 0:1])
                a.activation(qB_f[:], turn[:, T:2 * T], ACT.Identity, bias=b2[:, 1:2])
                a.activation(qB_h[:], turn[:, T:2 * T], ACT.Identity, bias=b2[:, 1:2]
                             ).then_inc(turn_freed, 1)

            def cross_shift(step, b, i):
                act.wait_ge(turn_filled, T0[step] + 1)
                if b:
                    act.wait_ge(qB_shifted, b)
                copy(cshiftT[64:128, :], turn[64:128, 0:T]).then_inc(turn_freed, 1)

            def cross_score(step, b, i):
                u = S0[step]
                n = b * KP + i
                act.wait_ge(score_filled, u + 1)
                if n >= NC:
                    act.wait_ge(cprobs_used, n - NC + 1)
                m, w = (P, 2 * T) if 2 * i + 2 <= KF else (KR, T)
                a.activation(cprobs[0:m, n % NC, 0:w], score[u % NS][0:m, 0:w], ACT.Exp
                             ).then_inc(score_freed, 1)

            def cross_pv(step, b, i):
                if i == KP - 1:
                    act.wait_ge(cprobs_used, KP * (b + 1))
                    if b:
                        act.wait_ge(work_filled, W0["cross_out", b - 1, 0] + 1)
                    copy(coT[:], cross_sum[0:KD + 1, 0:T]).then_inc(cross_sum_freed, 1)

            def turn3(step, b, i):
                if b >= 2:
                    act.wait_ge(work_filled, W0["gate", b - 2, 0] + 1)
                    act.wait_ge(low_ready, LOW["turn3", b - 2, 0] + 1)
                norm_out(step, x3T[:, b % 2, :], x3T_h[:, b * T:(b + 1) * T])

            steps = {"late_setup": late_setup, "ctx_copy": ctx_copy, "turn1": turn1,
                     "turn2": turn2, "turn3": turn3, "values": values, "qk": qk,
                     "self_shift": self_shift, "self_score": self_score, "self_pv": self_pv,
                     "self_turn": self_turn, "query": query, "cross_shift": cross_shift,
                     "cross_score": cross_score, "cross_pv": cross_pv}
            for step in SCHED:
                if step[0] in steps:
                    steps[step[0]](step, *step[1:])
            act.wait_ge(work_freed, W0["gate", B - 1, 0] + 1)
            a.activation(z[:], z[:], ACT.Exp, scale=-1.0).then_inc(ez_ready, 1)

            def hidden(e, i):
                for s in range(2):
                    n = (e * IT + i) * 2 + s
                    act.wait_ge(up_filled, n + 1)
                    if n >= NG:
                        act.wait_ge(hid_l_pool if s else hid_l_dve, (n - NG) // 2 + 1)
                    a.activation(hid[n % NG], up_banks[n % NU][:], ACT.Gelu,
                                 bias=up_bias[:, e, i:i + 1]).then_inc(hid_ready, 1)

            def widen(e):
                for s in range(2):
                    act.wait_ge(wide_filled, 2 * e + s + 1)
                    if e >= 2:
                        act.wait_ge(down_taken, 2 * (e - 1))
                    copy(wide[:, e % 2, s * HALF:(s + 1) * HALF], wide_banks[s][:]
                         ).then_inc(wide_ready, 1)

            for i in range(IT):
                hidden(0, i)
            for s in range(2):
                act.wait_ge(mix_turned, s + 1)
                copy(wgtT[:, s * HALF:(s + 1) * HALF], wide_banks[s][:]).then_inc(mixT_ready, 1)
            for e in range(E + 1):
                for i in range(IT):
                    if e < E:
                        hidden(e + 1, i)
                    if i == 0:
                        widen(e)

        @block.vector
        def _(dve):
            d = nc.vector
            done = [0]

            def link(ins):
                done[0] += 1
                ins.then_inc(dve_chain, 1)
                dve.wait_ge(dve_chain, done[0])

            def early_setup(step, b, i):
                dve.wait_ge(attn_loaded, 16 * (H + 2))
                dve.wait_ge(consts_ready, 2)
                link(d.tensor_scalar(geo_d[:], dirs[:], hs[:, 0:1], None, ALU.mult))
                d.scalar_tensor_tensor(out=geo[:], in0=ident[:], scalar=SCALE, in1=geo_d[:],
                                       op0=ALU.mult, op1=ALU.add)
                dve.wait_ge(weights_turned, 1)
                d.tensor_copy(wkT[:], self_sum[:, 0:P]).then_inc(weights_taken, 1)
                for k in range(3):
                    last = d.tensor_copy(wqk[:, 0:PAIRS, 32 * k:32 * k + 32],
                                         wqkv[:, 0:C].rearrange("p (r c) -> p r c", c=32))
                link(last)
                link(d.tensor_copy(wqk_h[:, 0:PAIRS, :], wqk[:, 0:PAIRS, :]))
                d.tensor_tensor(wqk_l[:, 0:PAIRS, :], wqk[:, 0:PAIRS, :], f(wqk_h[:, 0:PAIRS, :]),
                                ALU.subtract)
                dve.wait_ge(weights_turned, 2)
                for k in range(3):
                    for s in range(2):
                        last = d.tensor_copy(
                            wqk[:, PAIRS:, :].rearrange("p (r a) c -> p r a c", a=2)
                            [:, :, s, 32 * k + D * s:32 * k + D * s + D],
                            cross_sum[:, 0:P].rearrange("p (r a c) -> p r a c", a=2, c=D)
                            [:, :, s, :])
                link(last)
                link(d.tensor_copy(wqk_h[:, PAIRS:, :], wqk[:, PAIRS:, :]))
                d.tensor_tensor(wqk_l[:, PAIRS:, :], wqk[:, PAIRS:, :], f(wqk_h[:, PAIRS:, :]),
                                ALU.subtract).then_inc(weights_ready, 1)

            def late_setup(step, b, i):
                dve.wait_ge(consts_ready, 3)
                for s in range(2):
                    for k in range(2):
                        d.tensor_copy(
                            kS[96:128, s, :, :].rearrange("p (r a) t -> p r a t", a=2)[:, :, k, :],
                            aux_rows[96:128, k:k + 1, :].to_broadcast([32, PAIRS, T]))
                    d.tensor_copy(cB[64:128, s, :], ones[64:128, 0:1].to_broadcast([64, NKE]))
                u = W0[step]
                dve.wait_ge(work_filled, u + 1)
                d.tensor_copy(b2[:], work[u % NW][:, 2 * P:2 * P + 2])
                d.tensor_copy(w2[:], work[u % NW][:, 0:2 * P]).then_inc(work_freed, 1)
                dve.wait_ge(work_freed, u + 1)
                link(d.tensor_copy(w2_h[:], w2[:]))
                d.tensor_tensor(w2_l[:], w2[:], f(w2_h[:]), ALU.subtract).then_inc(weights_ready, 1)

            def stats(step, b, i):
                src = norm_src(step[0], b)
                if step[0] == "stats1":
                    dve.wait_ge(x_loaded[b], 16)
                for t in range(TT):
                    last = d.bn_stats(bn[:, t, :], src[:, t, :])
                link(last)
                for t in range(TT):
                    last = d.bn_aggr(mean_var[:, t, :], bn[:, t, :])
                link(last)
                d.tensor_scalar(var_eps[:], mean_var[:, :, 1], 1e-5, None, ALU.add
                                ).then_inc(var_ready, 1)

            def norm(step, b, i):
                kind = step[0][-1]
                src = norm_src("stats" + kind, b)
                n = L0["stats" + kind, b, 0]
                if n >= 2:
                    dve.wait_ge(turn_filled, TURNED[n - 2] + 1)
                dve.wait_ge(rstd_ready, n + 1)
                for t in range(TT):
                    last = d.tensor_scalar(xn[:, n % 2, t, :], src[:, t, :], mean_var[:, t, 0:1],
                                           rstd[:, t:t + 1], ALU.subtract, ALU.mult)
                last.then_inc(xn_ready, 1)

            def norm_src(kind, b):
                tiles = slice(TT * b, TT * b + TT)
                return {"stats1": x_in, "stats2": x1, "stats3": x2}[kind][:, tiles, :]

            def low_part(step, b, i):
                high, full, low = {
                    "turn1": (xT_h[:, b % 2, :], xT[:, b % 2, :], xT_l[:, b % 2, :]),
                    "turn2": (x2T_h[:], x2T[:], x2T_l[:]),
                    "turn3": (x3T_h[:, b * T:(b + 1) * T], x3T[:, b % 2, :],
                              x3T_l[:, b * T:(b + 1) * T])}[step[0]]
                dve.wait_ge(turn_freed, T0[step] + 1)
                d.tensor_tensor(low, full, f(high), ALU.subtract).then_inc(low_ready, 1)

            def ctx_split(step, b, i):
                dve.wait_ge(c_loaded[b], 48)
                if b:
                    dve.wait_ge(work_filled, W0["ctx_turn", b - 1, 3] + 1)
                parts = ((P, slice(0, KF)), (KR + 1, slice(KF, KT)))
                for n, j in parts:
                    last = d.tensor_copy(c_hl[0:n, j, 0:KD], c_nat[0:n, b, j, 0:KD])
                link(last)
                for n, j in parts:
                    last = d.tensor_tensor(c_hl[0:n, j, KD:2 * KD], c_nat[0:n, b, j, 0:KD],
                                           f(c_hl[0:n, j, 0:KD]), ALU.subtract)
                last.then_inc(c_split, 1)

            def ctx_turn(step, b, i):
                if b >= 2 and i == 0:
                    dve.wait_ge(score_filled, S0["cross_score", b - 2, KP - 1] + 1)
                a, n = 512 * i, min(512, NKE - 512 * i)
                dve.wait_ge(work_filled, W0[step] + 1)
                d.tensor_copy(cA[:, b % 2, a:a + n], work[W0[step] % NW][:, 0:n]
                              ).then_inc(work_freed, 1)

            def qk(step, b, i):
                n = b * 6 + i
                if b >= 2 and i == 0:
                    dve.wait_ge(score_filled, S0["self_score", b - 2, H - 1] + 1)
                dve.wait_ge(all_h_ready, n + 1)
                if i < PAIRS // 2:
                    dst, low = qS[0:96, b % 2, 2 * i:2 * i + 2, :], low_q
                else:
                    k = 2 * i - PAIRS
                    dst, low = kS[0:96, b % 2, k:k + 2, :], low_k
                d.scalar_tensor_tensor(
                    out=dst, in0=f(all_h[0:96, n % 2, :]).rearrange("p (a t) -> p a t", a=2),
                    scalar=low[0:96, 0:1],
                    in1=work[W0[step] % NW][0:96, :].rearrange("p (a t) -> p a t", a=2),
                    op0=ALU.mult, op1=ALU.add).then_inc(work_freed, 1)

            def self_max(step, b, r):
                for k, t in enumerate((1, 0)):
                    u = W0[step] + k
                    n = (t + 1) * P
                    dve.wait_ge(work_filled, u + 1)
                    d.tensor_reduce(nmax[:, t, 2 * r:2 * r + 2],
                                    work[u % NW][:, 0:2 * n].rearrange("p (a k) -> p a k", a=2),
                                    X, ALU.max, negate=True).then_inc(work_freed, 1)

            def self_split(step, b, i):
                dve.wait_ge(work_freed, W0["self_max", b, PAIRS - 1] + 2)
                if b:
                    dve.wait_ge(turn_filled, T0["self_shift", b - 1, 0] + 1)
                link(d.tensor_copy(nmax_h[:], nmax[:]))
                at = shift[:, :, :, 0:4].rearrange("p t r (a l) -> p (t r) a l", l=2)
                hi = f(nmax_h[:]).rearrange("p t (r a) -> p (t r) a", a=2)
                d.tensor_copy(at[:, :, :, 0], hi)
                d.tensor_tensor(at[:, :, :, 1], nmax[:].rearrange("p t (r a) -> p (t r) a", a=2),
                                hi, ALU.subtract).then_inc(shift_ready, 1)

            def self_norm(step, b, i):
                u = W0[step]
                dve.wait_ge(work_filled, u + 1)
                if b:
                    dve.wait_ge(turn_filled, T0["self_turn", b - 1, 0] + 1)
                src = work[u % NW][:].rearrange("p (t h c) -> p t h c", t=TT, c=32)
                link(d.reciprocal(rden[:], src[:, :, :, D:D + 1]))
                d.tensor_tensor(o[:], src[:, :, :, 0:D], rden[:].to_broadcast([P, TT, H, D]),
                                ALU.mult).then_inc(work_freed, 1)

            def self_out(step, b, i):
                u = W0[step]
                tiles = slice(TT * b, TT * b + TT)
                dve.wait_ge(work_filled, u + 1)
                d.tensor_tensor(x1[:, tiles, :],
                                work[u % NW][:, 0:T].rearrange("p (t c) -> p t c", t=TT),
                                x_in[:, tiles, :], ALU.add).then_inc(work_freed, 1)
                dve.wait_ge(work_freed, u + 1)

            def query(step, b, i):
                dve.wait_ge(turn_freed, T0[step] + 1)
                d.scalar_tensor_tensor(out=qB[:, b % 2, :], in0=f(qB_h[:]), scalar=low_c[:, 0:1],
                                       in1=qB_f[:], op0=ALU.mult, op1=ALU.add
                                       ).then_inc(qB_ready, 1)

            def cross_max(step, b, n):
                t, i = divmod(n, 4)
                u = W0[step]
                dve.wait_ge(work_filled, u + 1)
                d.tensor_reduce(cmax[:, t, i:i + 1], work[u % NW][:, 0:CH[i + 1] - CH[i]],
                                X, ALU.max).then_inc(work_freed, 1)

            def cross_split(step, b, i):
                dve.wait_ge(work_freed, W0["cross_max", b, 7] + 1)
                link(d.tensor_reduce(cnmax[:], cmax[:], X, ALU.max, negate=True))
                if b:
                    dve.wait_ge(turn_filled, T0["cross_shift", b - 1, 0] + 1)
                link(d.tensor_copy(cnmax_h[:], cnmax[:]))
                d.tensor_copy(cshift[:, :, KD + 2], f(cnmax_h[:]))
                d.tensor_tensor(cshift[:, :, KD + 3], cnmax[:], f(cnmax_h[:]), ALU.subtract
                                ).then_inc(cshift_ready, 1)

            def cross_shift(step, b, i):
                dve.wait_ge(turn_freed, T0[step] + 1)
                d.tensor_tensor(qB[64:128, b % 2, :], f(qB[64:128, b % 2, :]), cshiftT[64:128, :],
                                ALU.add).then_inc(qB_shifted, 1)

            def cross_out(step, b, i):
                u = W0[step]
                dve.wait_ge(work_filled, u + 1)
                src = work[u % NW][:].rearrange("p (t c) -> p t c", t=TT)
                link(d.reciprocal(crden[:], src[:, :, P:P + 1]))
                for t in range(TT):
                    last = d.scalar_tensor_tensor(
                        out=x2[:, TT * b + t, :], in0=src[:, t, 0:P], scalar=crden[:, t, :],
                        in1=x1[:, TT * b + t, :], op0=ALU.mult, op1=ALU.add)
                last.then_inc(work_freed, 1)
                dve.wait_ge(work_freed, u + 1)

            def gate_(step, b, i):
                dve.wait_ge(work_filled, W0[step] + 1)
                d.tensor_tensor(z[:, TT * b:TT * b + TT, :],
                                work[W0[step] % NW][:, 0:TT * E].rearrange("p (t e) -> p t e", e=E),
                                gate_bias[:].unsqueeze(1).to_broadcast([P, TT, E]), ALU.add
                                ).then_inc(work_freed, 1)

            steps = {"early_setup": early_setup, "late_setup": late_setup, "ctx_split": ctx_split,
                     "ctx_turn": ctx_turn, "stats1": stats, "stats2": stats, "stats3": stats,
                     "norm1": norm, "norm2": norm, "norm3": norm, "turn1": low_part,
                     "turn2": low_part, "turn3": low_part, "qk": qk, "self_max": self_max,
                     "self_split": self_split, "self_norm": self_norm, "self_out": self_out,
                     "query": query, "cross_max": cross_max, "cross_split": cross_split,
                     "cross_shift": cross_shift, "cross_out": cross_out, "gate": gate_}
            for step in SCHED:
                if step[0] in steps:
                    steps[step[0]](step, *step[1:])

            def weights_high(kind, e):
                loaded = up_loaded if kind == "up" else down_loaded
                dve.wait_ge(loaded[e % 2], 16 * (e // 2 + 1))
                if e >= 2 and kind == "up":
                    dve.wait_ge(up_filled, 2 * IT * (e - 1))
                if e >= 2 and kind == "down":
                    dve.wait_ge(hid_used, 2 * IT * (e - 1))
                raw, high, _ = weight_parts(kind, e)
                d.tensor_copy(high, raw).then_inc(w_high, 1)

            def hidden(e, i):
                for s in range(2):
                    n = (e * IT + i) * 2 + s
                    dve.wait_ge(hid_ready, n + 1)
                    if n >= NH:
                        dve.wait_ge(hid_used, n - NH + 1)
                    d.tensor_copy(hid_h[n % NH], hid[n % NG]).then_inc(hid_h_ready, 1)
                    if s == 0:
                        dve.wait_ge(hid_h_ready, n + 1)
                        d.tensor_tensor(hid_l[n % NH], hid[n % NG], f(hid_h[n % NH]), ALU.subtract
                                        ).then_inc(hid_l_dve, 1)

            def mixture():
                dve.wait_ge(ez_ready, 1)
                link(d.tensor_scalar(sig[:], z[:], 1.0, None, ALU.add))
                link(d.reciprocal(sig[:], sig[:]))
                for t in range(NT):
                    last = d.max(top[:, t, :], sig[:, t, :])
                link(last)
                for t in range(NT):
                    last = d.max_index(top_i[:, t, :], top[:, t, :], sig[:, t, :])
                link(d.scalar_tensor_tensor(out=den[:], in0=top[:, :, 0:1], scalar=1e-6,
                                            in1=top[:, :, 1:2], op0=ALU.add, op1=ALU.add))
                link(d.reciprocal(den[:], den[:]))
                d.scalar_tensor_tensor(out=share[:], in0=top[:, :, 0:2], scalar=0.1,
                                       in1=den[:].to_broadcast([P, NT, 2]), op0=ALU.mult,
                                       op1=ALU.mult)
                link(d.tensor_copy(top_f[:], top_i[:]))
                wide_iota = iota_e[:, 0:E].unsqueeze(1).to_broadcast([P, NT, E])
                for k in range(2):
                    last = d.tensor_tensor(hit[:, k, :, :], wide_iota,
                                           top_f[:, :, k:k + 1].to_broadcast([P, NT, E]),
                                           ALU.is_equal)
                link(last)
                for k in range(2):
                    last = d.tensor_tensor(hit[:, k, :, :], hit[:, k, :, :],
                                           share[:, :, k:k + 1].to_broadcast([P, NT, E]), ALU.mult)
                link(last)
                link(d.tensor_tensor(wgt[:, :, 0:E], hit[:, 0, :, :], hit[:, 1, :, :], ALU.add))
                link(d.tensor_copy(wgt_h[:], wgt[:]))
                d.tensor_copy(wgt_hl[:, :, 0:16], f(wgt_h[:]))
                d.tensor_tensor(wgt_hl[:, :, 16:32], wgt[:], f(wgt_h[:]), ALU.subtract
                                ).then_inc(mix_ready, 1)

            dve.wait_ge(consts_ready, 4)
            for kind, e in PARTS[0:3]:
                weights_high(kind, e)
            mixture()
            dve.wait_ge(score_filled, S_ALL)
            d.tensor_copy(pick[:], pick_f[:].to_broadcast([P, E + 1, P]))
            link(d.tensor_copy(bias_h[:], bias_f[:]))
            for i in range(IT):
                hidden(0, i)
            d.tensor_tensor(bias_l[:], bias_f[:], f(bias_h[:]), ALU.subtract).then_inc(weights_ready, 1)
            for e in range(E + 1):
                if e + 2 <= E:
                    weights_high("up", e + 2)
                if e + 1 <= E:
                    weights_high("down", e + 1)
                    for i in range(IT):
                        hidden(e + 1, i)
                dve.wait_ge(hid_used, 2 * IT * (e + 1))
                dve.wait_ge(wide_ready, 2 * e + 2)
                for s in range(2):
                    dst = acc[:, s, :] if e == 0 else part[:, s, :]
                    d.tensor_tensor(dst, score[s][:], wide[:, e % 2, s * HALF:(s + 1) * HALF],
                                    ALU.mult).then_inc(down_taken, 1)
                if e:
                    for s in range(2):
                        dve.wait_ge(down_taken, 2 * e + s + 1)
                        last = d.tensor_tensor(acc[:, s, :], acc[:, s, :], part[:, s, :], ALU.add)
                    link(last)
            for s in range(2):
                dve.wait_ge(bias_filled, s + 1)
                d.tensor_tensor(acc[:, s, :], acc[:, s, :], up_banks[s][:], ALU.add
                                ).then_inc(acc_ready, 1)
            for s in range(2):
                dve.wait_ge(acc_turned, s + 1)
                tiles = slice(4 * s, 4 * s + 4)
                src = score[s][:].rearrange("p (t c) -> p t c", t=4)
                link(d.tensor_reduce(peak[:, tiles], src, X, ALU.max, apply_absolute_value=True))
                link(d.tensor_scalar(peak[:, tiles], peak[:, tiles], 1e-6, None, ALU.add))
                link(d.reciprocal(peak[:, tiles], peak[:, tiles]))
                for t in range(4):
                    last = d.scalar_tensor_tensor(
                        out=y[:, 4 * s + t, :], in0=src[:, t, :],
                        scalar=peak[:, 4 * s + t:4 * s + t + 1], in1=x2[:, 4 * s + t, :],
                        op0=ALU.mult, op1=ALU.add)
                    if t % TT == TT - 1:
                        last.then_inc(y_ready, 1)


_INS = ["x", "ctx_512", "L0_attn_w_qkv", "L0_attn_w_out", "L0_attn_head_scales", "L0_xattn_Wq",
        "L0_xattn_bq", "L0_xattn_Wk", "L0_xattn_bk", "L0_xattn_Wv", "L0_xattn_bv",
        "L0_ffn_gate_w", "L0_ffn_bias", "L0_ffn_up_w", "L0_ffn_up_b", "L0_ffn_down_w",
        "L0_ffn_down_b", "L0_ffn_sw_up", "L0_ffn_sb_up", "L0_ffn_sw_down", "L0_ffn_sb_down"]


def head_dirs_outer(heads, dim):
    m = np.zeros((heads * dim, heads * dim), np.float32)
    for h in range(heads):
        v = np.array([(h >> 2 & 1) * 2 - 1, (h >> 1 & 1) * 2 - 1, (h & 1) * 2 - 1], np.float32)
        m[h * dim:h * dim + 3, h * dim:h * dim + 3] = np.outer(v, v) / np.float32(3.0)
    return m


def kernel(**inputs):
    import concourse.bacc as bacc
    from concourse.bass_utils import run_bass_kernel_spmd

    nc = bacc.Bacc("TRN2", target_bir_lowering=False, num_devices=1)
    arrays, args = {}, []
    given = {n: np.ascontiguousarray(inputs[n]) for n in _INS}
    given["dirs_outer"] = head_dirs_outer(8, 16)
    for name, a in given.items():
        arrays[f"in_{name}"] = a
        args.append(nc.dram_tensor(f"in_{name}", a.shape, mybir.dt.from_np(a.dtype),
                                   kind="ExternalInput").ap())
    args.append(nc.dram_tensor("out_x", given["x"].shape, F32, kind="ExternalOutput").ap())
    decoder_layer(nc, *args)
    r = run_bass_kernel_spmd(nc, [arrays], core_ids=[0])
    return r.results[0]["out_x"]
```

```python
import math
from contextlib import ExitStack

import numpy as np

import concourse.bass as bass
from concourse import mybir

F32 = mybir.dt.float32
F32R = mybir.dt.float32r
BF16 = mybir.dt.bfloat16
U32 = mybir.dt.uint32
ALU = mybir.AluOpType
ACT = mybir.ActivationFunctionType
X = mybir.AxisListType.X

P = 128
NEG = -1.0e30


SELF = [
    ("stats1", 1, (5.54, 6.16, 3.24, 5.38)),
    ("norm1", 1, (7.47, 8.88, 8.31, 10.26)),
    ("turn1", 1, (2.49, 3.22, 4.25, 1.43)),
    ("values", 1, (0.15, 0.02, 0.38, 0.14)),
    ("qk", 6, (0.72, 0.84, 0.9, 0.74)),
    ("self_max", 4, (1.54, 0.95, 1.12, 0.94)),
    ("self_split", 1, (2.16, 0.45, 1.78, 0.18)),
    ("self_shift", 1, (4.58, 1.98, 1.32, 1.56)),
    ("self_score", 8, (0.63, 0.92, 0.77, 0.75)),
    ("self_pv", 2, (0.17, 0.32, 0.11, 0.21)),
    ("self_norm", 1, (0.36, 2.56, 1.12, 1.87)),
    ("self_turn", 1, (0.73, 1.05, 1.42, 0.57)),
    ("self_out", 1, (2.82, 1.97, 2.65, 2.7)),
    ("stats2", 1, (0.7, 0.5, 1.15, 1.16)),
    ("norm2", 1, (1.92, 4.09, 2.6, 1.81)),
    ("turn2", 1, (2.81, 0.66, 1.01, 2.07)),
    ("query", 1, (2.82, 3.79, 2.08, 5.41)),
    ("cross_max", 8, (0.14, 0.01, 0.54, 0.14)),
    ("cross_split", 1, (0.1, 0.29, 0.28, 2.39)),
    ("cross_shift", 1, (1.09, 2.12, 0.01, 0.21)),
    ("cross_score", 7, (1.1, 0.89, 1.4, 0.82)),
    ("cross_pv", 7, (0.86, 0.75, 0.95, 0.7)),
    ("cross_out", 1, (0.74, 3.7, 1.44, 0.45)),
    ("stats3", 1, (0.85, 6.67, 2.23, 0.35)),
    ("norm3", 1, (9.44, 0.11, 0.64, 16.54)),
    ("turn3", 1, (9.34, 0.31, 12.48, 4824.4)),
    ("gate", 1, (0.04, 0.01, 16.96, 5.59)),
]
MIX = [
    ("mix", 1, (22.82, 12.75, 0.89, 0.02)),
    ("mix_turn", 1, (0.01, 0.01, 1.65, 0.01)),
]
CONTEXT = [
    ("ctx_split", 4, (0.64, 3.23, 1.49, 0.84)),
    ("ctx_turn", 4, (1.23, 0.34, 1.45, 0.19)),
    ("ctx_copy", 1, (0.15, 0.01, 0.01, 0.08)),
]
STATS = ("stats1", "stats2", "stats3")
START = [0.49, 16.11, 27.85, 36.15]
CONTEXT_START = [25.21, 35.65, 9.79, 77.6]
FFN_START = 61.7
FFN_PACE = 0.77
STACKS_START = 0.43
STACKS_PACE = 5.27
AHEAD_PACE = 5.39
EARLY_SETUP = 10.27
LATE_TURN = 3.71
LATE_SETUP = 10.4
CROSS_LAG = 4.25
SELF_LAG = 3.31


def schedule(B):
    steps = [(EARLY_SETUP, 0, ("early_setup", 0, 0)), (LATE_TURN, 0, ("late_turn", 0, 0)),
             (LATE_SETUP, 0, ("late_setup", 0, 0))]
    ends = {}
    for b in range(B):
        t = START[b]
        for name, count, paces in SELF + (MIX if b == 1 else []):
            pace = paces[b]
            if name == "qk" and b >= 2:
                t = max(t, ends["self_score", b - 2] + 0.1)
            if name == "query" and b >= 2:
                t = max(t, ends["cross_pv", b - 2] + 0.1)
            if name == "cross_max":
                t = max(t, ctx_end(b, ends) + 0.1)
            first = t
            for i in range(count):
                at = first + i * pace
                if name == "cross_pv":
                    at = ends["cross_score0", b] + (i + CROSS_LAG) * pace
                if name == "self_pv":
                    at = ends["self_score0", b] + 4 * i * score_pace + SELF_LAG
                steps.append((at, b, (name, b, i)))
            t = at + pace
            if name == "self_score":
                score_pace = pace
            if name in ("self_score", "cross_score"):
                ends[name + "0", b] = first
            ends[name, b] = at
            if name == "cross_score":
                t = first
    for b in range(B):
        t = ctx_begin(b, ends)
        for name, count, paces in CONTEXT:
            for i in range(count):
                steps.append((t, b, (name, b, i)))
                t += paces[b]
    for i in range(3):
        steps.append((FFN_START + FFN_PACE * i, 0, ("ffn_weights", 0, i)))
    for i in range(6):
        steps.append((STACKS_START + STACKS_PACE * i, 0, ("stacks", 0, i)))
    for i in range(4):
        steps.append((ends["cross_pv", B - 1] + 0.1 + AHEAD_PACE * i, B, ("ahead", B - 1, i)))
    order = [step for _, _, step in sorted(steps, key=lambda s: (s[0], s[1]))]
    at = {step: n for n, step in enumerate(order)}
    for name in {step[0] for step in order}:
        mine = [step for step in order if step[0] == name]
        assert mine == sorted(mine), name
    for b in range(B - 1):
        assert at["self_split", b, 0] < at["self_max", b + 1, 0]
        assert at["cross_split", b, 0] < at["cross_max", b + 1, 0]
    stats = [step for step in order if step[0] in STATS]
    norms = [at["norm" + name[-1], b, 0] for name, b, _ in stats]
    assert norms == sorted(norms)
    for n, norm in enumerate(norms[:-2]):
        assert norm < at[stats[n + 2]]
    for last in (("cross_pv", B - 1, 6), ("self_pv", B - 1, 1), ("turn3", 1, 0),
                 ("ffn_weights", 0, 2)):
        assert at[last] < at["ahead", B - 1, 0]
    return order


def ctx_begin(b, ends):
    return CONTEXT_START[b] if b < 2 else max(CONTEXT_START[b], ends["cross_pv", b - 2] + 0.1)


def ctx_end(b, ends):
    return ctx_begin(b, ends) + sum(count * paces[b] for _, count, paces in CONTEXT)


def decoder_layer(nc, x, ctx_in, w_qkv, w_out, head_scales, Wq, bq, Wk, bk, Wv, bv, gate_w,
                  gate_b, up_w, up_b, down_w, down_b, sw_up, sb_up, sw_down, sb_down, dirs_outer,
                  out):
    B, T, C = x.shape
    H = head_scales.shape[0]
    D = C // H
    NK, KD = ctx_in.shape[1:]
    E, _, I = up_w.shape
    TT = T // P
    NT = B * TT
    PAIRS = H // 2
    KF = NK // P
    KR = NK - KF * P
    KT = KF + 1
    NKE = KF * P + KR + KR % 2
    IT = I // P
    HALF = B * T // 2
    SCALE = 1.0 / math.sqrt(D)
    CH = [0, 402, 802, 1202, NKE]
    assert C == P and T == 2 * P and D == 16 and KD == 64 and HALF == 512

    SCHED = schedule(B)

    def turns(uses):
        at, first = 0, {}
        for step in SCHED:
            first[step] = at
            at += uses.get(step[0], 0)
        return first, at

    W0, W_ALL = turns({"ctx_turn": 1, "qk": 1, "self_max": 2, "self_norm": 1, "self_out": 1,
                       "cross_max": 1, "cross_out": 1, "gate": 1, "late_setup": 1})
    T0, T_ALL = turns({"turn1": 1, "values": 1, "self_shift": 1, "self_turn": 1, "turn2": 1,
                       "query": 1, "cross_shift": 1, "turn3": 1, "mix_turn": 1, "late_turn": 1})
    S0, S_ALL = turns({"self_score": 1, "cross_score": 1})
    L0, L_ALL = turns({"stats1": 1, "stats2": 1, "stats3": 1})
    LOW, LOW_ALL = turns({"turn1": 1, "turn2": 1, "turn3": 1})
    TURNED = {}
    for kind in "123":
        for b in range(B):
            TURNED[L0["stats" + kind, b, 0]] = T0["turn" + kind, b, 0]
    KP = (KT + 1) // 2
    NW, NS = 3, 2
    NP, NC = 6, 3
    NG, NH = 6, 12

    with ExitStack() as st:
        def sb(name, shape, dt=F32):
            return st.enter_context(nc.sbuf_tensor(name, shape, dt))

        def sem(name):
            return st.enter_context(nc.semaphore(name))

        work = [st.enter_context(nc.psum_tensor(f"work{i}", [P, 512], F32)) for i in range(NW)]
        score = [st.enter_context(nc.psum_tensor(f"score{i}", [P, 512], F32)) for i in range(NS)]
        turn = st.enter_context(nc.psum_tensor("turn", [P, 512], F32))
        self_sum = st.enter_context(nc.psum_tensor("self_sum", [P, 512], F32))
        cross_sum = st.enter_context(nc.psum_tensor("cross_sum", [P, 512], F32))

        up_banks = work + [self_sum]
        ahead_banks = [self_sum] + score + [cross_sum]
        NU = len(up_banks)
        wide_banks = [turn, cross_sum]

        ident = sb("ident", [P, P])
        identb = sb("identb", [P, P], BF16)
        ones = sb("ones", [P, P])
        causal_q = sb("causal_q", [P, P], BF16)
        causal_k = sb("causal_k", [P, P], BF16)
        aux_rows = sb("aux_rows", [P, 2, 1])
        low_q = sb("low_q", [P, 1])
        low_k = sb("low_k", [P, 1])
        low_c = sb("low_c", [P, 1])
        minus_half = sb("minus_half", [P, 2])
        iota_e = sb("iota_e", [P, 16])
        pick_f = sb("pick_f", [P, E + 1, 1])
        pick = sb("pick", [P, E + 1, P], F32R)

        x_in = sb("x_in", [P, NT, C])
        x1 = sb("x1", [P, NT, C])
        x2 = sb("x2", [P, NT, C])
        wqkv = sb("wqkv", [P, 3 * C])
        wout = sb("wout", [P, C])
        hs = sb("hs", [P, H])
        dirs = sb("dirs", [P, P])
        geo = sb("geo", [P, P])
        geo_d = sb("geo_d", [P, P])
        wkT = sb("wkT", [P, P])
        wqk_h = sb("wqk_h", [P, PAIRS + H, P], F32R)
        wqk_l = sb("wqk_l", [P, PAIRS + H, P], F32R)
        wq_x = sb("wq_x", [P, P])
        bq_x = sb("bq_x", [P, 1])
        wk_x = sb("wk_x", [KD, P])
        bk_x = sb("bk_x", [P, 1])
        wqT_x = sb("wqT_x", [P, P])
        wka = sb("wka", [P, 2 * P])
        w2 = sb("w2", [P, 2 * P])
        w2_h = sb("w2_h", [P, 2 * P], F32R)
        w2_l = sb("w2_l", [P, 2 * P], F32R)
        b2 = sb("b2", [P, 2])
        wva = sb("wva", [KD + 1, P + 2])
        gate = sb("gate", [P, E])
        gate_bias = sb("gate_bias", [P, E])
        bias_f = sb("bias_f", [P, P])
        bias_h = sb("bias_h", [P, P], F32R)
        bias_l = sb("bias_l", [P, P], F32R)
        up_bias = sb("up_bias", [P, E + 1, IT])

        bn = sb("bn", [P, TT, 6])
        mean_var = sb("mean_var", [P, 2, TT, 2])
        var_eps = sb("var_eps", [P, 2, TT])
        rstd = sb("rstd", [P, 2, TT])
        xn = sb("xn", [P, 2, TT, C])
        xT = sb("xT", [P, 2, T])
        xT_h = sb("xT_h", [P, 2, T], F32R)
        xT_l = sb("xT_l", [P, 2, T], F32R)
        all_h = sb("all_h", [P, 2, 512], F32R)
        qS = sb("qS", [P, 2, PAIRS, T], F32R)
        kS = sb("kS", [P, 2, H, T], F32R)
        v = sb("v", [P, 2, TT, H, 32])
        nmax = sb("nmax", [P, TT, H])
        nmax_h = sb("nmax_h", [P, TT, H], F32R)
        shift = sb("shift", [P, TT, PAIRS, 32])
        probs = sb("probs", [P, NP, 3 * P])
        oT = sb("oT", [P, 512])
        rden = sb("rden", [P, TT, H, 1])
        o = sb("o", [P, TT, H, D])
        onT = sb("onT", [P, T])

        c_nat = sb("c_nat", [P, B, KT, KD + 1])
        c_hl = sb("c_hl", [P, KT, P], F32R)
        cA = sb("cA", [P, 2, NKE], F32R)
        cB = sb("cB", [P, 2, NKE], F32R)
        x2T = sb("x2T", [P, T])
        x2T_h = sb("x2T_h", [P, T], F32R)
        x2T_l = sb("x2T_l", [P, T], F32R)
        qA = sb("qA", [P, 2, T], F32R)
        qB = sb("qB", [P, 2, T], F32R)
        qB_f = sb("qB_f", [P, T])
        qB_h = sb("qB_h", [P, T], F32R)
        cprobs = sb("cprobs", [P, NC, 2 * T])
        cmax = sb("cmax", [P, TT, 4])
        cnmax = sb("cnmax", [P, TT])
        cnmax_h = sb("cnmax_h", [P, TT], F32R)
        cshift = sb("cshift", [P, TT, P])
        cshiftT = sb("cshiftT", [P, T])
        coT = sb("coT", [KD + 1, T])
        crden = sb("crden", [P, TT, 1])

        x3T = sb("x3T", [P, 2, T])
        x3T_h = sb("x3T_h", [P, B * T], F32R)
        x3T_l = sb("x3T_l", [P, B * T], F32R)
        z = sb("z", [P, NT, E])
        sig = sb("sig", [P, NT, E])
        top = sb("top", [P, NT, 8])
        top_i = sb("top_i", [P, NT, 8], U32)
        top_f = sb("top_f", [P, NT, 8])
        den = sb("den", [P, NT, 1])
        share = sb("share", [P, NT, 2])
        hit = sb("hit", [P, 2, NT, E])
        wgt = sb("wgt", [P, NT, 16])
        wgt_h = sb("wgt_h", [P, NT, 16], F32R)
        wgt_hl = sb("wgt_hl", [P, NT, P])
        wgtT = sb("wgtT", [P, B * T], F32R)
        up_raw = sb("up_raw", [P, 2, I])
        up_h = sb("up_h", [P, 2, IT, P], F32R)
        up_l = sb("up_l", [P, 2, IT, P], F32R)
        down_raw = sb("down_raw", [P, 2, I])
        down_h = sb("down_h", [P, 2, IT, C], F32R)
        down_l = sb("down_l", [P, 2, IT, C], F32R)
        peak = sb("peak", [P, NT])
        free = c_nat[:].rearrange("p b j d -> p (b j d)")
        wide = free[:, 0:2 * B * T].rearrange("p (e t) -> p e t", e=2)
        acc = free[:, 2 * B * T:3 * B * T].rearrange("p (s t) -> p s t", s=2)
        part = x1[:].rearrange("p (s i) c -> p s (i c)", s=2)
        y = x_in

        def slots(t):
            flat = t[:].rearrange("p a b t -> p (a b t)") if len(t.shape) == 4 \
                else t[:].rearrange("p a t -> p (a t)")
            return [flat[:, i * HALF:(i + 1) * HALF] for i in range(flat.shape[1] // HALF)]

        hid_h = (slots(kS) + slots(qS))[0:NH]
        hid_l = (slots(cA) + slots(cB))[0:NH]
        flat = probs[:].rearrange("p n k -> p (n k)")
        hid = [flat[:, i * HALF:(i + 1) * HALF] for i in range(NG - NC)]
        hid += [cprobs[:, i, :] for i in range(NC)]

        x_loaded = [sem(f"x_loaded{b}") for b in range(B)]
        c_loaded = [sem(f"c_loaded{b}") for b in range(B)]
        up_loaded = [sem(f"up_loaded{i}") for i in range(2)]
        down_loaded = [sem(f"down_loaded{i}") for i in range(2)]
        attn_loaded, cross_loaded = sem("attn_loaded"), sem("cross_loaded")
        wout_loaded, wva_loaded = sem("wout_loaded"), sem("wva_loaded")
        ffn_loaded = sem("ffn_loaded")
        pool_chain, dve_chain = sem("pool_chain"), sem("dve_chain")
        consts_ready = sem("consts_ready")
        weights_turned = sem("weights_turned")
        weights_taken = sem("weights_taken")
        weights_ready = sem("weights_ready")
        stacks_ready = sem("stacks_ready")
        var_ready, rstd_ready, xn_ready = sem("var_ready"), sem("rstd_ready"), sem("xn_ready")
        low_ready = sem("low_ready")
        work_filled, work_freed = sem("work_filled"), sem("work_freed")
        turn_filled, turn_freed = sem("turn_filled"), sem("turn_freed")
        all_h_ready = sem("all_h_ready")
        shift_ready = sem("shift_ready")
        score_filled, score_freed = sem("score_filled"), sem("score_freed")
        probs_used, cprobs_used = sem("probs_used"), sem("cprobs_used")
        self_sum_freed, cross_sum_freed = sem("self_sum_freed"), sem("cross_sum_freed")
        c_split, cB_ready = sem("c_split"), sem("cB_ready")
        qB_ready, cshift_ready, qB_shifted = sem("qB_ready"), sem("cshift_ready"), sem("qB_shifted")
        ez_ready, mix_ready = sem("ez_ready"), sem("mix_ready")
        mix_turned, mixT_ready = sem("mix_turned"), sem("mixT_ready")
        w_high, w_low = sem("w_high"), sem("w_low")
        up_filled = sem("up_filled")
        hid_ready, hid_h_ready = sem("hid_ready"), sem("hid_h_ready")
        hid_l_dve, hid_l_pool = sem("hid_l_dve"), sem("hid_l_pool")
        hid_used = sem("hid_used")
        bias_filled = sem("bias_filled")
        wide_filled, wide_ready = sem("wide_filled"), sem("wide_ready")
        down_taken = sem("down_taken")
        acc_ready, acc_turned = sem("acc_ready"), sem("acc_turned")
        y_ready, y_stored = sem("y_ready"), sem("y_stored")

        PARTS = [("up", 0), ("up", 1), ("down", 0)]
        for e in range(2, E + 1):
            PARTS += [("up", e), ("down", e - 1)]
        PARTS.append(("down", E))
        PART = {p: n for n, p in enumerate(PARTS)}

        def tile(e, i, s):
            return s * IT + i if e == 0 else (e * IT + i) * 2 + s

        def used(n):
            return 2 * (n % IT) + n // IT + 1 if n < 2 * IT else n + 1

        def up_bank(n):
            return ahead_banks[n] if n < IT else up_banks[(n - IT) % NU]

        def f(ap):
            return ap.bitcast(F32)

        def weight_parts(kind, e):
            if kind == "up":
                return (up_raw[:, e % 2, :].rearrange("p (c i) -> p i c", i=IT),
                        up_h[:, e % 2, :, :], up_l[:, e % 2, :, :])
            return (down_raw[:, e % 2, :].rearrange("p (i c) -> p i c", i=IT),
                    down_h[:, e % 2, :, :], down_l[:, e % 2, :, :])

        block = st.enter_context(nc.Block())

        @block.sync
        def _(sp):
            def rows(t):
                return t.rearrange("(i p) c -> p i c", p=P)

            def load_x(b):
                sp.dma_start(x_in[:, TT * b:TT * b + TT, :], rows(x[b])).then_inc(x_loaded[b], 16)

            def load_ctx(b):
                sp.dma_start(c_nat[:, b, 0:KF, 0:KD],
                             ctx_in[b, 0:KF * P, :].rearrange("(p j) d -> p j d", j=KF)
                             ).then_inc(c_loaded[b], 16)
                sp.dma_start(c_nat[0:KR, b, KF, 0:KD], ctx_in[b, KF * P:NK, :]
                             ).then_inc(c_loaded[b], 16)
                sp.dma_start(c_nat[KR:KR + 1, b, KF, 0:KD], ctx_in[b, NK - 1:NK, :]
                             ).then_inc(c_loaded[b], 16)

            load_x(0)
            sp.dma_start(wqkv[:], w_qkv).then_inc(attn_loaded, 16)
            sp.dma_start(hs[:], head_scales.rearrange("(a h) -> a h", a=1).to_broadcast([P, H])
                         ).then_inc(attn_loaded, 16)
            sp.dma_start(dirs[:], dirs_outer).then_inc(attn_loaded, 16)
            sp.dma_start(wq_x[:], Wq).then_inc(cross_loaded, 16)
            sp.dma_start(wk_x[:], Wk).then_inc(cross_loaded, 16)
            sp.dma_start(bq_x[:], bq.rearrange("(a b) -> a b", b=1)).then_inc(cross_loaded, 16)
            sp.dma_start(bk_x[:], bk.rearrange("(a b) -> a b", b=1)).then_inc(cross_loaded, 16)
            load_x(1)
            load_ctx(0)
            sp.dma_start(wout[:], w_out).then_inc(wout_loaded, 16)
            for b in range(1, B):
                load_ctx(b)
                if b + 1 < B:
                    load_x(b + 1)
            sp.wait_ge(consts_ready, 4)
            sp.dma_start(wva[0:KD, 0:P], Wv).then_inc(wva_loaded, 16)
            sp.dma_start(wva[KD:KD + 1, 0:P], bv.rearrange("(a b) -> a b", a=1)
                         ).then_inc(wva_loaded, 16)
            sp.dma_start(gate[:], gate_w).then_inc(ffn_loaded, 16)
            sp.dma_start(gate_bias[:], gate_b.rearrange("(a e) -> a e", a=1).to_broadcast([P, E])
                         ).then_inc(ffn_loaded, 16)
            for r in (0, 16):
                sp.dma_start(bias_f[r:r + E, :], down_b).then_inc(ffn_loaded, 16)
                sp.dma_start(bias_f[r + E:r + E + 1, :], sb_down.rearrange("(a c) -> a c", a=1)
                             ).then_inc(ffn_loaded, 16)
            sp.dma_start(up_bias[:, 0:E, :], up_b.rearrange("e (p i) -> p e i", i=IT)
                         ).then_inc(ffn_loaded, 16)
            sp.dma_start(up_bias[:, E, :], sb_up.rearrange("(p i) -> p i", i=IT)
                         ).then_inc(ffn_loaded, 16)
            for kind, e in PARTS:
                if e >= 2:
                    sp.wait_ge(w_low, PART[kind, e - 2] + 1)
                if kind == "up":
                    sp.dma_start(up_raw[:, e % 2, :], up_w[e] if e < E else sw_up
                                 ).then_inc(up_loaded[e % 2], 16)
                else:
                    sp.dma_start(down_raw[:, e % 2, :], (down_w[e] if e < E else sw_down)
                                 .rearrange("(p i) c -> p (i c)", i=IT)
                                 ).then_inc(down_loaded[e % 2], 16)
            for b in range(B):
                sp.wait_ge(y_ready, b + 1)
                sp.dma_start(rows(out[b]), y[:, TT * b:TT * b + TT, :]).then_inc(y_stored, 16)
            sp.wait_ge(y_stored, 16 * B)

        @block.gpsimd
        def _(pool):
            done = [0]

            def link(ins):
                done[0] += 1
                ins.then_inc(pool_chain, 1)
                pool.wait_ge(pool_chain, done[0])

            g = nc.gpsimd

            def select(t, op, fill, base, pattern, by):
                return g.affine_select(out=t, in_=t, compare_op=op, fill=fill, base=base,
                                       pattern=pattern, channel_multiplier=by)

            link(g.memset(ident[:], 0.0))
            select(ident[:], ALU.not_equal, 1.0, 0, [[-1, P]], 1).then_inc(consts_ready, 1)
            pool.wait_ge(consts_ready, 1)
            link(g.memset(minus_half[:], -0.5))
            link(g.memset(f(wqk_h[:, 0:PAIRS, 96:P]), 0.0))
            link(g.memset(f(wqk_l[:, 0:PAIRS, 96:P]), 0.0))
            link(g.memset(f(wqk_h[:, PAIRS:, :]), 0.0))
            link(g.memset(f(wqk_l[:, PAIRS:, :]), 0.0))
            link(g.memset(low_q[:], 0.0))
            link(g.memset(low_k[:], 0.0))
            link(g.memset(low_q[32:64, :], -1.0))
            g.memset(low_k[64:96, :], -1.0).then_inc(consts_ready, 1)
            pool.wait_ge(consts_ready, 2)
            norms = [0]

            def rstd_next():
                k = norms[0] % 2
                norms[0] += 1
                pool.wait_ge(var_ready, norms[0])
                g.tensor_tensor(rstd[:, k, :], var_eps[:, k, :], minus_half[:, 0:TT], ALU.pow
                                ).then_inc(rstd_ready, 1)
                pool.wait_ge(rstd_ready, norms[0])

            rstd_next()
            link(g.memset(aux_rows[:], 0.0))
            for a in range(2):
                for r in range(2):
                    link(select(aux_rows[96:128, a, :], ALU.not_equal, 1.0, -(2 * a + r),
                                [[0, 1]], 1))
            g.memset(ones[:], 1.0).then_inc(consts_ready, 1)
            pool.wait_ge(consts_ready, 3)
            link(g.tensor_copy(identb[:], ident[:]))
            link(g.memset(causal_q[:], 0.0))
            link(g.memset(causal_k[:], 0.0))
            link(select(causal_q[:], ALU.is_ge, NEG, 0, [[-1, P]], 1))
            link(select(causal_k[:], ALU.is_ge, NEG, 0, [[1, P]], -1))
            link(g.memset(v[:, :, :, :, D + 1:32], 0.0))
            link(g.memset(v[:, :, :, :, D:D + 1], 1.0))
            link(g.memset(shift[:], 0.0))
            link(g.memset(wka[:], 0.0))
            link(g.memset(wva[:], 0.0))
            link(g.memset(wva[KD:KD + 1, P:P + 1], 1.0))
            link(g.memset(bias_f[:], 0.0))
            link(g.memset(c_nat[:, :, :, KD:KD + 1], 1.0))
            link(g.memset(low_c[:], 0.0))
            link(g.memset(low_c[0:64, :], -1.0))
            link(select(low_c[64:96, :], ALU.not_equal, -1.0, -1, [[0, 1]], 1))
            g.memset(cshift[:], 0.0).then_inc(consts_ready, 1)
            pool.wait_ge(consts_ready, 4)
            rstd_next()
            link(g.memset(wgt_hl[:], 0.0))
            link(g.memset(wgt[:], 0.0))
            link(g.memset(wgt[:, :, E:E + 1], 0.1))
            link(g.iota(iota_e[:], pattern=[[1, 16]], base=0, channel_multiplier=0,
                        allow_small_or_imprecise_dtypes=True))
            link(g.memset(pick_f[:], 0.0))
            link(select(pick_f[:], ALU.not_equal, 1.0, 0, [[-1, E + 1], [0, 1]], 1))
            select(pick_f[:], ALU.not_equal, 1.0, -16, [[-1, E + 1], [0, 1]], 1
                   ).then_inc(consts_ready, 1)
            pool.wait_ge(consts_ready, 5)

            def weights_low(kind, e):
                n = PART[kind, e]
                pool.wait_ge(w_high, n + 1)
                raw, high, low = weight_parts(kind, e)
                g.tensor_tensor(low, raw, f(high), ALU.subtract).then_inc(w_low, 1)

            def hidden_low(n):
                pool.wait_ge(hid_h_ready, n + 1)
                g.tensor_tensor(hid_l[n % NH], hid[n % NG], f(hid_h[n % NH]), ALU.subtract
                                ).then_inc(hid_l_pool, 1)

            def ctx_split(b, i):
                if i == 0:
                    pool.wait_ge(c_loaded[b], 48)
                    if b:
                        pool.wait_ge(work_filled, W0["ctx_turn", b - 1, 3] + 1)
                k = KF // 2
                pieces = [(P, slice(0, k))] if i % 2 == 0 else \
                    [(KR + 1, slice(KF, KT)), (P, slice(k, KF))]
                for p, (n, j) in enumerate(pieces):
                    high, raw = c_hl[0:n, j, 0:KD], c_nat[0:n, b, j, 0:KD]
                    if i < 2:
                        last = g.tensor_copy(high, raw)
                    else:
                        last = g.tensor_tensor(c_hl[0:n, j, KD:2 * KD], raw, f(high), ALU.subtract)
                    if p + 1 < len(pieces):
                        link(last)
                last.then_inc(c_split, 1)
                pool.wait_ge(c_split, 4 * b + i + 1)

            for name, b, i in SCHED:
                if name == "ctx_split":
                    ctx_split(b, i)
                elif name in STATS and L0[name, b, 0] >= norms[0]:
                    rstd_next()
                elif name == "ffn_weights":
                    weights_low(*PARTS[i])

            for n in range(1, 2 * IT, 2):
                hidden_low(n)
            for e in range(E + 1):
                if e + 2 <= E:
                    weights_low("up", e + 2)
                if e + 1 <= E:
                    weights_low("down", e + 1)
                    for i in range(IT):
                        hidden_low(tile(e + 1, i, 1))

        @block.tensor
        def _(pe):
            mm = nc.tensor.matmul
            tr = nc.tensor.transpose

            def work_bank(step):
                u = W0[step]
                if u >= NW:
                    pe.wait_ge(work_freed, u - NW + 1)
                return work[u % NW]

            def turn_bank(step):
                if T0[step]:
                    pe.wait_ge(turn_freed, T0[step])
                return turn

            def score_bank(step):
                u = S0[step]
                if u >= NS:
                    pe.wait_ge(score_freed, u - NS + 1)
                return score[u % NS]

            def three(dst, w_h, w_l, x_h, x_l):
                mm(dst, w_h, x_h, start=True, stop=False)
                mm(dst, w_l, x_h, start=False, stop=False)
                return mm(dst, w_h, x_l, start=False, stop=True)

            def early_setup(step, b, i):
                pe.wait_ge(consts_ready, 1)
                pe.wait_ge(attn_loaded, 16 * 3)
                tr(self_sum[:, 0:P], wqkv[:, C:2 * C], ident[:]).then_inc(weights_turned, 1)
                pe.wait_ge(weights_taken, 1)
                mm(cross_sum[:, 0:P], wkT[:], geo[:], start=True, stop=True
                   ).then_inc(weights_turned, 1)

            def late_turn(step, b, i):
                bank = turn_bank(step)
                pe.wait_ge(consts_ready, 1)
                pe.wait_ge(cross_loaded, 16 * 4)
                tr(bank[:, 0:P], wq_x[:], ident[:])
                tr(bank[:, P:P + KD], wk_x[:], ident[0:KD, 0:KD]).then_inc(turn_filled, 1)

            def late_setup(step, b, i):
                pe.wait_ge(turn_freed, T0["late_turn", 0, 0] + 1)
                bank = work_bank(step)
                mm(bank[:, 0:2 * P], wqT_x[:], wka[:], start=True, stop=True)
                mm(bank[:, 2 * P:2 * P + 1], wka[:, 0:P], bq_x[:], start=True, stop=True)
                mm(bank[:, 2 * P + 1:2 * P + 2], wka[:, P:2 * P], bq_x[:], start=True, stop=True
                   ).then_inc(work_filled, 1)

            def ctx_turn(step, b, i):
                bank = work_bank(step)
                pe.wait_ge(c_split, 4 * (b + 1))
                for j in range(4 * i, min(4 * i + 4, KT)):
                    m = P if j < KF else NKE - KF * P
                    at = (j - 4 * i) * P
                    last = tr(bank[:, at:at + m], f(c_hl[0:m, j, :]), ident[0:m, 0:m])
                last.then_inc(work_filled, 1)

            def turn_norm(step, b, i):
                n = L0["stats" + step[0][-1], b, 0]
                bank = turn_bank(step)
                pe.wait_ge(xn_ready, n + 1)
                for t in range(TT):
                    last = tr(bank[:, t * P:(t + 1) * P], xn[:, n % 2, t, :], ident[:])
                last.then_inc(turn_filled, 1)

            def values(step, b, i):
                bank = turn_bank(step)
                pe.wait_ge(turn_freed, T0["turn1", b, 0] + 1)
                for t in range(TT):
                    last = mm(bank[:, t * P:(t + 1) * P], xT[:, b % 2, t * P:(t + 1) * P],
                              wqkv[:, 2 * C:3 * C], start=True, stop=True)
                last.then_inc(turn_filled, 1)

            def qk(step, b, i):
                bank = work_bank(step)
                if i == 0:
                    pe.wait_ge(low_ready, LOW["turn1", b, 0] + 1)
                if b == 0 and i in (0, PAIRS // 2):
                    pe.wait_ge(weights_ready, 1 if i == 0 else 2)
                for s in range(2):
                    c = 2 * i + s
                    last = three(bank[:, s * T:(s + 1) * T], wqk_h[:, c, :], wqk_l[:, c, :],
                                 xT_h[:, b % 2, :], xT_l[:, b % 2, :])
                last.then_inc(work_filled, 1)

            def self_max(step, b, r):
                if r == 0:
                    pe.wait_ge(work_freed, W0["qk", b, 5] + 1)
                    if b == 0:
                        pe.wait_ge(consts_ready, 4)
                for k, t in enumerate((1, 0)):
                    n = (t + 1) * P
                    u = W0[step] + k
                    if u >= NW:
                        pe.wait_ge(work_freed, u - NW + 1)
                    dst = work[u % NW][:, 0:2 * n].rearrange("p (a k) -> p a k", a=2)
                    mm(dst, qS[0:96, b % 2, r, t * P:(t + 1) * P],
                       kS[0:96, b % 2, 2 * r:2 * r + 2, 0:n], start=True, stop=False)
                    mm(dst[:, :, t * P:n], identb[:],
                       causal_q[:].unsqueeze(1).to_broadcast([P, 2, P]),
                       start=False, stop=True).then_inc(work_filled, 1)

            def self_shift(step, b, i):
                bank = turn_bank(step)
                pe.wait_ge(shift_ready, b + 1)
                for t in range(TT):
                    last = tr(bank[:, t * P:(t + 1) * P],
                              shift[:, t, :, :].rearrange("p r c -> p (r c)"), ident[:])
                last.then_inc(turn_filled, 1)

            def self_score(step, b, h):
                bank = score_bank(step)
                if h == 0:
                    pe.wait_ge(turn_freed, T0["self_shift", b, 0] + 1)
                    if b == 0:
                        pe.wait_ge(stacks_ready, 6)
                mm(bank[:, P:3 * P], kS[:, b % 2, h, P:2 * P], qS[:, b % 2, h // 2, :],
                   start=True, stop=False)
                mm(bank[:, 2 * P:3 * P], identb[:], causal_k[:], start=False, stop=True)
                mm(bank[:, 0:2 * P], kS[:, b % 2, h, 0:P], qS[:, b % 2, h // 2, :],
                   start=True, stop=False)
                mm(bank[:, 0:P], identb[:], causal_k[:], start=False, stop=True
                   ).then_inc(score_filled, 1)

            def self_pv(step, b, g):
                if g == 0 and b:
                    pe.wait_ge(self_sum_freed, b)
                pe.wait_ge(score_freed, S0["self_score", b, 4 * g + 3] + 1)
                for k in range(2):
                    for j in range(4):
                        s = (b * H + 4 * g + j) % NP
                        src = probs[:, s, 0:2 * P] if k == 0 else probs[:, s, 2 * P:3 * P]
                        last = mm(self_sum[32 * j:32 * j + 32, g * T + k * P:(g + 1) * T],
                                  v[:, b % 2, k, 4 * g + j, :], src, start=(k == 0), stop=(k == 1))
                        if k == 1:
                            last.then_inc(probs_used, 1)

            def self_norm(step, b, i):
                bank = work_bank(step)
                pe.wait_ge(self_sum_freed, b + 1)
                for t in range(TT):
                    for g in range(2):
                        last = tr(bank[:, (2 * t + g) * P:(2 * t + g + 1) * P],
                                  oT[:, g * T + t * P:g * T + (t + 1) * P], ident[:])
                last.then_inc(work_filled, 1)

            def self_turn(step, b, i):
                bank = turn_bank(step)
                pe.wait_ge(work_freed, W0["self_norm", b, 0] + 1)
                for t in range(TT):
                    last = tr(bank[:, t * P:(t + 1) * P],
                              o[:, t, :, :].rearrange("p h d -> p (h d)"), ident[:])
                last.then_inc(turn_filled, 1)

            def self_out(step, b, i):
                bank = work_bank(step)
                pe.wait_ge(turn_freed, T0["self_turn", b, 0] + 1)
                if b == 0:
                    pe.wait_ge(wout_loaded, 16)
                for t in range(TT):
                    last = mm(bank[:, t * P:(t + 1) * P], onT[:, t * P:(t + 1) * P], wout[:],
                              start=True, stop=True)
                last.then_inc(work_filled, 1)

            def query(step, b, i):
                bank = turn_bank(step)
                pe.wait_ge(low_ready, LOW["turn2", b, 0] + 1)
                for s in range(2):
                    cols = slice(s * P, (s + 1) * P)
                    last = three(bank[:, s * T:(s + 1) * T], w2_h[:, cols], w2_l[:, cols],
                                 x2T_h[:], x2T_l[:])
                last.then_inc(turn_filled, 1)

            def cross_max(step, b, n):
                t, i = divmod(n, 4)
                if n == 0:
                    pe.wait_ge(cB_ready, b + 1)
                    pe.wait_ge(qB_ready, b + 1)
                bank = work_bank(step)
                rows = slice(t * P, (t + 1) * P)
                a, m = CH[i], CH[i + 1] - CH[i]
                mm(bank[:, 0:m], qA[:, b % 2, rows], cA[:, b % 2, a:a + m], start=True, stop=False)
                mm(bank[:, 0:m], qB[:, b % 2, rows], cB[:, b % 2, a:a + m], start=False, stop=True
                   ).then_inc(work_filled, 1)

            def cross_shift(step, b, i):
                bank = turn_bank(step)
                pe.wait_ge(cshift_ready, b + 1)
                for t in range(TT):
                    last = tr(bank[:, t * P:(t + 1) * P], cshift[:, t, :], ident[:])
                last.then_inc(turn_filled, 1)

            def cross_score(step, b, i):
                bank = score_bank(step)
                if i == 0:
                    pe.wait_ge(qB_shifted, b + 1)
                for j in range(2 * i, min(2 * i + 2, KT)):
                    m = P if j < KF else KR
                    dst = bank[0:m, (j % 2) * T:(j % 2 + 1) * T]
                    mm(dst, cA[:, b % 2, j * P:j * P + m], qA[:, b % 2, :], start=True, stop=False)
                    last = mm(dst, cB[:, b % 2, j * P:j * P + m], qB[:, b % 2, :],
                              start=False, stop=True)
                last.then_inc(score_filled, 1)

            def cross_pv(step, b, i):
                if i == 0 and b:
                    pe.wait_ge(cross_sum_freed, b)
                pe.wait_ge(score_freed, S0["cross_score", b, i] + 1)
                for j in range(2 * i, min(2 * i + 2, KT)):
                    m = P if j < KF else KR
                    last = mm(cross_sum[0:KD + 1, 0:T], c_nat[0:m, b, j, :],
                              cprobs[0:m, (b * KP + i) % NC, (j % 2) * T:(j % 2 + 1) * T],
                              start=(j == 0), stop=(j == KT - 1))
                last.then_inc(cprobs_used, 1)

            def cross_out(step, b, i):
                bank = work_bank(step)
                pe.wait_ge(cross_sum_freed, b + 1)
                if b == 0:
                    pe.wait_ge(wva_loaded, 32)
                for t in range(TT):
                    last = mm(bank[:, t * 256:t * 256 + P + 2], coT[:, t * P:(t + 1) * P], wva[:],
                              start=True, stop=True)
                last.then_inc(work_filled, 1)

            def gate_(step, b, i):
                bank = work_bank(step)
                pe.wait_ge(turn_freed, T0["turn3", b, 0] + 1)
                if b == 0:
                    pe.wait_ge(ffn_loaded, 16 * 8)
                for t in range(TT):
                    last = mm(bank[:, t * E:(t + 1) * E], x3T[:, b % 2, t * P:(t + 1) * P], gate[:],
                              start=True, stop=True)
                last.then_inc(work_filled, 1)

            def mix_turn(step, b, i):
                bank = turn_bank(step)
                pe.wait_ge(mix_ready, 1)
                for t in range(4):
                    last = tr(bank[:, t * P:(t + 1) * P], wgt_hl[:, t, :], ident[:])
                last.then_inc(turn_filled, 1)

            half = [slice(s * HALF, (s + 1) * HALF) for s in range(2)]

            def ahead(step, b, i):
                if i == 0:
                    pe.wait_ge(w_low, PART["up", 0] + 1)
                    pe.wait_ge(low_ready, LOW["turn3", 1, 0] + 1)
                    pe.wait_ge(self_sum_freed, B)
                    pe.wait_ge(cross_sum_freed, B)
                    pe.wait_ge(score_freed, S_ALL)
                three(up_bank(i)[:], up_h[:, 0, i, :], up_l[:, 0, i, :], x3T_h[:, half[0]],
                      x3T_l[:, half[0]]).then_inc(up_filled, 1)

            steps = {"early_setup": early_setup, "late_turn": late_turn,
                     "late_setup": late_setup, "ctx_turn": ctx_turn,
                     "mix_turn": mix_turn, "ahead": ahead, "turn1": turn_norm,
                     "turn2": turn_norm, "turn3": turn_norm, "values": values,
                     "qk": qk, "self_max": self_max, "self_shift": self_shift,
                     "self_score": self_score, "self_pv": self_pv, "self_norm": self_norm,
                     "self_turn": self_turn, "self_out": self_out, "query": query,
                     "cross_max": cross_max, "cross_shift": cross_shift,
                     "cross_score": cross_score, "cross_pv": cross_pv, "cross_out": cross_out,
                     "gate": gate_}
            for step in SCHED:
                if step[0] in steps:
                    steps[step[0]](step, *step[1:])

            pe.wait_ge(turn_freed, T_ALL)
            pe.wait_ge(work_freed, W_ALL)
            pe.wait_ge(low_ready, LOW_ALL)

            def up(e, i, halves=(0, 1)):
                if i == 0:
                    pe.wait_ge(w_low, PART["up", e] + 1)
                for s in halves:
                    pe.wait_ge(hid_ready, tile(e, i, s) - NU + 1)
                w_h, w_l = up_h[:, e % 2, i, :], up_l[:, e % 2, i, :]
                for s in halves:
                    mm(up_bank(tile(e, i, s))[:], w_h, x3T_h[:, half[s]], start=True, stop=False)
                for s in halves:
                    mm(up_bank(tile(e, i, s))[:], w_h, x3T_l[:, half[s]], start=False, stop=False)
                for s in halves:
                    mm(up_bank(tile(e, i, s))[:], w_l, x3T_h[:, half[s]], start=False, stop=True
                       ).then_inc(up_filled, 1)

            def widen(e):
                for s in range(2):
                    if e:
                        pe.wait_ge(wide_ready, 2 * e + s - 1)
                    mm(wide_banks[s][:], pick[:, e, :], wgtT[:, half[s]], start=True, stop=True
                       ).then_inc(wide_filled, 1)

            def down(e, i):
                if i == 0:
                    pe.wait_ge(w_low, PART["down", e] + 1)
                    if e == E:
                        pe.wait_ge(wide_ready, 2 * E)
                    elif e:
                        pe.wait_ge(down_taken, 2 * e)
                banks = wide_banks if e == E else score
                w_h, w_l = down_h[:, e % 2, i, :], down_l[:, e % 2, i, :]
                for s in range(2):
                    n = tile(e, i, s)
                    pe.wait_ge(hid_h_ready, n + 1)
                    mm(banks[s][:], w_h, hid_h[n % NH], start=(i == 0), stop=False)
                for s in range(2):
                    mm(banks[s][:], w_l, hid_h[tile(e, i, s) % NH], start=False, stop=False)
                for s in range(2):
                    n = tile(e, i, s)
                    pe.wait_ge(hid_l_pool if n % 2 else hid_l_dve, n // 2 + 1)
                    mm(banks[s][:], w_h, hid_l[n % NH], start=False, stop=(i == IT - 1)
                       ).then_inc(hid_used, 1)

            for i in range(IT):
                up(0, i, halves=(1,))
            for e in range(E):
                for i in range(0, IT, 2):
                    up(e + 1, i)
                    up(e + 1, i + 1)
                    down(e, i)
                    down(e, i + 1)
                    if e == 0 and i == 0:
                        pe.wait_ge(mix_ready, 2)
                        for t in range(4):
                            last = tr(wide_banks[1][:, t * P:(t + 1) * P], wgt_hl[:, 4 + t, :],
                                      ident[:])
                        last.then_inc(mix_turned, 1)
                        pe.wait_ge(mixT_ready, 1)
                    if i == 0:
                        widen(e)
            down(E, 0)
            pe.wait_ge(hid_ready, 2 * IT * (E + 1))
            for s in range(2):
                mm(up_banks[2 + s][:], bias_h[:], wgtT[:, half[s]], start=True, stop=False)
                mm(up_banks[2 + s][:], bias_l[:], wgtT[:, half[s]], start=False, stop=True
                   ).then_inc(bias_filled, 1)
            down(E, 1)
            down(E, 2)
            down(E, 3)

            for s in range(2):
                pe.wait_ge(acc_ready, s + 1)
                for t in range(4):
                    last = tr(up_banks[s][:, t * P:(t + 1) * P], acc[:, s, t * P:(t + 1) * P],
                              ident[:])
                last.then_inc(acc_turned, 1)

        @block.scalar
        def _(act):
            a = nc.scalar

            def copy(dst, src):
                return a.activation(dst, src, ACT.Copy)

            def stacks(step, b, i):
                s, k = divmod(i, 3)
                if i == 0:
                    act.wait_ge(consts_ready, 3)
                if k < 2:
                    last = copy(kS[96:128, s, :, :].rearrange("p (r a) t -> p r a t", a=2)
                                [:, :, k, :],
                                aux_rows[96:128, k:k + 1, :].to_broadcast([32, PAIRS, T]))
                else:
                    last = copy(cB[64:128, s, :], ones[64:128, 0:1].to_broadcast([64, NKE]))
                last.then_inc(stacks_ready, 1)

            def late_turn(step, b, i):
                act.wait_ge(turn_filled, T0[step] + 1)
                act.wait_ge(consts_ready, 4)
                copy(wqT_x[:], turn[:, 0:P])
                for k in range(3):
                    copy(wka[:, k * KD:(k + 1) * KD], turn[:, P:P + KD])
                copy(wka[:, 3 * KD:3 * KD + 2], bk_x[:].to_broadcast([P, 2])
                     ).then_inc(turn_freed, 1)

            def ctx_copy(step, b, i):
                act.wait_ge(work_freed, W0["ctx_turn", b, 3] + 1)
                if b >= 2:
                    act.wait_ge(score_filled, S0["cross_score", b - 2, KP - 1] + 1)
                copy(cB[0:KD, b % 2, :], f(cA[0:KD, b % 2, :])).then_inc(cB_ready, 1)

            def norm_out(step, dst, dst_h):
                act.wait_ge(turn_filled, T0[step] + 1)
                copy(dst, turn[:, 0:T])
                copy(dst_h, turn[:, 0:T]).then_inc(turn_freed, 1)

            def turn1(step, b, i):
                if b >= 2:
                    act.wait_ge(work_filled, W0["qk", b - 2, 5] + 1)
                norm_out(step, xT[:, b % 2, :], xT_h[:, b % 2, :])

            def values(step, b, i):
                act.wait_ge(turn_filled, T0[step] + 1)
                if b >= 2:
                    act.wait_ge(probs_used, H * (b - 1))
                if b == 0:
                    act.wait_ge(consts_ready, 4)
                copy(v[:, b % 2, :, :, 0:D],
                     turn[:, 0:T].rearrange("p (t h d) -> p t h d", t=TT, d=D)
                     ).then_inc(turn_freed, 1)

            def qk(step, b, i):
                n = b * 6 + i
                act.wait_ge(work_filled, W0[step] + 1)
                if n >= 2:
                    act.wait_ge(work_freed, W0["qk", (n - 2) // 6, (n - 2) % 6] + 1)
                copy(all_h[0:96, n % 2, :], work[W0[step] % NW][0:96, :]).then_inc(all_h_ready, 1)

            def self_shift(step, b, i):
                act.wait_ge(turn_filled, T0[step] + 1)
                for r in range(PAIRS):
                    last = copy(qS[96:128, b % 2, r, :], turn[32 * r:32 * r + 32, 0:T])
                last.then_inc(turn_freed, 1)

            def self_score(step, b, h):
                u = S0[step]
                n = b * H + h
                act.wait_ge(score_filled, u + 1)
                if n >= NP:
                    act.wait_ge(probs_used, n - NP + 1)
                a.activation(probs[:, n % NP, :], score[u % NS][:, 0:3 * P], ACT.Exp
                             ).then_inc(score_freed, 1)

            def self_pv(step, b, g):
                if g == 1:
                    act.wait_ge(probs_used, H * (b + 1))
                    if b:
                        act.wait_ge(work_filled, W0["self_norm", b - 1, 0] + 1)
                    copy(oT[:], self_sum[:]).then_inc(self_sum_freed, 1)

            def self_turn(step, b, i):
                act.wait_ge(turn_filled, T0[step] + 1)
                if b:
                    act.wait_ge(work_filled, W0["self_out", b - 1, 0] + 1)
                copy(onT[:], turn[:, 0:T]).then_inc(turn_freed, 1)

            def turn2(step, b, i):
                if b:
                    act.wait_ge(turn_filled, T0["query", b - 1, 0] + 1)
                norm_out(step, x2T[:], x2T_h[:])

            def query(step, b, i):
                act.wait_ge(turn_filled, T0[step] + 1)
                if b == 0:
                    act.wait_ge(weights_ready, 3)
                if b:
                    act.wait_ge(qB_ready, b)
                if b >= 2:
                    act.wait_ge(score_filled, S0["cross_score", b - 2, KP - 1] + 1)
                a.activation(qA[:, b % 2, :], turn[:, 0:T], ACT.Identity, bias=b2[:, 0:1])
                a.activation(qB_f[:], turn[:, T:2 * T], ACT.Identity, bias=b2[:, 1:2])
                a.activation(qB_h[:], turn[:, T:2 * T], ACT.Identity, bias=b2[:, 1:2]
                             ).then_inc(turn_freed, 1)

            def cross_shift(step, b, i):
                act.wait_ge(turn_filled, T0[step] + 1)
                if b:
                    act.wait_ge(qB_shifted, b)
                copy(cshiftT[64:128, :], turn[64:128, 0:T]).then_inc(turn_freed, 1)

            def cross_score(step, b, i):
                u = S0[step]
                n = b * KP + i
                act.wait_ge(score_filled, u + 1)
                if n >= NC:
                    act.wait_ge(cprobs_used, n - NC + 1)
                m, w = (P, 2 * T) if 2 * i + 2 <= KF else (KR, T)
                a.activation(cprobs[0:m, n % NC, 0:w], score[u % NS][0:m, 0:w], ACT.Exp
                             ).then_inc(score_freed, 1)

            def cross_pv(step, b, i):
                if i == KP - 1:
                    act.wait_ge(cprobs_used, KP * (b + 1))
                    if b:
                        act.wait_ge(work_filled, W0["cross_out", b - 1, 0] + 1)
                    copy(coT[:], cross_sum[0:KD + 1, 0:T]).then_inc(cross_sum_freed, 1)

            def turn3(step, b, i):
                if b >= 2:
                    act.wait_ge(work_filled, W0["gate", b - 2, 0] + 1)
                    act.wait_ge(low_ready, LOW["turn3", b - 2, 0] + 1)
                norm_out(step, x3T[:, b % 2, :], x3T_h[:, b * T:(b + 1) * T])

            def mix(step, b, i):
                s = b // 2
                act.wait_ge(work_freed, W0["gate", b, 0] + 1)
                a.activation(z[:, 4 * s:4 * s + 4, :], z[:, 4 * s:4 * s + 4, :], ACT.Exp,
                             scale=-1.0).then_inc(ez_ready, 1)

            def mix_turn(step, b, i):
                act.wait_ge(turn_filled, T0[step] + 1)
                copy(wgtT[:, 0:HALF], turn[:]).then_inc(turn_freed, 1)

            def hidden(n, bias):
                act.wait_ge(up_filled, n + 1)
                if n >= NG:
                    m = n - NG
                    act.wait_ge(hid_l_pool if m % 2 else hid_l_dve, m // 2 + 1)
                a.activation(hid[n % NG], up_bank(n)[:], ACT.Gelu, bias=bias
                             ).then_inc(hid_ready, 1)

            def ahead(step, b, i):
                if i == 0:
                    act.wait_ge(ffn_loaded, 16 * 8)
                hidden(i, up_bias[:, 0, i:i + 1])

            steps = {"mix": mix, "mix_turn": mix_turn, "ahead": ahead, "stacks": stacks,
                     "late_turn": late_turn, "ctx_copy": ctx_copy, "turn1": turn1,
                     "turn2": turn2, "turn3": turn3, "values": values, "qk": qk,
                     "self_shift": self_shift, "self_score": self_score, "self_pv": self_pv,
                     "self_turn": self_turn, "query": query, "cross_shift": cross_shift,
                     "cross_score": cross_score, "cross_pv": cross_pv}
            for step in SCHED:
                if step[0] in steps:
                    steps[step[0]](step, *step[1:])
            mix(None, B - 1, 0)

            def widen(e):
                for s in range(2):
                    act.wait_ge(wide_filled, 2 * e + s + 1)
                    if e >= 2:
                        act.wait_ge(down_taken, 2 * (e - 1))
                    copy(wide[:, e % 2, s * HALF:(s + 1) * HALF], wide_banks[s][:]
                         ).then_inc(wide_ready, 1)

            for i in range(IT):
                hidden(tile(0, i, 1), up_bias[:, 0, i:i + 1])
            for e in range(E):
                for i in range(IT):
                    for s in range(2):
                        hidden(tile(e + 1, i, s), up_bias[:, e + 1, i:i + 1])
                    if e == 0 and i == 1:
                        act.wait_ge(mix_turned, 1)
                        copy(wgtT[:, HALF:2 * HALF], wide_banks[1][:]).then_inc(mixT_ready, 1)
                    if i == 1:
                        widen(e)

        @block.vector
        def _(dve):
            d = nc.vector
            done = [0]

            def link(ins):
                done[0] += 1
                ins.then_inc(dve_chain, 1)
                dve.wait_ge(dve_chain, done[0])

            def early_setup(step, b, i):
                dve.wait_ge(attn_loaded, 16 * 3)
                dve.wait_ge(consts_ready, 2)
                link(d.tensor_tensor(geo_d[:].rearrange("p (h c) -> p h c", c=D),
                                     dirs[:].rearrange("p (h c) -> p h c", c=D),
                                     hs[:].unsqueeze(2).to_broadcast([P, H, D]), ALU.mult))
                d.scalar_tensor_tensor(out=geo[:], in0=ident[:], scalar=SCALE, in1=geo_d[:],
                                       op0=ALU.mult, op1=ALU.add)
                dve.wait_ge(weights_turned, 1)
                d.tensor_copy(wkT[:], self_sum[:, 0:P]).then_inc(weights_taken, 1)
                wq = wqkv[:, 0:C].rearrange("p (r c) -> p r c", c=32)
                for k in range(3):
                    last = d.tensor_copy(wqk_h[:, 0:PAIRS, 32 * k:32 * k + 32], wq)
                link(last)
                for k in range(3):
                    part = slice(32 * k, 32 * k + 32)
                    last = d.tensor_tensor(wqk_l[:, 0:PAIRS, part], wq,
                                           f(wqk_h[:, 0:PAIRS, part]), ALU.subtract)
                last.then_inc(weights_ready, 1)
                dve.wait_ge(weights_turned, 2)
                wk = cross_sum[:, 0:P].rearrange("p (r a c) -> p r a c", a=2, c=D)

                def keys(w, k, s):
                    at = 32 * k + D * s
                    return w[:, PAIRS:, :].rearrange("p (r a) c -> p r a c", a=2)[
                        :, :, s, at:at + D]

                for k in range(3):
                    for s in range(2):
                        last = d.tensor_copy(keys(wqk_h, k, s), wk[:, :, s, :])
                link(last)
                for k in range(3):
                    for s in range(2):
                        last = d.tensor_tensor(keys(wqk_l, k, s), wk[:, :, s, :],
                                               f(keys(wqk_h, k, s)), ALU.subtract)
                last.then_inc(weights_ready, 1)

            def late_setup(step, b, i):
                u = W0[step]
                dve.wait_ge(work_filled, u + 1)
                d.tensor_copy(b2[:], work[u % NW][:, 2 * P:2 * P + 2])
                d.tensor_copy(w2[:], work[u % NW][:, 0:2 * P]).then_inc(work_freed, 1)
                dve.wait_ge(work_freed, u + 1)
                link(d.tensor_copy(w2_h[:], w2[:]))
                d.tensor_tensor(w2_l[:], w2[:], f(w2_h[:]), ALU.subtract).then_inc(weights_ready, 1)

            def stats(step, b, i):
                k = L0[step] % 2
                src = norm_src(step[0], b)
                if step[0] == "stats1":
                    dve.wait_ge(x_loaded[b], 16)
                for t in range(TT):
                    last = d.bn_stats(bn[:, t, :], src[:, t, :])
                link(last)
                for t in range(TT):
                    last = d.bn_aggr(mean_var[:, k, t, :], bn[:, t, :])
                link(last)
                d.tensor_scalar(var_eps[:, k, :], mean_var[:, k, :, 1], 1e-5, None, ALU.add
                                ).then_inc(var_ready, 1)

            def norm(step, b, i):
                kind = step[0][-1]
                src = norm_src("stats" + kind, b)
                n = L0["stats" + kind, b, 0]
                if n >= 2:
                    dve.wait_ge(turn_filled, TURNED[n - 2] + 1)
                dve.wait_ge(rstd_ready, n + 1)
                for t in range(TT):
                    last = d.tensor_scalar(xn[:, n % 2, t, :], src[:, t, :],
                                           mean_var[:, n % 2, t, 0:1], rstd[:, n % 2, t:t + 1],
                                           ALU.subtract, ALU.mult)
                last.then_inc(xn_ready, 1)

            def norm_src(kind, b):
                tiles = slice(TT * b, TT * b + TT)
                return {"stats1": x_in, "stats2": x1, "stats3": x2}[kind][:, tiles, :]

            def low_part(step, b, i):
                high, full, low = {
                    "turn1": (xT_h[:, b % 2, :], xT[:, b % 2, :], xT_l[:, b % 2, :]),
                    "turn2": (x2T_h[:], x2T[:], x2T_l[:]),
                    "turn3": (x3T_h[:, b * T:(b + 1) * T], x3T[:, b % 2, :],
                              x3T_l[:, b * T:(b + 1) * T])}[step[0]]
                dve.wait_ge(turn_freed, T0[step] + 1)
                d.tensor_tensor(low, full, f(high), ALU.subtract).then_inc(low_ready, 1)

            def ctx_turn(step, b, i):
                if b >= 2 and i == 0:
                    dve.wait_ge(score_filled, S0["cross_score", b - 2, KP - 1] + 1)
                a, n = 512 * i, min(512, NKE - 512 * i)
                dve.wait_ge(work_filled, W0[step] + 1)
                d.tensor_copy(cA[:, b % 2, a:a + n], work[W0[step] % NW][:, 0:n]
                              ).then_inc(work_freed, 1)

            def qk(step, b, i):
                n = b * 6 + i
                if b >= 2 and i == 0:
                    dve.wait_ge(score_filled, S0["self_score", b - 2, H - 1] + 1)
                dve.wait_ge(all_h_ready, n + 1)
                if i < PAIRS // 2:
                    dst, low = qS[0:96, b % 2, 2 * i:2 * i + 2, :], low_q
                else:
                    k = 2 * i - PAIRS
                    dst, low = kS[0:96, b % 2, k:k + 2, :], low_k
                d.scalar_tensor_tensor(
                    out=dst, in0=f(all_h[0:96, n % 2, :]).rearrange("p (a t) -> p a t", a=2),
                    scalar=low[0:96, 0:1],
                    in1=work[W0[step] % NW][0:96, :].rearrange("p (a t) -> p a t", a=2),
                    op0=ALU.mult, op1=ALU.add).then_inc(work_freed, 1)

            def self_max(step, b, r):
                for k, t in enumerate((1, 0)):
                    u = W0[step] + k
                    n = (t + 1) * P
                    dve.wait_ge(work_filled, u + 1)
                    d.tensor_reduce(nmax[:, t, 2 * r:2 * r + 2],
                                    work[u % NW][:, 0:2 * n].rearrange("p (a k) -> p a k", a=2),
                                    X, ALU.max, negate=True).then_inc(work_freed, 1)

            def self_split(step, b, i):
                dve.wait_ge(work_freed, W0["self_max", b, PAIRS - 1] + 2)
                if b:
                    dve.wait_ge(turn_filled, T0["self_shift", b - 1, 0] + 1)
                link(d.tensor_copy(nmax_h[:], nmax[:]))
                at = shift[:, :, :, 0:4].rearrange("p t r (a l) -> p (t r) a l", l=2)
                hi = f(nmax_h[:]).rearrange("p t (r a) -> p (t r) a", a=2)
                d.tensor_copy(at[:, :, :, 0], hi)
                d.tensor_tensor(at[:, :, :, 1], nmax[:].rearrange("p t (r a) -> p (t r) a", a=2),
                                hi, ALU.subtract).then_inc(shift_ready, 1)

            def self_norm(step, b, i):
                u = W0[step]
                dve.wait_ge(work_filled, u + 1)
                if b:
                    dve.wait_ge(turn_filled, T0["self_turn", b - 1, 0] + 1)
                src = work[u % NW][:].rearrange("p (t h c) -> p t h c", t=TT, c=32)
                link(d.reciprocal(rden[:], src[:, :, :, D:D + 1]))
                d.tensor_tensor(o[:], src[:, :, :, 0:D], rden[:].to_broadcast([P, TT, H, D]),
                                ALU.mult).then_inc(work_freed, 1)

            def self_out(step, b, i):
                u = W0[step]
                tiles = slice(TT * b, TT * b + TT)
                dve.wait_ge(work_filled, u + 1)
                d.tensor_tensor(x1[:, tiles, :],
                                work[u % NW][:, 0:T].rearrange("p (t c) -> p t c", t=TT),
                                x_in[:, tiles, :], ALU.add).then_inc(work_freed, 1)
                dve.wait_ge(work_freed, u + 1)

            def query(step, b, i):
                dve.wait_ge(turn_freed, T0[step] + 1)
                d.scalar_tensor_tensor(out=qB[:, b % 2, :], in0=f(qB_h[:]), scalar=low_c[:, 0:1],
                                       in1=qB_f[:], op0=ALU.mult, op1=ALU.add
                                       ).then_inc(qB_ready, 1)

            def cross_max(step, b, n):
                t, i = divmod(n, 4)
                u = W0[step]
                dve.wait_ge(work_filled, u + 1)
                d.tensor_reduce(cmax[:, t, i:i + 1], work[u % NW][:, 0:CH[i + 1] - CH[i]],
                                X, ALU.max).then_inc(work_freed, 1)

            def cross_split(step, b, i):
                dve.wait_ge(work_freed, W0["cross_max", b, 7] + 1)
                link(d.tensor_reduce(cnmax[:], cmax[:], X, ALU.max, negate=True))
                if b:
                    dve.wait_ge(turn_filled, T0["cross_shift", b - 1, 0] + 1)
                link(d.tensor_copy(cnmax_h[:], cnmax[:]))
                d.tensor_copy(cshift[:, :, KD + 2], f(cnmax_h[:]))
                d.tensor_tensor(cshift[:, :, KD + 3], cnmax[:], f(cnmax_h[:]), ALU.subtract
                                ).then_inc(cshift_ready, 1)

            def cross_shift(step, b, i):
                dve.wait_ge(turn_freed, T0[step] + 1)
                d.tensor_tensor(qB[64:128, b % 2, :], f(qB[64:128, b % 2, :]), cshiftT[64:128, :],
                                ALU.add).then_inc(qB_shifted, 1)

            def cross_out(step, b, i):
                u = W0[step]
                dve.wait_ge(work_filled, u + 1)
                src = work[u % NW][:].rearrange("p (t c) -> p t c", t=TT)
                link(d.reciprocal(crden[:], src[:, :, P:P + 1]))
                for t in range(TT):
                    last = d.scalar_tensor_tensor(
                        out=x2[:, TT * b + t, :], in0=src[:, t, 0:P], scalar=crden[:, t, :],
                        in1=x1[:, TT * b + t, :], op0=ALU.mult, op1=ALU.add)
                last.then_inc(work_freed, 1)
                dve.wait_ge(work_freed, u + 1)

            def gate_(step, b, i):
                dve.wait_ge(work_filled, W0[step] + 1)
                d.tensor_tensor(z[:, TT * b:TT * b + TT, :],
                                work[W0[step] % NW][:, 0:TT * E].rearrange("p (t e) -> p t e", e=E),
                                gate_bias[:].unsqueeze(1).to_broadcast([P, TT, E]), ALU.add
                                ).then_inc(work_freed, 1)

            def weights_high(kind, e):
                loaded = up_loaded if kind == "up" else down_loaded
                dve.wait_ge(loaded[e % 2], 16 * (e // 2 + 1))
                if e >= 2 and kind == "up":
                    dve.wait_ge(up_filled, 2 * IT * (e - 1))
                if e >= 2 and kind == "down":
                    dve.wait_ge(hid_used, 2 * IT * (e - 1))
                raw, high, _ = weight_parts(kind, e)
                d.tensor_copy(high, raw).then_inc(w_high, 1)

            def ffn_weights(step, b, i):
                weights_high(*PARTS[i])
                if i == 2:
                    dve.wait_ge(consts_ready, 5)
                    dve.wait_ge(ffn_loaded, 16 * 8)
                    d.tensor_copy(pick[:], pick_f[:].to_broadcast([P, E + 1, P]))
                    link(d.tensor_copy(bias_h[:], bias_f[:]))
                    d.tensor_tensor(bias_l[:], bias_f[:], f(bias_h[:]), ALU.subtract
                                    ).then_inc(weights_ready, 1)

            def mix(step, b, i):
                half = b // 2
                tiles = slice(4 * half, 4 * half + 4)
                dve.wait_ge(ez_ready, half + 1)
                dve.wait_ge(consts_ready, 5)
                link(d.tensor_scalar(sig[:, tiles, :], z[:, tiles, :], 1.0, None, ALU.add))
                link(d.reciprocal(sig[:, tiles, :], sig[:, tiles, :]))
                for t in range(4 * half, 4 * half + 4):
                    last = d.max(top[:, t, :], sig[:, t, :])
                link(last)
                for t in range(4 * half, 4 * half + 4):
                    last = d.max_index(top_i[:, t, :], top[:, t, :], sig[:, t, :])
                link(d.scalar_tensor_tensor(out=den[:, tiles, :], in0=top[:, tiles, 0:1],
                                            scalar=1e-6, in1=top[:, tiles, 1:2], op0=ALU.add,
                                            op1=ALU.add))
                link(d.reciprocal(den[:, tiles, :], den[:, tiles, :]))
                d.scalar_tensor_tensor(out=share[:, tiles, :], in0=top[:, tiles, 0:2], scalar=0.1,
                                       in1=den[:, tiles, :].to_broadcast([P, 4, 2]),
                                       op0=ALU.mult, op1=ALU.mult)
                link(d.tensor_copy(top_f[:, tiles, 0:2], top_i[:, tiles, 0:2]))
                wide_iota = iota_e[:, 0:E].unsqueeze(1).to_broadcast([P, 4, E])
                for k in range(2):
                    last = d.tensor_tensor(hit[:, k, tiles, :], wide_iota,
                                           top_f[:, tiles, k:k + 1].to_broadcast([P, 4, E]),
                                           ALU.is_equal)
                link(last)
                for k in range(2):
                    last = d.tensor_tensor(hit[:, k, tiles, :], hit[:, k, tiles, :],
                                           share[:, tiles, k:k + 1].to_broadcast([P, 4, E]),
                                           ALU.mult)
                link(last)
                link(d.tensor_tensor(wgt[:, tiles, 0:E], hit[:, 0, tiles, :], hit[:, 1, tiles, :],
                                     ALU.add))
                link(d.tensor_copy(wgt_h[:, tiles, :], wgt[:, tiles, :]))
                d.tensor_copy(wgt_hl[:, tiles, 0:16], f(wgt_h[:, tiles, :]))
                d.tensor_tensor(wgt_hl[:, tiles, 16:32], wgt[:, tiles, :], f(wgt_h[:, tiles, :]),
                                ALU.subtract).then_inc(mix_ready, 1)

            steps = {"ffn_weights": ffn_weights, "mix": mix, "early_setup": early_setup,
                     "late_setup": late_setup,
                     "ctx_turn": ctx_turn, "stats1": stats, "stats2": stats, "stats3": stats,
                     "norm1": norm, "norm2": norm, "norm3": norm, "turn1": low_part,
                     "turn2": low_part, "turn3": low_part, "qk": qk, "self_max": self_max,
                     "self_split": self_split, "self_norm": self_norm, "self_out": self_out,
                     "query": query, "cross_max": cross_max, "cross_split": cross_split,
                     "cross_shift": cross_shift, "cross_out": cross_out, "gate": gate_}
            for step in SCHED:
                if step[0] in steps:
                    steps[step[0]](step, *step[1:])

            def hidden(n):
                dve.wait_ge(hid_ready, n + 1)
                if n >= NH:
                    dve.wait_ge(hid_used, used(n - NH))
                d.tensor_copy(hid_h[n % NH], hid[n % NG]).then_inc(hid_h_ready, 1)
                if n % 2 == 0:
                    dve.wait_ge(hid_h_ready, n + 1)
                    d.tensor_tensor(hid_l[n % NH], hid[n % NG], f(hid_h[n % NH]), ALU.subtract
                                    ).then_inc(hid_l_dve, 1)

            for n in range(IT):
                hidden(n)
            mix(None, B - 1, 0)
            for n in range(IT, 2 * IT):
                hidden(n)
            for e in range(E):
                if e + 2 <= E:
                    weights_high("up", e + 2)
                weights_high("down", e + 1)
                for i in range(IT):
                    for s in range(2):
                        hidden(tile(e + 1, i, s))
                dve.wait_ge(hid_used, 2 * IT * (e + 1))
                dve.wait_ge(wide_ready, 2 * e + 2)
                for s in range(2):
                    dst = acc[:, s, :] if e == 0 else part[:, s, :]
                    d.tensor_tensor(dst, score[s][:], wide[:, e % 2, s * HALF:(s + 1) * HALF],
                                    ALU.mult).then_inc(down_taken, 1)
                if e:
                    for s in range(2):
                        dve.wait_ge(down_taken, 2 * e + s + 1)
                        last = d.tensor_tensor(acc[:, s, :], acc[:, s, :], part[:, s, :], ALU.add)
                    link(last)
            for s in range(2):
                dve.wait_ge(bias_filled, s + 1)
                last = d.tensor_tensor(acc[:, s, :], acc[:, s, :], up_banks[2 + s][:], ALU.add)
            link(last)
            dve.wait_ge(hid_used, 2 * IT * (E + 1))
            for s in range(2):
                d.scalar_tensor_tensor(out=acc[:, s, :], in0=wide_banks[s][:], scalar=0.1,
                                       in1=acc[:, s, :], op0=ALU.mult, op1=ALU.add
                                       ).then_inc(acc_ready, 1)
            for s in range(2):
                dve.wait_ge(acc_turned, s + 1)
                last = d.tensor_reduce(peak[:, 4 * s:4 * s + 4],
                                       up_banks[s][:].rearrange("p (t c) -> p t c", t=4), X,
                                       ALU.max, apply_absolute_value=True)
            link(last)
            link(d.tensor_scalar(peak[:], peak[:], 1e-6, None, ALU.add))
            link(d.reciprocal(peak[:], peak[:]))
            for t in range(NT):
                last = d.scalar_tensor_tensor(
                    out=y[:, t, :], in0=up_banks[t // 4][:, (t % 4) * P:(t % 4 + 1) * P],
                    scalar=peak[:, t:t + 1], in1=x2[:, t, :], op0=ALU.mult, op1=ALU.add)
                if t % TT == TT - 1:
                    last.then_inc(y_ready, 1)


_INS = ["x", "ctx_512", "L0_attn_w_qkv", "L0_attn_w_out", "L0_attn_head_scales", "L0_xattn_Wq",
        "L0_xattn_bq", "L0_xattn_Wk", "L0_xattn_bk", "L0_xattn_Wv", "L0_xattn_bv",
        "L0_ffn_gate_w", "L0_ffn_bias", "L0_ffn_up_w", "L0_ffn_up_b", "L0_ffn_down_w",
        "L0_ffn_down_b", "L0_ffn_sw_up", "L0_ffn_sb_up", "L0_ffn_sw_down", "L0_ffn_sb_down"]


def head_dirs_outer(heads, dim):
    m = np.zeros((heads * dim, heads * dim), np.float32)
    for h in range(heads):
        v = np.array([(h >> 2 & 1) * 2 - 1, (h >> 1 & 1) * 2 - 1, (h & 1) * 2 - 1], np.float32)
        m[h * dim:h * dim + 3, h * dim:h * dim + 3] = np.outer(v, v) / np.float32(3.0)
    return m


def kernel(**inputs):
    import concourse.bacc as bacc
    from concourse.bass_utils import run_bass_kernel_spmd

    nc = bacc.Bacc("TRN2", target_bir_lowering=False, num_devices=1)
    arrays, args = {}, []
    given = {n: np.ascontiguousarray(inputs[n]) for n in _INS}
    given["dirs_outer"] = head_dirs_outer(8, 16)
    for name, a in given.items():
        arrays[f"in_{name}"] = a
        args.append(nc.dram_tensor(f"in_{name}", a.shape, mybir.dt.from_np(a.dtype),
                                   kind="ExternalInput").ap())
    args.append(nc.dram_tensor("out_x", given["x"].shape, F32, kind="ExternalOutput").ap())
    decoder_layer(nc, *args)
    r = run_bass_kernel_spmd(nc, [arrays], core_ids=[0])
    return r.results[0]["out_x"]
```
